# Optimizing a Trainium2 kernel written in Bass

```python
import numpy as np
import jax
import jax.numpy as jnp

def _softmax(x, axis=-1):
    return jax.nn.softmax(x, axis=axis)

def _gelu(x):
    return jax.nn.gelu(x, approximate=True)

def _silu(x):
    return jax.nn.silu(x)

def _sigmoid(x):
    return jax.nn.sigmoid(x)

def _layernorm(x, axis=-1, eps=1e-05):
    m = jnp.mean(x, axis=axis, keepdims=True)
    v = jnp.var(x, axis=axis, keepdims=True)
    return (x - m) / jnp.sqrt(v + eps)

def _scatter_add(tgt, idx, src, axis=0):
    return tgt.at[idx].add(src)

def _segment_sum(src, seg, n):
    return jax.ops.segment_sum(src, seg, n)
kernel_name = 'mk_vit_tower_postln_d2_tok_img768_r4_590d81'

def setup_inputs(seed: int=0):
    np.random.seed(seed)
    _w = jnp.asarray

    def _rec_inputs():
        import jax
        import jax.numpy as jnp
        _rk = jax.random.key(seed)
        x = -0.00016672 + 0.999947 * jax.random.normal(jax.random.fold_in(_rk, 1), (32, 96, 96, 3), jnp.float32)
        return x
    x = _rec_inputs()

    def _L0_tok_setup():
        import jax, jax.numpy as jnp
        import numpy as np
        PATCH = 16
        HIDDEN = 192

        def extract_patches(x, p):
            B, H, W, C = x.shape
            Hp, Wp = (H // p, W // p)
            x = x.reshape(B, Hp, p, Wp, p, C)
            x = x.transpose(0, 1, 3, 2, 4, 5)
            return x.reshape(B, Hp * Wp, p * p * C)
        key = jax.random.key(seed)
        k1, k2, k3, k4, k5 = jax.random.split(key, 5)
        B, H, W, C = (64, 96, 96, 3)
        num_patches = (H // PATCH) ** 2
        patch_dim = PATCH * PATCH * C
        contactMap = jax.random.normal(k1, (B, H, W, C), dtype=jnp.float32)
        W_proj = jax.random.normal(k2, (patch_dim, HIDDEN), dtype=jnp.float32) * (1.0 / np.sqrt(patch_dim))
        b_proj = jnp.zeros((HIDDEN,), dtype=jnp.float32)
        cls_token = jax.random.normal(k3, (1, 1, HIDDEN), dtype=jnp.float32) * 0.05
        pos_embedding = jax.random.normal(k4, (num_patches + 1, HIDDEN), dtype=jnp.float32) * 0.05
        return {'contactMap': contactMap, 'W_proj': W_proj, 'b_proj': b_proj, 'cls_token': cls_token, 'pos_embedding': pos_embedding}
    _L0_tok_all = _L0_tok_setup()
    _L0_tok_in = {k: v for k, v in _L0_tok_all.items() if k in ('W_proj', 'b_proj', 'cls_token', 'pos_embedding')}
    del _L0_tok_all

    def _L0_attn_setup():
        import jax, jax.numpy as jnp
        import numpy as np
        NUM_HEADS = 12

        def _split_heads(x, N, S):
            return x.reshape(N, S, NUM_HEADS, -1).transpose(0, 2, 1, 3)
        key = jax.random.key(seed)
        ks = jax.random.split(key, 12)
        N, S, E, R, RM = (8, 256, 192, 96, 64)
        hd = E // NUM_HEADS
        s = 0.02
        return {'hidden_states': jax.random.normal(ks[0], (N, S, E), dtype=jnp.float32), 'U_Q': jax.random.normal(ks[1], (R, E), dtype=jnp.float32) * s, 'V_Q': jax.random.normal(ks[2], (E, R), dtype=jnp.float32) * s, 'U_K': jax.random.normal(ks[3], (R, E), dtype=jnp.float32) * s, 'V_K': jax.random.normal(ks[4], (E, R), dtype=jnp.float32) * s, 'U_V': jax.random.normal(ks[5], (R, E), dtype=jnp.float32) * s, 'V_V': jax.random.normal(ks[6], (E, R), dtype=jnp.float32) * s, 'bias_q': jax.random.normal(ks[7], (E,), dtype=jnp.float32) * s, 'bias_k': jax.random.normal(ks[8], (E,), dtype=jnp.float32) * s, 'bias_v': jax.random.normal(ks[9], (E,), dtype=jnp.float32) * s, 'M_U': jax.random.normal(ks[10], (hd, RM), dtype=jnp.float32) * 0.1, 'M_V': jax.random.normal(ks[11], (RM, hd), dtype=jnp.float32) * 0.1}
    _L0_attn_all = _L0_attn_setup()
    _L0_attn_in = {k: v for k, v in _L0_attn_all.items() if k in ('U_Q', 'V_Q', 'U_K', 'V_K', 'U_V', 'V_V', 'bias_q', 'bias_k', 'bias_v', 'M_U', 'M_V')}
    del _L0_attn_all

    def _L0_ffn_setup():
        import jax, jax.numpy as jnp
        import numpy as np
        EPS_NORM = 1e-05
        RMS_EPS = 1e-05

        def _l2_normalize(v):
            n = jnp.sqrt(jnp.sum(v * v, axis=-1, keepdims=True))
            return v / jnp.maximum(n, EPS_NORM)

        def _rms_norm(x, weight, eps):
            ms = jnp.mean(x * x, axis=-1, keepdims=True)
            return x * jax.lax.rsqrt(ms + eps) * weight
        key = jax.random.key(seed)
        ks = jax.random.split(key, 6)
        B, T, D = (8, 1024, 192)
        S, F = (64, 768)
        x = jax.random.normal(ks[0], (B, T, D), dtype=jnp.float32)
        slots = 0.02 * jax.random.normal(ks[1], (S, D), dtype=jnp.float32)
        scale = jnp.ones((S,), dtype=jnp.float32)
        fc1_weight = 0.02 * jax.random.normal(ks[2], (S, D, F), dtype=jnp.float32)
        fc1_bias = jnp.zeros((S, F), dtype=jnp.float32)
        fc2_weight = 0.02 * jax.random.normal(ks[3], (S, F, D), dtype=jnp.float32)
        fc2_bias = jnp.zeros((S, D), dtype=jnp.float32)
        norm_weight = jnp.ones((D,), dtype=jnp.float32)
        return {'x': x, 'slots': slots, 'scale': scale, 'fc1_weight': fc1_weight, 'fc1_bias': fc1_bias, 'fc2_weight': fc2_weight, 'fc2_bias': fc2_bias, 'norm_weight': norm_weight}
    _L0_ffn_all = _L0_ffn_setup()
    _L0_ffn_in = {k: v for k, v in _L0_ffn_all.items() if k in ('slots', 'scale', 'fc1_weight', 'fc1_bias', 'fc2_weight', 'fc2_bias', 'norm_weight')}
    del _L0_ffn_all

    def _L1_attn_setup():
        import jax, jax.numpy as jnp
        import numpy as np
        H = 12

        def _attn(q, k, v):
            D = q.shape[-1]
            scores = jnp.einsum('bhnd,bhmd->bhnm', q, k) / jnp.sqrt(jnp.asarray(D, q.dtype))
            p = jax.nn.softmax(scores, axis=-1)
            return jnp.einsum('bhnm,bhmd->bhnd', p, v)
        key = jax.random.key(seed)
        ks = jax.random.split(key, 5)
        B, N, C = (2, 512, 192)
        s = 0.02
        return {'x': jax.random.normal(ks[0], (B, N, C), jnp.float32), 'Wq': jax.random.normal(ks[1], (C, 2 * C), jnp.float32) * s, 'Wk': jax.random.normal(ks[2], (C, 2 * C), jnp.float32) * s, 'Wv': jax.random.normal(ks[3], (C, C), jnp.float32) * s, 'lambda_p': jnp.zeros((H, 1, 1), jnp.float32), 'Wo': jax.random.normal(ks[4], (C, C), jnp.float32) * s, 'bo': jnp.zeros((C,), jnp.float32)}
    _L1_attn_all = _L1_attn_setup()
    _L1_attn_in = {k: v for k, v in _L1_attn_all.items() if k in ('Wq', 'Wk', 'Wv', 'lambda_p', 'Wo', 'bo')}
    del _L1_attn_all

    def _L1_ffn_setup():
        import jax, jax.numpy as jnp
        import numpy as np
        B, T, D = (2, 512, 192)
        S, R, M, K = (8, 16, 64, 4)
        H, G = (32, 64)

        def _ssinf3(x, P, C, W1, b1, W2, b2, G1, g1b, G2, g2b):
            shp = x.shape
            xf = x.reshape(-1, shp[-1])
            z = jnp.einsum('nd,sdr->nsr', xf, P)
            scores = jnp.einsum('nsr,smr->nsm', z, C)
            topv, topi = jax.lax.top_k(scores, K)
            w = jax.nn.softmax(topv, axis=-1)
            sidx = jnp.arange(S)[None, :, None]
            W1g = W1[sidx, topi]
            b1g = b1[sidx, topi]
            W2g = W2[sidx, topi]
            b2g = b2[sidx, topi]
            h = jax.nn.gelu(jnp.einsum('nsr,nskrh->nskh', z, W1g) + b1g)
            yl = jnp.einsum('nskh,nskhr->nskr', h, W2g) + b2g
            comb = jnp.einsum('nskr,nsk->nsr', yl, w)
            comb = comb.reshape(xf.shape[0], S * R)
            out = jax.nn.gelu(comb @ G1 + g1b) @ G2 + g2b
            return out.reshape(shp)
        key = jax.random.key(seed)
        k = jax.random.split(key, 8)
        rn = lambda kk, shape, s: jax.random.normal(kk, shape, dtype=jnp.float32) * s
        return {'x': rn(k[0], (B, T, D), 1.0), 'P': rn(k[1], (S, D, R), D ** (-0.5)), 'C': rn(k[2], (S, M, R), R ** (-0.5)), 'W1': rn(k[3], (S, M, R, H), R ** (-0.5)), 'b1': jnp.zeros((S, M, H), jnp.float32), 'W2': rn(k[4], (S, M, H, R), H ** (-0.5)), 'b2': jnp.zeros((S, M, R), jnp.float32), 'G1': rn(k[5], (S * R, G), (S * R) ** (-0.5)), 'g1b': jnp.zeros((G,), jnp.float32), 'G2': rn(k[6], (G, D), G ** (-0.5)), 'g2b': jnp.zeros((D,), jnp.float32)}
    _L1_ffn_all = _L1_ffn_setup()
    _L1_ffn_in = {k: v for k, v in _L1_ffn_all.items() if k in ('P', 'C', 'W1', 'b1', 'W2', 'b2', 'G1', 'g1b', 'G2', 'g2b')}
    del _L1_ffn_all
    return {'x': x, 'L0_tok_W_proj': _L0_tok_in['W_proj'], 'L0_tok_b_proj': _L0_tok_in['b_proj'], 'L0_tok_cls_token': _L0_tok_in['cls_token'], 'L0_tok_pos_embedding': _L0_tok_in['pos_embedding'], 'L0_attn_U_Q': _L0_attn_in['U_Q'], 'L0_attn_V_Q': _L0_attn_in['V_Q'], 'L0_attn_U_K': _L0_attn_in['U_K'], 'L0_attn_V_K': _L0_attn_in['V_K'], 'L0_attn_U_V': _L0_attn_in['U_V'], 'L0_attn_V_V': _L0_attn_in['V_V'], 'L0_attn_bias_q': _L0_attn_in['bias_q'], 'L0_attn_bias_k': _L0_attn_in['bias_k'], 'L0_attn_bias_v': _L0_attn_in['bias_v'], 'L0_attn_M_U': _L0_attn_in['M_U'], 'L0_attn_M_V': _L0_attn_in['M_V'], 'L0_ffn_slots': _L0_ffn_in['slots'], 'L0_ffn_scale': _L0_ffn_in['scale'], 'L0_ffn_fc1_weight': _L0_ffn_in['fc1_weight'], 'L0_ffn_fc1_bias': _L0_ffn_in['fc1_bias'], 'L0_ffn_fc2_weight': _L0_ffn_in['fc2_weight'], 'L0_ffn_fc2_bias': _L0_ffn_in['fc2_bias'], 'L0_ffn_norm_weight': _L0_ffn_in['norm_weight'], 'L1_attn_Wq': _L1_attn_in['Wq'], 'L1_attn_Wk': _L1_attn_in['Wk'], 'L1_attn_Wv': _L1_attn_in['Wv'], 'L1_attn_lambda_p': _L1_attn_in['lambda_p'], 'L1_attn_Wo': _L1_attn_in['Wo'], 'L1_attn_bo': _L1_attn_in['bo'], 'L1_ffn_P': _L1_ffn_in['P'], 'L1_ffn_C': _L1_ffn_in['C'], 'L1_ffn_W1': _L1_ffn_in['W1'], 'L1_ffn_b1': _L1_ffn_in['b1'], 'L1_ffn_W2': _L1_ffn_in['W2'], 'L1_ffn_b2': _L1_ffn_in['b2'], 'L1_ffn_G1': _L1_ffn_in['G1'], 'L1_ffn_g1b': _L1_ffn_in['g1b'], 'L1_ffn_G2': _L1_ffn_in['G2'], 'L1_ffn_g2b': _L1_ffn_in['g2b']}

def reference(x, L0_tok_W_proj, L0_tok_b_proj, L0_tok_cls_token, L0_tok_pos_embedding, L0_attn_U_Q, L0_attn_V_Q, L0_attn_U_K, L0_attn_V_K, L0_attn_U_V, L0_attn_V_V, L0_attn_bias_q, L0_attn_bias_k, L0_attn_bias_v, L0_attn_M_U, L0_attn_M_V, L0_ffn_slots, L0_ffn_scale, L0_ffn_fc1_weight, L0_ffn_fc1_bias, L0_ffn_fc2_weight, L0_ffn_fc2_bias, L0_ffn_norm_weight, L1_attn_Wq, L1_attn_Wk, L1_attn_Wv, L1_attn_lambda_p, L1_attn_Wo, L1_attn_bo, L1_ffn_P, L1_ffn_C, L1_ffn_W1, L1_ffn_b1, L1_ffn_W2, L1_ffn_b2, L1_ffn_G1, L1_ffn_g1b, L1_ffn_G2, L1_ffn_g2b):
    import jax
    import jax.numpy as jnp

    def _L0_tok_ref(contactMap, W_proj, b_proj, cls_token, pos_embedding):
        import jax, jax.numpy as jnp
        import numpy as np
        PATCH = 16
        HIDDEN = 192

        def extract_patches(x, p):
            B, H, W, C = x.shape
            Hp, Wp = (H // p, W // p)
            x = x.reshape(B, Hp, p, Wp, p, C)
            x = x.transpose(0, 1, 3, 2, 4, 5)
            return x.reshape(B, Hp * Wp, p * p * C)
        B = contactMap.shape[0]
        patches = extract_patches(contactMap, PATCH)
        enc = jnp.einsum('bnd,dh->bnh', patches, W_proj) + b_proj
        cls = jnp.broadcast_to(cls_token.astype(contactMap.dtype), (B, 1, enc.shape[-1]))
        enc = jnp.concatenate([cls, enc], axis=1)
        return enc + pos_embedding

    def _L0_attn_ref(hidden_states, U_Q, V_Q, U_K, V_K, U_V, V_V, bias_q, bias_k, bias_v, M_U, M_V):
        import jax, jax.numpy as jnp
        import numpy as np
        NUM_HEADS = 12

        def _split_heads(x, N, S):
            return x.reshape(N, S, NUM_HEADS, -1).transpose(0, 2, 1, 3)
        N, S, E = hidden_states.shape
        hd = E // NUM_HEADS
        scale = 1.0 / jnp.sqrt(jnp.asarray(hd, hidden_states.dtype))
        q = hidden_states @ V_Q @ U_Q + bias_q
        k = hidden_states @ V_K @ U_K + bias_k
        v = hidden_states @ V_V @ U_V + bias_v
        q = _split_heads(q, N, S)
        k = _split_heads(k, N, S)
        v = _split_heads(v, N, S)
        qm = jnp.einsum('bhsd,dr->bhsr', q, M_U)
        km = jnp.einsum('rd,bhtd->bhrt', M_V, k)
        attn = jnp.einsum('bhsr,bhrt->bhst', qm, km) * scale
        attn = jax.nn.softmax(attn, axis=-1)
        out = jnp.einsum('bhst,bhtd->bhsd', attn, v)
        out = out.transpose(0, 2, 1, 3).reshape(N, S, E)
        return out

    def _L0_ffn_ref(x, slots, scale, fc1_weight, fc1_bias, fc2_weight, fc2_bias, norm_weight):
        import jax, jax.numpy as jnp
        import numpy as np
        EPS_NORM = 1e-05
        RMS_EPS = 1e-05

        def _l2_normalize(v):
            n = jnp.sqrt(jnp.sum(v * v, axis=-1, keepdims=True))
            return v / jnp.maximum(n, EPS_NORM)

        def _rms_norm(x, weight, eps):
            ms = jnp.mean(x * x, axis=-1, keepdims=True)
            return x * jax.lax.rsqrt(ms + eps) * weight
        xn = _rms_norm(x, norm_weight, RMS_EPS)
        tok = _l2_normalize(xn)
        sl = _l2_normalize(slots) * scale[:, None]
        logits = jnp.einsum('sd,btd->bst', sl, tok)
        dispatch_w = jax.nn.softmax(logits, axis=-1)
        combine_w = jax.nn.softmax(logits, axis=-2)
        y = jnp.einsum('btd,bst->bsd', xn, dispatch_w)
        y = jnp.einsum('sio,bsi->bso', fc1_weight, y) + fc1_bias
        y = jax.nn.gelu(y, approximate=False)
        y = jnp.einsum('sio,bsi->bso', fc2_weight, y) + fc2_bias
        out = jnp.einsum('bsd,bst->btd', y, combine_w)
        return out

    def _L1_attn_ref(x, Wq, Wk, Wv, lambda_p, Wo, bo):
        import jax, jax.numpy as jnp
        import numpy as np
        H = 12

        def _attn(q, k, v):
            D = q.shape[-1]
            scores = jnp.einsum('bhnd,bhmd->bhnm', q, k) / jnp.sqrt(jnp.asarray(D, q.dtype))
            p = jax.nn.softmax(scores, axis=-1)
            return jnp.einsum('bhnm,bhmd->bhnd', p, v)
        B, N, C = x.shape
        D = C // H
        q = (x @ Wq).reshape(B, N, 2, H, D).transpose(2, 0, 3, 1, 4)
        k = (x @ Wk).reshape(B, N, 2, H, D).transpose(2, 0, 3, 1, 4)
        v = (x @ Wv).reshape(B, N, H, D).transpose(0, 2, 1, 3)
        out1 = _attn(q[0], k[0], v)
        out2 = _attn(q[1], k[1], v)
        lam = jnp.exp(lambda_p)
        out = out1 - lam * out2
        out = out.transpose(0, 2, 1, 3).reshape(B, N, C)
        return out @ Wo + bo

    def _L1_ffn_ref(x, P, C, W1, b1, W2, b2, G1, g1b, G2, g2b):
        import jax, jax.numpy as jnp
        import numpy as np
        B, T, D = (2, 512, 192)
        S, R, M, K = (8, 16, 64, 4)
        H, G = (32, 64)

        def _ssinf3(x, P, C, W1, b1, W2, b2, G1, g1b, G2, g2b):
            shp = x.shape
            xf = x.reshape(-1, shp[-1])
            z = jnp.einsum('nd,sdr->nsr', xf, P)
            scores = jnp.einsum('nsr,smr->nsm', z, C)
            topv, topi = jax.lax.top_k(scores, K)
            w = jax.nn.softmax(topv, axis=-1)
            sidx = jnp.arange(S)[None, :, None]
            W1g = W1[sidx, topi]
            b1g = b1[sidx, topi]
            W2g = W2[sidx, topi]
            b2g = b2[sidx, topi]
            h = jax.nn.gelu(jnp.einsum('nsr,nskrh->nskh', z, W1g) + b1g)
            yl = jnp.einsum('nskh,nskhr->nskr', h, W2g) + b2g
            comb = jnp.einsum('nskr,nsk->nsr', yl, w)
            comb = comb.reshape(xf.shape[0], S * R)
            out = jax.nn.gelu(comb @ G1 + g1b) @ G2 + g2b
            return out.reshape(shp)
        return _ssinf3(x, P, C, W1, b1, W2, b2, G1, g1b, G2, g2b)
    h = _L0_tok_ref(x, L0_tok_W_proj, L0_tok_b_proj, L0_tok_cls_token, L0_tok_pos_embedding)
    h = _layernorm(h + _L0_attn_ref(h, L0_attn_U_Q, L0_attn_V_Q, L0_attn_U_K, L0_attn_V_K, L0_attn_U_V, L0_attn_V_V, L0_attn_bias_q, L0_attn_bias_k, L0_attn_bias_v, L0_attn_M_U, L0_attn_M_V), axis=-1)
    h = _layernorm(h + _L0_ffn_ref(h, L0_ffn_slots, L0_ffn_scale, L0_ffn_fc1_weight, L0_ffn_fc1_bias, L0_ffn_fc2_weight, L0_ffn_fc2_bias, L0_ffn_norm_weight), axis=-1)
    h = _layernorm(h + _L1_attn_ref(h, L1_attn_Wq, L1_attn_Wk, L1_attn_Wv, L1_attn_lambda_p, L1_attn_Wo, L1_attn_bo), axis=-1)
    h = _layernorm(h + _L1_ffn_ref(h, L1_ffn_P, L1_ffn_C, L1_ffn_W1, L1_ffn_b1, L1_ffn_W2, L1_ffn_b2, L1_ffn_G1, L1_ffn_g1b, L1_ffn_G2, L1_ffn_g2b), axis=-1)
    return h

_drawn_inputs = setup_inputs


def setup_inputs(seed=0):
    import zlib

    import numpy as np

    out = dict(_drawn_inputs(seed))
    spreads = {'L0_tok_b_proj': (0.0, 0.1),
     'L0_ffn_scale': (1.0, 0.6),
     'L0_ffn_fc1_bias': (0.0, 0.748),
     'L0_ffn_fc2_bias': (0.0, 0.356),
     'L0_ffn_norm_weight': (1.0, 0.6),
     'L1_attn_lambda_p': (0.0, 0.8),
     'L1_attn_bo': (0.0, 0.338),
     'L1_ffn_b1': (0.0, 0.421),
     'L1_ffn_b2': (0.0, 0.274),
     'L1_ffn_g1b': (0.0, 0.1),
     'L1_ffn_g2b': (0.0, 0.1)}
    factors = {'L0_attn_U_Q': 8.0,
     'L0_attn_V_Q': 8.0,
     'L0_attn_U_K': 8.0,
     'L0_attn_V_K': 8.0,
     'L0_attn_bias_q': 8.0,
     'L0_attn_bias_k': 64.0,
     'L0_attn_M_U': 8.0,
     'L0_attn_M_V': 8.0,
     'L0_ffn_slots': 8.0,
     'L0_ffn_fc1_weight': 8.0,
     'L0_ffn_fc2_weight': 5.437,
     'L1_attn_Wq': 8.0,
     'L1_attn_Wk': 8.0,
     'L1_attn_Wv': 7.086,
     'L1_attn_Wo': 7.005}
    for name, (base, spread) in spreads.items():
        noise = np.random.default_rng([zlib.crc32(name.encode()), seed]).standard_normal(out[name].shape)
        drawn = base * np.exp(spread * noise) if base else spread * noise
        out[name] = jnp.asarray(drawn.astype(out[name].dtype))
    for name, factor in factors.items():
        out[name] = (out[name] * factor).astype(out[name].dtype)
    return out
```

```python
from contextlib import ExitStack

import concourse.bass as bass
from concourse import mybir

B, T, D = 32, 37, 192
NPATCH = T - 1
PD = 768
PC = PD // 128
NH, HD = 12, 16
HH = NH // 2
FH = D // 2
R0 = 96
RM = 64
SLOTS = 64
HID = 768
HC = HID // 128
PAIRS = B // 2
QP = 4
QB = 2 * QP
QUADS = PAIRS // QP
QT = QB * T
ROWS = 64 + T
GS = 4
GROUPS = SLOTS // GS
TOK = B * T
SEG, SR, SM, SH, SK, SG = 8, 16, 64, 32, 4, 64
CH = SM * SH // 128
TC = 396
TP = 3 * TC
TT = 10
TZ = TT * 128
PARTS = 3
ZR = 6 * SR + PARTS
EPS = 1e-5
TINY = 1e-10
LOW = -3.0e38
WORK = 12310


def tower(nc, io):
    f32 = mybir.dt.float32
    bf16 = mybir.dt.bfloat16
    ALU = mybir.AluOpType
    ACT = mybir.ActivationFunctionType
    AX = mybir.AxisListType.X
    ds = bass.ds

    def spread(ap, axis, n):
        ap = ap.unsqueeze(axis)
        shape = list(ap.shape)
        shape[axis] = n
        return ap.to_broadcast(shape)

    def nth(step, per, n):
        return step * per + n

    def settle(eng, s, value):
        eng.wait_ge(s, value)
        eng.sem_inc(s_settled, 1)

    with ExitStack() as ctx:
        def sb(name, shape, dt=f32):
            return ctx.enter_context(nc.sbuf_tensor(name, shape, dt))

        def sem(name):
            return ctx.enter_context(nc.semaphore(name))

        def dram(name, shape, dt):
            return nc.dram_tensor(name, shape, dt, kind="Internal").ap()

        EXPERT, KH, ZW = 2 * GS * HID, 2 * QB * HH * T, SEG * TP // 2
        early = sb("early", [128, PC * QB * T + PC * D + KH + 2 * SLOTS * B])
        stream = sb("stream", [128, 2 * EXPERT + 2 * HC * GS * D])

        def tenant(home, rows, at, shape, dt=f32):
            n = 1
            for x in shape:
                n *= x
            words = n // (2 if dt == bf16 else 1)
            ap = home[0:rows, at:at + words]
            if dt != f32:
                ap = ap.bitcast(dt)
            names = "abcde"[:len(shape)]
            kw = {c: x for c, x in zip(names, shape)}
            return ap.rearrange(f"p ({' '.join(names)}) -> p {' '.join(names)}", **kw)

        class Tenants:
            def __init__(self, home, at=0):
                self.home, self.at = home, at

            def __call__(self, shape, dt=f32):
                ap = tenant(self.home, shape[0], self.at, shape[1:], dt)
                n = 1
                for x in shape[1:]:
                    n *= x
                self.at += n // (2 if dt == bf16 else 1)
                assert self.at <= self.home.shape[1], (self.at, self.home.shape)
                return ap

        patches = tenant(early, 128, 0, [PC, QB, T])
        w_patch = tenant(early, 128, PC * QB * T, [PC, D])
        k_heads0 = tenant(early, FH, PC * QB * T + PC * D, [1, 2, QB, HH, T])
        y_t = tenant(early, FH + 1, PC * QB * T + PC * D + KH, [2, SLOTS, B])
        fc1 = tenant(stream, FH + 1, 0, [2, 2, GS, HID])
        fc2 = tenant(stream, 128, 2 * EXPERT, [2, HC, GS, D])
        k_heads1 = tenant(stream, FH, 0, [2, 2, QB, HH, T])
        w1s = tenant(stream, ZR, 2 * EXPERT + 2 * HC * GS * D - SEG * SM * SH // 2, [SEG, SM * SH], bf16)
        late = Tenants(stream, KH * 2)
        w_q1 = late([FH, 2, 2 * D]); w_k1 = late([FH, 2, 2 * D]); w_v1 = late([FH, 2, D]); w_o1 = late([FH, 2, D])
        gate_parts = tenant(stream, 128, 0, [PARTS, 4, TZ], bf16)
        zs = tenant(stream, ZR, PARTS * 4 * TZ // 2, [SEG, TP], bf16)
        ws = tenant(early, PARTS * 32, 0, [2 * SEG, TP], bf16)

        ident = sb("ident", [128, 128])
        hmask = sb("hmask", [FH, HH])
        bmask = sb("bmask", [FH, FH])
        rowc = sb("rowc", [128, 6, D])
        embed_add = sb("embed_add", [128, D])
        lam = sb("lam", [128, NH])
        negh = sb("negh", [128, QP])
        prep = Tenants(early, PC * QB * T + PC * D + KH)
        v_q_t = prep([R0, D]); u_q_t = prep([FH, 2, R0])
        v_k_t = prep([R0, D]); u_k = prep([R0, D])
        v_v_t = prep([R0, D]); u_v = prep([R0, D])
        m_u = prep([RM, FH]); m_v = prep([RM, FH])
        bias_qk = sb("bias_qk", [FH, 2, 2])
        mixer = prep([FH, FH])
        u_qm = prep([R0, D])
        middle = sb("middle", [128, PARTS * 4 * 64 + SM // 8 * 64])
        w = Tenants(middle)
        w_q0 = w([FH, 2, D]); w_k0 = w([FH, 2, D]); w_v0 = w([FH, 2, D])
        w = Tenants(middle)
        b2s = w([128, PARTS, 4, 128], bf16)
        gate_sel = w([PARTS * 32, SM // 8, 128], bf16)
        bias_qm = sb("bias_qm", [FH, 2])
        bias_km = sb("bias_km", [FH, 2, HH])
        slots = prep([SLOTS, D]); slot_scale = sb("slot_scale", [SLOTS, 1])
        slot_n = sb("slot_n", [SLOTS, 4])
        slot_dir = prep([SLOTS, D])
        slots_t = sb("slots_t", [FH, 2, SLOTS])

        slot_sel = sb("slot_sel", [GS, 128])
        out1_b = sb("out1_b", [SG, 1])

        h1_all = sb("h1_all", [128, PAIRS, D])
        h3_all = h1_all
        combine_all = sb("combine_all", [128, PAIRS, ROWS])

        work = sb("work", [128, WORK])
        w = Tenants(work)
        v_blk = w([128, QB, HH, 2 * (HD + 1)])
        probs = w([128, 2, HH, 2, 64])
        h_in = w([128, QP, D])
        attn = w([128, QP, D])
        attn2 = w([128, 2, D])
        row_max = w([128, 2, NH])
        rsum = w([128, 2, 2, NH])
        stats = w([128, QP, 6]); mv = w([128, QP, 2])
        rstd = w([128, QP]); var_e = w([128, QP])
        h_out = w([128, QP, D])
        norms = w([128, 4, QP])
        small = w([128, 6, QP])
        rmx = w([128, 6, QP])
        shared = w.at
        h_t = w([FH, 2, QB, T])
        q_t = w([FH, 2, 2, QB * T])
        sq = tenant(work, 128, w.at, [QP, D])
        shifted = w([128, 2, NH, T])
        probs_t = w([128, 2, HH, ROWS])
        tok_t = w([FH, QP, 2, ROWS])
        xn = w([128, QP, D])
        tok = attn
        r = Tenants(work, shared)
        cw2 = r([128, QP, SLOTS])
        dw = r([128, QP, T]); dw2 = r([128, QP, T])
        disp = r([128, QP, SLOTS])
        ce = r([128, QP, SLOTS]); de = r([128, QP, T])
        cw = sb("cw", [128, QP, 2 * SLOTS])
        w = Tenants(work, shared)
        y_ring = w([FH + 1, 2, 2, GS * B])
        hidden = w([128, 2, 2, HID // 2])
        hidden_t = w([128, 2, HC, 128])
        y_out = w([128, 2, D])
        moe_end = w.at
        w = Tenants(work)
        w2 = w([128, CH, SEG, 32])
        act_out = w([128, 4, TC])
        gated = w([128, 4, TC])
        z = w([128, TZ])
        z_left = w([128, TP])
        z_parts = w([128, PARTS, TP], bf16)
        mlp_out = w([128, 2, TC])
        w = Tenants(work, CH * SEG * 32)
        scored = w([128, 2, 2, SEG, SM + SK])
        z_tile = w([128, 2, 128])
        top8 = w([128, 2, SEG, 8]); top4 = w([128, 2, SEG, 8])
        top_e = w([128, 2, SEG, SK])
        gate_sum = w([128, 2, 2, SEG])
        assert w.at <= CH * SEG * 32 + 8 * TC
        w = Tenants(early)
        y2 = w([128, PAIRS, D])
        x3_t = w([FH, 2, B, T])
        comb_r = w([128, QP, ROWS])
        gate_e = w([128, 2, SEG * SM])
        gate = w([128, 2, SEG * SM])
        gate_left = w([128, 2, SEG * SM])
        assert w.at <= SEG * TP

        P = ctx.enter_context(nc.psum_tensor("P", [128, 8, 512], f32))

        def bank(n):
            return P[:, n, :]

        s_small = sem("s_small_loaded")
        s_psum0 = sem("s_psum_cleared")
        s_prep_pe = sem("s_prep_products")
        s_prep_dve = sem("s_prep_taken")
        s_prep_pool = sem("s_prep_powers")
        s_patches = sem("s_patches_loaded")
        s_emb = sem("s_embedded")
        s_hin = sem("s_h_in_ready")
        s_done = sem("s_done")
        s_settled = sem("s_settled_waits")
        s_slot_dir = sem("s_slot_dir"); s_slot_sum = sem("s_slot_sum"); s_consts = sem("s_consts_set"); s_vz = sem("s_v_blk_cleared"); s_prep_misc = sem("s_prep_weights")

        NORM = "resid stats mv var rstd h_out"
        TURN = "h_turned h_t"
        ATTENTION = ("q_made k_made v_made q_ready k_ready_a k_ready_v v_ready scores row_max shifted probs "
                     "probs_turned probs_t mixed sums normed")

        def layer_sems(p, *names):
            return {n: sem(f"{p}_{n}") for n in " ".join(names).split()}

        L0 = layer_sems("l0", TURN, ATTENTION, NORM)
        s_ssq = sem("s_square_sums"); s_ms = sem("s_mean_squares"); s_rr = sem("s_rms")
        s_xn = sem("s_xn"); s_n2 = sem("s_norm_squares"); s_tn = sem("s_tok_norms"); s_tok = sem("s_tok")
        s_tokp = sem("s_tok_turned"); s_tokt = sem("s_tok_t")
        s_lg = sem("s_logits"); s_lt = sem("s_logits_t")
        s_cd = sem("s_routing_steps"); s_ce = sem("s_routing_exps")
        s_cp = sem("s_combine_turned"); s_ct = sem("s_combine_t")
        s_dp = sem("s_dispatch_turned"); s_dt = sem("s_dispatch")
        s_y = sem("s_slot_inputs"); s_yt = sem("s_slot_inputs_taken")
        s_keep = sem("s_h1_kept")


        SMALL_LOADS = [
            (ident, "ident"), (hmask, "hmask"), (bmask, "bmask"), (rowc, "rowc"), (lam, "lam"), (w_patch, "w_patch"),
            (v_q_t, "v_q_t"), (u_q_t, "u_q_t"), (v_k_t, "v_k_t"), (u_k, "u_k"), (v_v_t, "v_v_t"), (u_v, "u_v"),
            (m_u, "m_u"), (m_v, "m_v"), (bias_qk, "bias_qk"), (slots, "slots"), (slot_scale, "slot_scale"),
            (slot_sel, "slot_sel"), (out1_b, "out1_b")]
        SMALL = 16 * len(SMALL_LOADS)

        def pe_turn(pe, L, it, src, ready, per, past=0):
            for j in range(QP):
                pe.wait_ge(ready, nth(it, per, past * per + j + 1))
                for kc in range(2):
                    at = ((j % 2) * 2 + kc) * 128
                    mm = pe.transpose(P[0:FH, 4 + j // 2, at:at + ROWS],
                                      src[0:ROWS, j, kc * FH:(kc + 1) * FH], ident[0:ROWS, 0:ROWS])
                if j % 2:
                    mm.then_inc(L["h_turned"], 1)

        def take_turned(eng, copy, L, it, g, dst):
            eng.wait_ge(L["h_turned"], nth(it, 2, g + 1))
            src = P[0:FH, 4 + g, :].rearrange("p (j k e r) -> p j k e r", j=2, k=2, e=2)
            for j in range(2):
                copy(dst[:, :, 4 * g + 2 * j:4 * g + 2 * j + 2, :], src[:, j, :, :, 0:T]).then_inc(L["h_t"], 1)

        def pe_qk(pe, L, it, maps, w_q, w_k):
            pe.wait_ge(L["h_t"], nth(it, QP, QP))
            for m in range(maps):
                if m:
                    pe.wait_ge(L["q_ready"], nth(it, 2 * maps, 2))
                    pe.wait_ge(L["k_ready_a"], nth(it, HH * maps, HH))
                    pe.wait_ge(L["k_ready_v"], nth(it, HH * maps, HH))
                for w, at, made in ((w_q, 0, "q_made"), (w_k, 2, "k_made")):
                    for mc in range(2):
                        for kc in range(2):
                            mm = pe.matmul(P[0:FH, at + mc, 0:QT], w[:, kc, m * D + mc * FH:m * D + (mc + 1) * FH],
                                           h_t[:, kc, :, :], start=(kc == 0), stop=(kc == 1))
                        mm.then_inc(L[made], 1)

        def pe_v(pe, L, it, w_v):
            for b in range(QB):
                for e in range(2):
                    for kc in range(2):
                        mm = pe.matmul(P[64 * e:64 * e + T, 6 + b // 4, (b % 4) * FH:(b % 4 + 1) * FH],
                                       h_t[:, kc, b, :], w_v[:, kc, e * FH:(e + 1) * FH],
                                       start=(kc == 0), stop=(kc == 1), skip_group_check=True)
                if b % 4 == 3:
                    mm.then_inc(L["v_made"], 1)

        def pe_scores(pe, L, it, maps, u, k_heads):
            j, m = u // maps, u % maps
            if u == 0:
                pe.wait_ge(L["q_ready"], nth(it, 2 * maps, 2 * maps))
                pe.wait_ge(L["k_ready_a"], nth(it, HH * maps, HH * maps))
                pe.wait_ge(L["k_ready_v"], nth(it, HH * maps, HH * maps))
            if u >= 2:
                pe.wait_ge(L["shifted"], nth(it, QP * maps, u - 1))
            for e in range(2):
                b = 2 * j + e
                for mc in range(2):
                    mm = pe.matmul(P[64 * e:64 * e + T, u % 2, mc * HH * T:(mc + 1) * HH * T],
                                   q_t[:, m, mc, b * T:(b + 1) * T], k_heads[:, m, mc, b, :, :],
                                   start=True, stop=True, skip_group_check=True)
            mm.then_inc(L["scores"], 1)

        def pe_turn_probs(pe, L, it, maps, u):
            pe.wait_ge(L["probs"], nth(it, QP * maps, u + 1))
            if u == 0:
                pe.wait_ge(L["v_ready"], nth(it, 4, 4))
            for hp in range(HH):
                mm = pe.transpose(P[:, 4 + 2 * (u % 2) + hp // 3, (hp % 3) * ROWS:(hp % 3 + 1) * ROWS],
                                  probs[0:ROWS, u % 2, hp, :, :].rearrange("p a k -> p (a k)"), ident[0:ROWS, 0:ROWS])
            mm.then_inc(L["probs_turned"], 1)

        def pe_mix(pe, L, it, maps, u):
            j = u // maps
            pe.wait_ge(L["probs_t"], nth(it, QP * maps, u + 1))
            if u >= 2:
                pe.wait_ge(L["normed"], nth(it, QP * maps, u - 1))
            for e in range(2):
                for hp in range(HH):
                    w2 = 2 * (HD + 1)
                    mm = pe.matmul(P[64 * e:64 * e + T, 2 + u % 2, hp * w2:(hp + 1) * w2],
                                   probs_t[0:ROWS, u % 2, hp, 64 * e:64 * e + T], v_blk[0:ROWS, 2 * j + e, hp, :],
                                   start=True, stop=True, skip_group_check=True)
            mm.then_inc(L["mixed"], 1)

        def pe_attention(pe, L, it, maps, k_heads):
            U = QP * maps
            for k in range(U + 2):
                if k < U:
                    pe_scores(pe, L, it, maps, k, k_heads)
                if 1 <= k <= U:
                    pe_turn_probs(pe, L, it, maps, k - 1)
                if k >= 2:
                    pe_mix(pe, L, it, maps, k - 2)

        def act_q(act, L, it, maps, bias, k_heads):
            for m in range(maps):
                for mc in range(2):
                    act.wait_ge(L["q_made"], nth(it, 2 * maps, 2 * m + mc + 1))
                    act.activation(q_t[:, m, mc, :], P[0:FH, mc, 0:QT], ACT.Identity,
                                   bias=0.0 if bias is None else bias[:, mc:mc + 1]).then_inc(L["q_ready"], 1)
                act.wait_ge(L["k_made"], nth(it, 2 * maps, 2 * m + 1))
                for h in range(HH):
                    act.activation(k_heads[:, m, 0, :, h, :], P[0:FH, 2, 0:QT].rearrange("p (b t) -> p b t", t=T),
                                   ACT.Identity, scale=hmask[:, h:h + 1],
                                   bias=0.0 if bias is None else bias_km[:, 0, h:h + 1]).then_inc(L["k_ready_a"], 1)

        def dve_k(dve, L, it, maps, bias, k_heads):
            for m in range(maps):
                dve.wait_ge(L["k_made"], nth(it, 2 * maps, 2 * m + 2))
                for h in range(HH):
                    src = P[0:FH, 3, 0:QT].rearrange("p (b t) -> p b t", t=T)
                    if bias is None:
                        ins = dve.tensor_scalar(k_heads[:, m, 1, :, h, :], src, hmask[:, h:h + 1], None, ALU.mult)
                    else:
                        ins = dve.tensor_scalar(k_heads[:, m, 1, :, h, :], src, hmask[:, h:h + 1],
                                                bias_km[:, 1, h:h + 1], ALU.mult, ALU.add)
                    ins.then_inc(L["k_ready_v"], 1)

        def dve_v(dve, L, it, bias):
            for half in range(2):
                dve.wait_ge(L["v_made"], nth(it, 2, half + 1))
                for e in range(2):
                    rows = slice(64 * e, 64 * e + T)
                    src = P[rows, 6 + half, 0:4 * FH].rearrange("p (b h d) -> p b h d", b=4, d=HD)
                    dst = v_blk[rows, 4 * half:4 * half + 4, :, e * (HD + 1):e * (HD + 1) + HD]
                    if bias:
                        add = spread(rowc[rows, 3, 0:FH].rearrange("p (h d) -> p h d", d=HD), 1, 4)
                        ins = dve.tensor_tensor(dst, src, add, ALU.add)
                    else:
                        ins = dve.tensor_copy(dst, src)
                    ins.then_inc(L["v_ready"], 1)

        def dve_softmax(dve, L, it, maps, u):
            src = P[0:ROWS, u % 2, 0:NH * T].rearrange("p (h k) -> p h k", k=T)
            dve.wait_ge(L["scores"], nth(it, QP * maps, u + 1))
            dve.tensor_reduce(row_max[0:ROWS, u % 2, :], src, AX, ALU.max).then_inc(L["row_max"], 1)
            dve.wait_ge(L["row_max"], nth(it, QP * maps, u + 1))
            if u >= 2:
                dve.wait_ge(L["probs"], nth(it, QP * maps, u - 1))
            dve.tensor_tensor(shifted[0:ROWS, u % 2, :, :], src, spread(row_max[0:ROWS, u % 2, :], 2, T),
                              ALU.subtract).then_inc(L["shifted"], 1)

        def act_exp(act, L, it, maps, u):
            act.wait_ge(L["shifted"], nth(it, QP * maps, u + 1))
            act.activation(probs[0:ROWS, u % 2, :, :, 0:T].rearrange("p a b k -> p (a b) k"), shifted[0:ROWS, u % 2, :, :],
                           ACT.Exp, scale=HD ** -0.5).then_inc(L["probs"], 1)

        def act_probs_t(act, L, it, maps, u):
            act.wait_ge(L["probs_turned"], nth(it, QP * maps, u + 1))
            if u >= 2:
                act.wait_ge(L["mixed"], nth(it, QP * maps, u - 1))
            act.activation(probs_t[:, u % 2, :, :].rearrange("p (g h) t -> p g (h t)", g=2),
                           P[:, 4 + 2 * (u % 2):6 + 2 * (u % 2), 0:3 * ROWS], ACT.Copy).then_inc(L["probs_t"], 1)

        def act_attention(act, L, it, maps):
            U = QP * maps
            for k in range(U + 1):
                if k < U:
                    act_exp(act, L, it, maps, k)
                if k >= 1:
                    act_probs_t(act, L, it, maps, k - 1)

        def dve_norm(dve, L, it, maps, u):
            j, m = u // maps, u % maps
            U = QP * maps
            o = P[0:ROWS, 2 + u % 2, 0:NH * (HD + 1)].rearrange("p (h c) -> p h c", c=HD + 1)
            r = rsum[0:ROWS, u % 2]
            dve.wait_ge(L["mixed"], nth(it, U, u + 1))
            step = nth(it, QP * (2 if maps == 1 else 5), j * (2 if maps == 1 else 5) + 2 * m)
            dve.tensor_scalar(r[:, 0, :], o[:, :, HD], 0.5, None, ALU.max).then_inc(L["sums"], 1)
            dve.wait_ge(L["sums"], step + 1)
            dve.reciprocal(r[:, 1, :], r[:, 0, :]).then_inc(L["sums"], 1)
            dve.wait_ge(L["sums"], step + 2)
            if m:
                dve.tensor_tensor(r[:, 0, :], r[:, 1, :], lam[0:ROWS, :], ALU.mult).then_inc(L["sums"], 1)
                dve.wait_ge(L["sums"], step + 3)
            out = attn[0:ROWS, j, :] if m == 0 else attn2[0:ROWS, j % 2, :]
            by = r[:, 0 if m else 1, :]
            out = out.rearrange("p (h d) -> p h d", d=HD)
            dve.tensor_tensor(out, o[:, :, 0:HD], spread(by, 2, HD), ALU.mult).then_inc(L["normed"], 1)
            if m:
                dve.wait_ge(L["normed"], nth(it, U, u + 1))
                dve.tensor_tensor(attn[0:ROWS, j, :], attn[0:ROWS, j, :], attn2[0:ROWS, j % 2, :],
                                  ALU.subtract).then_inc(L["mapped"], 1)

        def dve_attention(dve, L, it, maps):
            U = QP * maps
            for k in range(U + 2):
                if k < U:
                    dve_softmax(dve, L, it, maps, k)
                if k >= 2:
                    dve_norm(dve, L, it, maps, k - 2)

        def pe_turn_rows(pe, it, src, ready, turned):
            for j in range(QP):
                pe.wait_ge(ready, nth(it, QP, j + 1))
                for kc in range(2):
                    at = ((j % 2) * 2 + kc) * ROWS
                    mm = pe.transpose(P[0:FH, 4 + j // 2, at:at + ROWS], src[0:ROWS, j, kc * FH:(kc + 1) * FH],
                                      ident[0:ROWS, 0:ROWS])
                if j % 2:
                    mm.then_inc(turned, 1)

        def take_rows(act, it, turned, taken):
            for g in range(2):
                act.wait_ge(turned, nth(it, 2, g + 1))
                act.copy(tok_t[:, 2 * g:2 * g + 2, :, :].rearrange("p j k t -> p (j k t)"),
                         P[0:FH, 4 + g, 0:4 * ROWS]).then_inc(taken, 1)

        def dve_ln(dve, L, it, src, dst):
            for j in range(QP):
                dve.wait_ge(L["resid"], nth(it, QP, j + 1))
                dve.bn_stats(stats[0:ROWS, j, :], src[0:ROWS, j, :]).then_inc(L["stats"], 1)
            for j in range(QP):
                settle(dve, L["stats"], nth(it, QP, j + 1))
                dve.bn_aggr(mv[0:ROWS, j, :], stats[0:ROWS, j, :]).then_inc(L["mv"], 1)
            dve.wait_ge(L["rstd"], nth(it, 1, 1))
            for j in range(QP):
                dve.tensor_scalar(dst[0:ROWS, j, :], src[0:ROWS, j, :], mv[0:ROWS, j, 0:1], rstd[0:ROWS, j:j + 1],
                                  ALU.subtract, ALU.mult).then_inc(L["h_out"], 1)

        def pool_rstd(pool, L, it):
            settle(pool, L["mv"], nth(it, QP, QP))
            pool.tensor_scalar(var_e[0:ROWS, :], mv[0:ROWS, :, 1], EPS, None, ALU.add).then_inc(L["var"], 1)
            pool.wait_ge(L["var"], nth(it, 1, 1))
            pool.tensor_tensor(rstd[0:ROWS, :], var_e[0:ROWS, :], negh[0:ROWS, :], ALU.pow).then_inc(L["rstd"], 1)
        fc2_b = sb("fc2_b", [GS, 2, D])
        w = Tenants(stream, PARTS * 4 * TZ // 2 + ZW)
        z_proj = w([FH, 2, 128]); out1_w = w([128, 2, SG]); out2_w = w([SG, D])
        w = Tenants(early, SEG * TP)
        score_w = w([128, SEG * SM])
        w = Tenants(work, moe_end)
        split_in = w([128, 512]); split_left = w([128, 512])
        split_out = w([128, PARTS, 512], bf16)
        out_t = tenant(combine_all[:, :, :].rearrange("p a b -> p (a b)"), SG, 0, [TP])
        out_r = tenant(work, SG, CH * SEG * 32 + 8 * TC, [QB, T])
        y_dram = dram("y_dram", [SLOTS, B, D], f32)
        w1_dram = dram("w1_dram", [PARTS, 128, SM * SH], bf16)
        b1_dram = dram("b1_dram", [PARTS, 128, 128], bf16)
        z_dram = dram("z_dram", [PARTS, 128, TP], bf16)
        s_late2 = sem("s_mlp_weights_loaded")
        s_fc1 = [sem("s_fc1_even"), sem("s_fc1_odd")]
        s_fc2 = [sem("s_fc2_even"), sem("s_fc2_odd")]
        s_yr = sem("s_slot_inputs_staged"); s_hid = sem("s_hidden_made"); s_act = sem("s_hidden_active")
        s_hp = sem("s_hidden_turned"); s_ht = sem("s_hidden_t"); s_fo = sem("s_slots_out_made")
        s_yo = sem("s_slots_out_taken"); s_yd = [sem("s_slots_out_stored_even"), sem("s_slots_out_stored_odd")]
        s_split_in = sem("s_split_loaded"); s_split = sem("s_split_steps"); s_split_out = sem("s_split_stored")
        s_b2 = sem("s_b2_loaded")
        s_late = sem("s_late_weights_loaded"); s_y2 = sem("s_slot_outputs_loaded")
        s_lam = sem("s_lambda"); s_cr = sem("s_combine_staged"); s_mix = sem("s_combined")
        L1 = layer_sems("l1", TURN, ATTENTION, "mapped")
        LO = layer_sems("lo", NORM, TURN)
        s_at = sem("s_attn_turned"); s_att = sem("s_attn_t"); s_wo = sem("s_attn_projected")
        s_hb = sem("s_h_in_and_bias"); s_h3 = sem("s_h3_kept"); s_x3p = sem("s_x3_turned")
        s_w1s = sem("s_w1_stacked"); s_w2 = sem("s_w2_loaded")
        s_z = sem("s_z_made"); s_zc = sem("s_z_taken"); s_zp = sem("s_z_split_steps"); s_zd = sem("s_z_parts_stored")
        s_zs = sem("s_z_parts_stacked"); s_set = sem("s_mlp_ones_set"); s_zb = sem("s_mlp_padding_set")
        s_zt = sem("s_z_tile"); s_sc = sem("s_scores_made"); s_sr = sem("s_scores_taken"); s_mx = sem("s_top8"); s_t4 = sem("s_top4")
        s_rp = sem("s_top_marked"); s_gs = sem("s_gate_steps"); s_gate = sem("s_gates")
        s_sh = sem("s_scores_shifted"); s_ge = sem("s_gate_exps"); s_gt = sem("s_gates_turned")
        s_g0 = sem("s_gate_first_part"); s_g1 = sem("s_gate_second_part"); s_g2 = sem("s_gate_third_part")
        s_gl = sem("s_gate_rest"); s_ws = sem("s_gate_parts_stacked")
        s_u1 = sem("s_unit_hidden"); s_bc = sem("s_unit_gate_spread"); s_ua = sem("s_unit_active")
        s_ug = sem("s_unit_gated"); s_u2 = sem("s_unit_summed")
        s_ac = sem("s_segments_taken"); s_o1 = sem("s_out1_made"); s_ot = sem("s_out1_active")
        s_or = sem("s_out1_staged"); s_o2 = sem("s_out2_made"); s_out = sem("s_out_stored")

        def moe_sync_first(sp):
            for g in range(2):
                sp.dma_start(fc1[:, g], io["fc1"][g]).then_inc(s_fc1[g], 16)
                sp.dma_start(fc2[:, g], io["fc2"][g]).then_inc(s_fc2[g], 16)
                sp.dma_start(fc2_b[:, g, :], io["fc2_b"][g]).then_inc(s_fc2[g], 16)

        def moe_sync(sp):
            def store(g, u):
                sp.dma_start(y_dram.rearrange("s b d -> (s b) d")[ds(g * 128, 128), :], y_out[:, u, :]).then_inc(s_yd[u], 16)

            with sp.Fori(1, GROUPS // 2) as it:
                for u in range(2):
                    sp.wait_ge(s_hid, it * 2 + (u - 1))
                    sp.dma_start(fc1[:, u], io["fc1"][it * 2 + u]).then_inc(s_fc1[u], 16)
                    sp.wait_ge(s_fo, it * 2 + (u - 1))
                    sp.dma_start(fc2[:, u], io["fc2"][it * 2 + u]).then_inc(s_fc2[u], 16)
                    sp.dma_start(fc2_b[:, u, :], io["fc2_b"][it * 2 + u]).then_inc(s_fc2[u], 16)
                    sp.wait_ge(s_yo, it * 2 + (u - 1))
                    store(it * 2 + (u - 2), u)
            for g in (GROUPS - 2, GROUPS - 1):
                sp.wait_ge(s_yo, g + 1)
                store(g, g % 2)
            for dst, name in ((w_q1, "w_q1"), (w_k1, "w_k1"), (w_v1, "w_v1"), (w_o1, "w_o1")):
                sp.dma_start(dst, io[name]).then_inc(s_late, 16)
            for u in range(2):
                sp.wait_ge(s_yd[u], 16 + 16 * (GROUPS // 2))
            for e in range(2):
                sp.dma_start(y2[64 * e:64 * e + SLOTS, :, :],
                             y_dram.rearrange("s (p e) d -> e s p d", e=2)[e]).then_inc(s_y2, 16)
            for dst, name in ((z_proj, "z_proj"), (out1_w, "out1_w"), (out2_w, "out2_w"),
                              (score_w, "score_w")):
                sp.dma_start(dst, io[name]).then_inc(s_late2, 16)
            sp.wait_ge(s_split_out, 16 * 5)
            w1v = w1_dram.rearrange("n (s r) c -> n r s c", r=SR)
            for k, part in enumerate((0, 0, 0, 1, 1, 2)):
                sp.dma_start(w1s[SR * k:SR * (k + 1), :, :], w1v[part]).then_inc(s_w1s, 16)
            b1v = b1_dram.rearrange("n (o s a) c -> n o s (a c)", o=1, s=SEG)
            for part in range(PARTS):
                sp.dma_start(w1s[6 * SR + part:6 * SR + part + 1, :, :], b1v[part]).then_inc(s_w1s, 16)

        def moe_pe(pe):
            with pe.Fori(0, GROUPS // 2) as it:
                for u in range(2):
                    pe.wait_ge(s_fc1[u], nth(it, 16, 16))
                    pe.wait_ge(s_yr, nth(it, 2, u + 1))
                    for n in range(2):
                        for kc in range(2):
                            for j in range(GS):
                                mm = pe.matmul(P[32 * j:32 * j + B, 2 * u + n, 0:HID // 2], y_ring[:, kc, u, B * j:B * (j + 1)],
                                               fc1[:, u, kc, j, n * (HID // 2):(n + 1) * (HID // 2)],
                                               start=(kc == 0), stop=(kc == 1), skip_group_check=True)
                    mm.then_inc(s_hid, 1)
                    pe.wait_ge(s_act, nth(it, 2, u + 1))
                    for c in range(HC):
                        mm = pe.transpose(P[:, 4 + c // 3, (c % 3) * 128:(c % 3 + 1) * 128],
                                          hidden[:, u, c // 3, (c % 3) * 128:(c % 3 + 1) * 128], ident[:, :])
                    mm.then_inc(s_hp, 1)
                    pe.wait_ge(s_ht, nth(it, 2, u + 1))
                    pe.wait_ge(s_fc2[u], nth(it, 32, 32))
                    pe.matmul(P[:, 6 + u, 0:D], slot_sel[:, :], fc2_b[:, u, :],
                              start=True, stop=False, skip_group_check=True)
                    for c in range(HC):
                        for j in range(GS):
                            mm = pe.matmul(P[32 * j:32 * j + B, 6 + u, 0:D], hidden_t[:, u, c, B * j:B * (j + 1)],
                                           fc2[:, u, c, j, :], start=False, stop=(c == HC - 1), skip_group_check=True)
                    mm.then_inc(s_fo, 1)

        def moe_act(act):
            act.wait_ge(s_yt, 2 + 2 * QUADS)
            with act.Fori(0, GROUPS // 2) as it:
                for u in range(2):
                    act.copy(y_ring[:, :, u, :],
                             y_t[:, :, ds(it * 2 * GS + u * GS, GS), :].rearrange("p k s b -> p k (s b)")).then_inc(s_yr, 1)
                    act.wait_ge(s_hid, nth(it, 2, u + 1))
                    act.activation(hidden[:, u, :, :], P[:, 2 * u:2 * u + 2, 0:HID // 2], ACT.Gelu).then_inc(s_act, 1)

        def moe_dve(dve):
            with dve.Fori(0, GROUPS // 2) as it:
                for u in range(2):
                    dve.wait_ge(s_hp, nth(it, 2, u + 1))
                    dve.tensor_copy(hidden_t[:, u, :, :].rearrange("p (a c) s -> p a (c s)", a=2),
                                    P[:, 4:6, 0:3 * 128]).then_inc(s_ht, 1)
                    dve.wait_ge(s_fo, nth(it, 2, u + 1))
                    dve.wait_ge(s_yd[u], nth(it, 16, 16))
                    dve.tensor_copy(y_out[:, u, :], P[:, 6 + u, 0:D]).then_inc(s_yo, 1)

        def split_pool(pool):
            def parts(rows, cols, out, base):
                src, left = split_in[0:rows, 0:cols], split_left[0:rows, 0:cols]
                pool.tensor_copy(out[:, 0, :], src).then_inc(s_split, 1)
                pool.wait_ge(s_split, base + 1)
                pool.tensor_tensor(left, src, out[:, 0, :], ALU.subtract).then_inc(s_split, 1)
                pool.wait_ge(s_split, base + 2)
                pool.tensor_copy(out[:, 1, :], left).then_inc(s_split, 1)
                pool.wait_ge(s_split, base + 3)
                pool.tensor_tensor(out[:, 2, :], left, out[:, 1, :], ALU.subtract).then_inc(s_split, 1)
                pool.wait_ge(s_split, base + 4)

            pool.wait_ge(s_yt, 2 + 2 * QUADS)
            for n in range(4):
                pool.dma_start(split_in[:, :], io["w1"][:, n * 512:(n + 1) * 512]).then_inc(s_split_in, 16)
                pool.wait_ge(s_split_in, 16 * (n + 1))
                parts(128, 512, split_out[:, :, :], 4 * n)
                pool.dma_start(w1_dram.rearrange("n p c -> p n c")[:, :, n * 512:(n + 1) * 512],
                               split_out[:, :, :]).then_inc(s_split_out, 16)
                pool.wait_ge(s_split_out, 16 * (n + 1))
            pool.dma_start(split_in[:, 0:128], io["b1"]).then_inc(s_split_in, 16)
            pool.wait_ge(s_split_in, 16 * 5)
            parts(128, 128, split_out[:, :, 0:128], 16)
            pool.dma_start(b1_dram.rearrange("n p c -> p n c"), split_out[:, :, 0:128]).then_inc(s_split_out, 16)
            pool.wait_ge(s_split_out, 16 * 5)
            pool.dma_start(split_in[:, :], io["b2"]).then_inc(s_split_in, 16)
            pool.wait_ge(s_split_in, 16 * 6)
            parts(128, 512, b2s[:, :, :, :].rearrange("p n s r -> p n (s r)"), 20)
            for n in range(2):
                pool.dma_start(split_in[0:PARTS * 32, :], io["gate_sel"][:, n]).then_inc(s_split_in, 16)
                pool.wait_ge(s_split_in, 16 * (7 + n))
                pool.tensor_copy(gate_sel[:, 4 * n:4 * n + 4, :].rearrange("p c m -> p (c m)"),
                                 split_in[0:PARTS * 32, :]).then_inc(s_split, 1)
                pool.wait_ge(s_split, 25 + n)

        def l1_pe(pe):
            pe.wait_ge(s_late, 64)
            pe.wait_ge(s_y2, 32)
            with pe.Fori(0, QUADS) as it:
                pe.wait_ge(s_cr, nth(it, 1, 1))
                for j in range(QP):
                    mm = pe.matmul(P[0:ROWS, 6 + j // 2, (j % 2) * D:(j % 2 + 1) * D], comb_r[:, j, :],
                                   y2[:, ds(it * QP + j, 1), :].rearrange("p a d -> p (a d)"),
                                   start=True, stop=True, skip_group_check=True)
                    if j % 2:
                        mm.then_inc(s_mix, 1)
                pe.wait_ge(LO["h_t"], nth(it, QP, QP))
                pe_turn(pe, L1, it, h_in, L0["h_out"], QP, QUADS)
                pe_qk(pe, L1, it, 2, w_q1, w_k1)
                pe_v(pe, L1, it, w_v1)
                pe_attention(pe, L1, it, 2, k_heads1)
                pe_turn_rows(pe, it, attn, L1["mapped"], s_at)
                for j in range(QP):
                    pe.wait_ge(s_att, nth(it, 2, j // 2 + 1))
                    for kc in range(2):
                        mm = pe.matmul(P[0:ROWS, 6 + j // 2, (j % 2) * D:(j % 2 + 1) * D], tok_t[:, j, kc, :], w_o1[:, kc, :],
                                       start=(kc == 0), stop=(kc == 1), skip_group_check=True)
                    if j % 2:
                        mm.then_inc(s_wo, 1)
                for j in range(QP):
                    pe.wait_ge(LO["h_out"], nth(it, QP, j + 1))
                    for kc in range(2):
                        at = ((j % 2) * 2 + kc) * 128
                        mm = pe.transpose(P[0:FH, 4 + j // 2, at:at + ROWS], h_out[0:ROWS, j, kc * FH:(kc + 1) * FH],
                                          ident[0:ROWS, 0:ROWS])
                    if j % 2:
                        mm.then_inc(LO["h_turned"], 1)

        def l1_dve(dve):
            dve.wait_ge(s_lam, 1)
            with dve.Fori(0, QUADS) as it:
                for g in range(2):
                    dve.wait_ge(s_mix, nth(it, 2, g + 1))
                    dve.tensor_tensor(attn[0:ROWS, 2 * g:2 * g + 2, :], P[0:ROWS, 6 + g, 0:2 * D].rearrange("p (j d) -> p j d", j=2),
                                      h1_all[0:ROWS, ds(it * QP + 2 * g, 2), :], ALU.add).then_inc(L0["resid"], 2)
                dve_ln(dve, L0, it + QUADS, attn, h_in)
                take_turned(dve, dve.tensor_copy, L1, it, 1, h_t)
                dve_k(dve, L1, it, 2, None, k_heads1)
                dve_v(dve, L1, it, False)
                dve_attention(dve, L1, it, 2)
                dve.tensor_tensor(h_out[0:ROWS, :, :], h_in[0:ROWS, :, :], spread(rowc[0:ROWS, 4, :], 1, QP),
                                  ALU.add).then_inc(s_hb, 1)
                dve.wait_ge(s_hb, nth(it, 1, 1))
                for g in range(2):
                    dve.wait_ge(s_wo, nth(it, 2, g + 1))
                    dve.tensor_tensor(attn[0:ROWS, 2 * g:2 * g + 2, :], P[0:ROWS, 6 + g, 0:2 * D].rearrange("p (j d) -> p j d", j=2),
                                      h_out[0:ROWS, 2 * g:2 * g + 2, :], ALU.add).then_inc(LO["resid"], 2)
                dve_ln(dve, LO, it, attn, h_out)
                take_x3(dve, dve.tensor_copy, it, 1)

        def take_x3(eng, copy, it, g):
            eng.wait_ge(LO["h_turned"], nth(it, 2, g + 1))
            src = P[0:FH, 4 + g, :].rearrange("p (j k e r) -> p j k e r", j=2, k=2, e=2)
            for j in range(2):
                copy(x3_t[:, :, ds(it * QB + 4 * g + 2 * j, 2), :], src[:, j, :, :, 0:T]).then_inc(LO["h_t"], 1)

        def l1_act(act):
            act.activation(lam[:, :], lam[:, :], ACT.Exp).then_inc(s_lam, 1)
            with act.Fori(0, QUADS) as it:
                take_turned(act, act.copy, L1, it, 0, h_t)
                act_q(act, L1, it, 2, None, k_heads1)
                act_attention(act, L1, it, 2)
                take_rows(act, it, s_at, s_att)
                take_x3(act, act.copy, it, 0)

        def l1_pool(pool):
            pool.wait_ge(s_ct, QUADS)
            with pool.Fori(0, QUADS) as it:
                pool.tensor_copy(comb_r[:, :, :], combine_all[:, ds(it * QP, QP), :]).then_inc(s_cr, 1)
                pool_rstd(pool, L0, it + QUADS)
                pool_rstd(pool, LO, it)
                pool.wait_ge(LO["h_out"], nth(it, QP, QP))
                pool.tensor_tensor(h3_all[0:ROWS, ds(it * QP, QP), :], h_out[0:ROWS, :, :],
                                   spread(rowc[0:ROWS, 5, :], 1, QP), ALU.add).then_inc(s_h3, 1)

        def prep_pe(pe):
            pe.wait_ge(s_small, SMALL)
            pe.wait_ge(s_psum0, 1)
            pe.matmul(P[0:FH, 0, 0:FH], m_u[:, :], m_v[:, :], start=True, stop=True).then_inc(s_prep_pe, 1)
            for kc in range(2):
                pe.matmul(P[0:FH, 1, kc * D:(kc + 1) * D], v_k_t[:, kc * FH:(kc + 1) * FH], u_k[:, :], start=True, stop=True)
                mm = pe.matmul(P[0:FH, 2, kc * D:(kc + 1) * D], v_v_t[:, kc * FH:(kc + 1) * FH], u_v[:, :], start=True, stop=True)
            mm.then_inc(s_prep_pe, 1)
            pe.wait_ge(s_prep_dve, 1)
            for hc in range(2):
                pe.matmul(P[0:R0, 3, hc * FH:(hc + 1) * FH], u_q_t[:, hc, :], mixer[:, :], start=True, stop=True)
            pe.matmul(P[0:FH, 0, 256:258], mixer[:, :], bias_qk[:, 0, :], start=True, stop=True).then_inc(s_prep_pe, 1)
            pe.wait_ge(s_prep_dve, 2)
            for kc in range(2):
                mm = pe.matmul(P[0:FH, 4, kc * D:(kc + 1) * D], v_q_t[:, kc * FH:(kc + 1) * FH], u_qm[:, :], start=True, stop=True)
            mm.then_inc(s_prep_pe, 1)
            pe.wait_ge(s_slot_dir, 1)
            for kc in range(2):
                mm = pe.transpose(P[0:FH, 5, kc * SLOTS:(kc + 1) * SLOTS], slot_dir[:, kc * FH:(kc + 1) * FH],
                                  ident[0:SLOTS, 0:SLOTS])
            mm.then_inc(s_prep_pe, 1)

        def prep_dve(dve):
            dve.memset(P[:, :, :], 0.0).then_inc(s_psum0, 1)
            dve.memset(negh[:, :], -0.5).then_inc(s_consts, 1)
            dve.memset(v_blk[:, :, :, :], 0.0).then_inc(s_vz, 1)
            dve.memset(cw[:, :, :], 0.0).then_inc(s_consts, 1)
            dve.memset(probs[:, :, :, :, :], 0.0).then_inc(s_consts, 1)
            dve.memset(y_t[FH:FH + 1, :, :, :], 1.0).then_inc(s_consts, 1)
            dve.wait_ge(s_vz, 1)
            dve.memset(v_blk[0:T, :, :, HD:HD + 1], 1.0).then_inc(s_consts, 1)
            dve.memset(v_blk[64:64 + T, :, :, 2 * HD + 1:2 * HD + 2], 1.0).then_inc(s_consts, 1)
            dve.wait_ge(s_small, SMALL)
            dve.tensor_tensor(embed_add[:, :], rowc[:, 0, :], rowc[:, 1, :], ALU.add).then_inc(s_prep_misc, 1)
            dve.tensor_tensor(bias_km[:, :, :], spread(bias_qk[:, 1, :], 2, HH), spread(hmask[:, :], 1, 2),
                              ALU.mult).then_inc(s_prep_misc, 1)
            dve.wait_ge(s_prep_pe, 1)
            dve.tensor_tensor(mixer[:, :], P[0:FH, 0, 0:FH], bmask[:, :], ALU.mult).then_inc(s_prep_dve, 1)
            dve.tensor_tensor_reduce(slot_dir[:, :], slots[:, :], slots[:, :], 1.0, 0.0, ALU.mult, ALU.add,
                                     slot_n[:, 0:1]).then_inc(s_slot_sum, 1)
            dve.wait_ge(s_prep_pe, 3)
            dve.tensor_copy(bias_qm[:, :], P[0:FH, 0, 256:258]).then_inc(s_prep_misc, 1)
            dve.tensor_copy(u_qm[:, :], P[0:R0, 3, 0:D]).then_inc(s_prep_dve, 1)
            dve.tensor_copy(w_k0[:, :, :], P[0:FH, 1, 0:2 * D].rearrange("p (k d) -> p k d", k=2)).then_inc(s_prep_misc, 1)
            dve.tensor_copy(w_v0[:, :, :], P[0:FH, 2, 0:2 * D].rearrange("p (k d) -> p k d", k=2)).then_inc(s_prep_misc, 1)
            dve.wait_ge(s_prep_pe, 4)
            dve.tensor_copy(w_q0[:, :, :], P[0:FH, 4, 0:2 * D].rearrange("p (k d) -> p k d", k=2)).then_inc(s_prep_misc, 1)
            dve.wait_ge(s_prep_pool, 2)
            dve.tensor_tensor(slot_n[:, 3:4], slot_n[:, 2:3], slot_scale[:, :], ALU.mult).then_inc(s_slot_sum, 1)
            dve.wait_ge(s_slot_sum, 2)
            dve.tensor_scalar(slot_dir[:, :], slots[:, :], slot_n[:, 3:4], None, ALU.mult).then_inc(s_slot_dir, 1)
            dve.wait_ge(s_prep_pe, 5)
            dve.tensor_copy(slots_t[:, :, :], P[0:FH, 5, 0:2 * SLOTS].rearrange("p (k s) -> p k s", k=2)).then_inc(s_prep_misc, 1)

        PREP_MISC = 7

        def prep_pool(pool):
            pool.wait_ge(s_slot_sum, 1)
            pool.wait_ge(s_consts, 6)
            pool.tensor_scalar(slot_n[:, 1:2], slot_n[:, 0:1], TINY, None, ALU.max).then_inc(s_prep_pool, 1)
            pool.wait_ge(s_prep_pool, 1)
            pool.tensor_tensor(slot_n[:, 2:3], slot_n[:, 1:2], negh[0:SLOTS, 0:1], ALU.pow).then_inc(s_prep_pool, 1)

        def l0_pe(pe):
            pe.wait_ge(s_prep_misc, PREP_MISC)
            pe.wait_ge(s_consts, 6)
            with pe.Fori(0, QUADS) as it:
                pe.wait_ge(s_patches, nth(it, 16, 16))
                for j in range(QP):
                    for e in range(2):
                        for c in range(PC):
                            mm = pe.matmul(P[64 * e:64 * e + T, 6 + j // 2, (j % 2) * D:(j % 2 + 1) * D],
                                           patches[:, c, 2 * j + e, :], w_patch[:, c, :],
                                           start=(c == 0), stop=(c == PC - 1), skip_group_check=True)
                    mm.then_inc(s_emb, 1)
                pe.wait_ge(s_yt, nth(it, 2, 2))
                pe_turn(pe, L0, it, h_in, s_hin, QP)
                pe_qk(pe, L0, it, 1, w_q0, w_k0)
                pe_v(pe, L0, it, w_v0)
                pe_attention(pe, L0, it, 1, k_heads0)
                pe_turn_rows(pe, it, tok, s_tok, s_tokp)
                for j in range(QP):
                    pe.wait_ge(s_tokt, nth(it, 2, j // 2 + 1))
                    for kc in range(2):
                        mm = pe.matmul(P[0:ROWS, 6, j * SLOTS:(j + 1) * SLOTS], tok_t[:, j, kc, :], slots_t[:, kc, :],
                                       start=(kc == 0), stop=(kc == 1), skip_group_check=True)
                mm.then_inc(s_lg, 1)
                for j in range(QP):
                    for e in range(2):
                        for kc in range(2):
                            mm = pe.matmul(P[64 * e:64 * e + SLOTS, 7, j * T:(j + 1) * T], slots_t[:, kc, :],
                                           tok_t[:, j, kc, 64 * e:64 * e + T],
                                           start=(kc == 0), stop=(kc == 1), skip_group_check=True)
                mm.then_inc(s_lt, 1)
                settle(pe, s_cd, nth(it, 11, 11))
                for j in range(QP):
                    for e in range(2):
                        r = slice(64 * e, 64 * e + SLOTS)
                        mm = pe.matmul(P[64 * e:64 * e + T, 1, j * SLOTS:(j + 1) * SLOTS], dw[r, j, :], ident[r, r],
                                       start=True, stop=True, skip_group_check=True)
                mm.then_inc(s_dp, 1)
                for j in range(QP):
                    mm = pe.transpose(P[:, 0, j * ROWS:(j + 1) * ROWS], cw[0:ROWS, j, :], ident[0:ROWS, 0:ROWS])
                mm.then_inc(s_cp, 1)
                pe.wait_ge(s_dt, nth(it, 1, 1))
                for kc in range(2):
                    for e, j in [(e, j) for e in range(2) for j in range(QP)]:
                        mm = pe.matmul(P[0:FH, 4 + kc - 2 * e, j * SLOTS:(j + 1) * SLOTS],
                                       xn[64 * e:64 * e + T, j, kc * FH:(kc + 1) * FH], disp[64 * e:64 * e + T, j, :],
                                       start=True, stop=True, skip_group_check=True)
                    mm.then_inc(s_y, 1)

        def take_y(copy, it, kc):
            dst = y_t[0:FH, kc, :, ds(it * QB, QB)].rearrange("p s (j e) -> p e j s", e=2)
            for e in range(2):
                ins = copy(dst[:, e], P[0:FH, 4 + kc - 2 * e, 0:QP * SLOTS].rearrange("p (j s) -> p j s", j=QP))
            ins.then_inc(s_yt, 1)

        def l0_dve(dve):
            dve.wait_ge(s_prep_misc, PREP_MISC)
            with dve.Fori(0, QUADS) as it:
                for g in range(2):
                    dve.wait_ge(s_emb, nth(it, QP, 2 * g + 2))
                    dve.tensor_tensor(h_in[0:ROWS, 2 * g:2 * g + 2, :],
                                      P[0:ROWS, 6 + g, 0:2 * D].rearrange("p (j d) -> p j d", j=2),
                                      spread(embed_add[0:ROWS, :], 1, 2), ALU.add).then_inc(s_hin, 2)
                take_turned(dve, dve.tensor_copy, L0, it, 1, h_t)
                dve_k(dve, L0, it, 1, bias_km, k_heads0)
                dve_v(dve, L0, it, True)
                dve_attention(dve, L0, it, 1)
                for j in range(QP):
                    dve.wait_ge(L0["normed"], nth(it, QP, j + 1))
                    dve.tensor_tensor(attn[0:ROWS, j, :], attn[0:ROWS, j, :], h_in[0:ROWS, j, :],
                                      ALU.add).then_inc(L0["resid"], 1)
                dve_ln(dve, L0, it, attn, h_out)
                for j in range(QP):
                    dve.wait_ge(L0["h_out"], nth(it, QP, j + 1))
                    dve.tensor_tensor_reduce(sq[0:ROWS, j, :], h_out[0:ROWS, j, :], h_out[0:ROWS, j, :], 1.0, 0.0,
                                             ALU.mult, ALU.add, norms[0:ROWS, 0, j:j + 1]).then_inc(s_ssq, 1)
                dve.wait_ge(s_rr, nth(it, 1, 1))
                for j in range(QP):
                    dve.scalar_tensor_tensor(xn[0:ROWS, j, :], h_out[0:ROWS, j, :], norms[0:ROWS, 2, j:j + 1],
                                             rowc[0:ROWS, 2, :], ALU.mult, ALU.mult).then_inc(s_xn, 1)
                for j in range(QP):
                    dve.wait_ge(s_xn, nth(it, QP, j + 1))
                    dve.tensor_tensor_reduce(sq[0:ROWS, j, :], xn[0:ROWS, j, :], xn[0:ROWS, j, :], 1.0, 0.0,
                                             ALU.mult, ALU.add, norms[0:ROWS, 3, j:j + 1]).then_inc(s_n2, 1)
                dve.wait_ge(s_tn, nth(it, 1, 1))
                for j in range(QP):
                    dve.tensor_scalar(tok[0:ROWS, j, :], xn[0:ROWS, j, :], small[0:ROWS, 1, j:j + 1], None,
                                      ALU.mult).then_inc(s_tok, 1)
                lg = P[0:ROWS, 6, 0:QP * SLOTS].rearrange("p (j s) -> p j s", j=QP)
                lt = P[:, 7, 0:QP * T].rearrange("p (j t) -> p j t", j=QP)
                dve.wait_ge(s_lg, nth(it, 1, 1))
                dve.tensor_reduce(rmx[0:ROWS, 0, :], lg, AX, ALU.max).then_inc(s_cd, 1)
                dve.wait_ge(s_lt, nth(it, 1, 1))
                dve.tensor_reduce(rmx[:, 3, :], lt, AX, ALU.max).then_inc(s_cd, 1)
                dve.wait_ge(s_cd, nth(it, 11, 1))
                dve.tensor_tensor(cw2[0:ROWS, :, :], lg, spread(rmx[0:ROWS, 0, :], 2, SLOTS), ALU.subtract).then_inc(s_cd, 1)
                dve.wait_ge(s_cd, nth(it, 11, 2))
                dve.tensor_tensor(dw2[:, :, :], lt, spread(rmx[:, 3, :], 2, T), ALU.subtract).then_inc(s_cd, 1)
                dve.wait_ge(s_ce, nth(it, 2, 1))
                dve.tensor_reduce(rmx[0:ROWS, 1, :], ce[0:ROWS, :, :], AX, ALU.add).then_inc(s_cd, 1)
                dve.wait_ge(s_ce, nth(it, 2, 2))
                dve.tensor_reduce(rmx[:, 4, :], de[:, :, :], AX, ALU.add).then_inc(s_cd, 1)
                dve.wait_ge(s_cd, nth(it, 11, 5))
                dve.reciprocal(rmx[0:ROWS, 2, :], rmx[0:ROWS, 1, :]).then_inc(s_cd, 1)
                dve.wait_ge(s_cd, nth(it, 11, 6))
                dve.reciprocal(rmx[:, 5, :], rmx[:, 4, :]).then_inc(s_cd, 1)
                dve.wait_ge(s_cd, nth(it, 11, 7))
                for e in range(2):
                    r = slice(64 * e, 64 * e + T)
                    dve.tensor_tensor(cw[r, :, e * SLOTS:(e + 1) * SLOTS], ce[r, :, :], spread(rmx[r, 2, :], 2, SLOTS),
                                      ALU.mult).then_inc(s_cd, 1)
                dve.wait_ge(s_cd, nth(it, 11, 8))
                dve.tensor_tensor(dw[:, :, :], de[:, :, :], spread(rmx[:, 5, :], 2, T), ALU.mult).then_inc(s_cd, 1)
                dve.wait_ge(s_dp, nth(it, 1, 1))
                dve.tensor_copy(disp[0:ROWS, :, :], P[0:ROWS, 1, 0:QP * SLOTS].rearrange("p (j s) -> p j s", j=QP)).then_inc(s_dt, 1)
                dve.wait_ge(s_y, nth(it, 2, 1))
                take_y(dve.tensor_copy, it, 0)

        def l0_act(act):
            act.wait_ge(s_prep_misc, PREP_MISC)
            act.wait_ge(s_consts, 6)
            with act.Fori(0, QUADS) as it:
                take_turned(act, act.copy, L0, it, 0, h_t)
                act_q(act, L0, it, 1, bias_qm, k_heads0)
                act_attention(act, L0, it, 1)
                take_rows(act, it, s_tokp, s_tokt)
                act.wait_ge(s_cd, nth(it, 11, 3))
                act.activation(ce[0:ROWS, :, :], cw2[0:ROWS, :, :], ACT.Exp).then_inc(s_ce, 1)
                act.wait_ge(s_cd, nth(it, 11, 4))
                act.activation(de[:, :, :], dw2[:, :, :], ACT.Exp).then_inc(s_ce, 1)
                act.wait_ge(s_cp, nth(it, 1, 1))
                act.copy(combine_all[:, ds(it * QP, QP), :],
                         P[:, 0, 0:QP * ROWS].rearrange("p (j t) -> p j t", j=QP)).then_inc(s_ct, 1)
                act.wait_ge(s_y, nth(it, 2, 2))
                take_y(act.copy, it, 1)

        def l0_pool(pool):
            with pool.Fori(0, QUADS) as it:
                pool_rstd(pool, L0, it)
                settle(pool, s_ssq, nth(it, QP, QP))
                pool.tensor_scalar(norms[0:ROWS, 1, :], norms[0:ROWS, 0, :], 1.0 / D, EPS, ALU.mult, ALU.add).then_inc(s_ms, 1)
                pool.wait_ge(s_ms, nth(it, 2, 1))
                pool.tensor_tensor(norms[0:ROWS, 2, :], norms[0:ROWS, 1, :], negh[0:ROWS, :], ALU.pow).then_inc(s_rr, 1)
                settle(pool, s_n2, nth(it, QP, QP))
                pool.tensor_scalar(small[0:ROWS, 0, :], norms[0:ROWS, 3, :], TINY, None, ALU.max).then_inc(s_ms, 1)
                pool.wait_ge(s_ms, nth(it, 2, 2))
                pool.tensor_tensor(small[0:ROWS, 1, :], small[0:ROWS, 0, :], negh[0:ROWS, :], ALU.pow).then_inc(s_tn, 1)
                pool.wait_ge(L0["h_out"], nth(it, QP, QP))
                pool.tensor_copy(h1_all[0:ROWS, ds(it * QP, QP), :], h_out[0:ROWS, :, :]).then_inc(s_keep, 1)

        def l0_sync(sp):
            sp.sem_inc(s_yt, 2)
            sp.sem_inc(LO["h_t"], QP)
            sp.sem_inc(s_ot, 1)
            sp.sem_inc(s_o2, 2)
            sp.sem_inc(s_ac, 2)
            sp.sem_inc(s_out, 32)
            for u in range(2):
                sp.sem_inc(s_yd[u], 16)
            for dst, name in SMALL_LOADS:
                sp.dma_start(dst[:], io[name]).then_inc(s_small, 16)
            sp.dma_start(patches[:, :, :, :], io["patches"][0]).then_inc(s_patches, 16)
            moe_sync_first(sp)
            with sp.Fori(1, QUADS) as it:
                sp.wait_ge(s_emb, it * QP)
                sp.dma_start(patches[:, :, :, :], io["patches"][it]).then_inc(s_patches, 16)

        CHUNKS = [(n * TC, min(TC, TOK - n * TC)) for n in range(3)]
        SPLIT = 4
        UNITS = [(sq, hh, c, j) for sq in range(2) for hh in range(2) for c in range(CH // 2) for j in range(4)]
        NU = len(UNITS)
        LAG = 3
        PRODUCTS = [(0, 0), (0, 1), (1, 0), (0, 2), (1, 1), (2, 0)]

        def mlp_sync(sp):
            sp.wait_ge(LO["h_t"], QP + QP * QUADS)
            sp.wait_ge(s_h3, QUADS)
            sp.dma_start(w2[:, :, :, :], io["w2"]).then_inc(s_w2, 16)
            sp.wait_ge(s_zp, SPLIT)
            sp.dma_start(z_dram.rearrange("n p t -> p n t"), z_parts[:, :, :]).then_inc(s_zd, 16)
            sp.wait_ge(s_zd, 16)
            zv = z_dram.rearrange("n (s r) t -> n r s t", r=SR)
            for k, part in enumerate((0, 1, 2, 0, 1, 0)):
                sp.dma_start(zs[SR * k:SR * (k + 1), :, :], zv[part]).then_inc(s_zs, 16)
            sp.wait_ge(s_g1, TT)
            sp.wait_ge(s_g2, TT)
            for part in range(PARTS):
                for q in range(4):
                    sp.dma_start(ws[32 * part:32 * (part + 1), :, :].rearrange("p (s q) t -> p q s t", q=4)[:, q],
                                 gate_parts[32 * q:32 * (q + 1), part, :, 0:TP]).then_inc(s_ws, 16)

        def mlp_pe(pe):
            pe.wait_ge(LO["h_t"], QP + QP * QUADS)
            pe.wait_ge(s_late2, 16 * 4)
            for n, (at, cols) in enumerate(CHUNKS):
                for kc in range(2):
                    mm = pe.matmul(P[:, n, 0:cols], z_proj[:, kc, :],
                                   x3_t[:, kc, :, :].rearrange("p b t -> p (b t)")[:, at:at + cols],
                                   start=(kc == 0), stop=(kc == 1))
                mm.then_inc(s_z, 1)
            with pe.Fori(0, TT // 2) as it:
                for u in range(2):
                    pe.wait_ge(s_zt, nth(it, 2, u + 1))
                    pe.matmul(P[:, 4 + u, :], z_tile[:, u, :], score_w[:, :], start=True, stop=True).then_inc(s_sc, 1)
                for u in range(2):
                    pe.wait_ge(s_gate, nth(it, 2, u + 1))
                    for sg in range(4):
                        mm = pe.transpose(P[:, 6 + u, sg * 128:(sg + 1) * 128], gate[:, u, sg * 128:(sg + 1) * 128],
                                          ident[:, :])
                    mm.then_inc(s_gt, 1)
            pe.wait_ge(s_zs, 16 * 6)
            pe.wait_ge(s_w1s, 16 * 9)
            pe.wait_ge(s_set, 1)
            pe.wait_ge(s_split, 26)
            pe.wait_ge(s_ws, 16 * 12)
            pe.wait_ge(s_w2, 16)
            with pe.Fori(0, 3) as it:
                def hidden_and_gate(n):
                    sq, hh, c, j = UNITS[n]
                    seg, i = 4 * sq + j, hh * (CH // 2) + c
                    if n == 0:
                        pe.wait_ge(s_ot, nth(it, 1, 1))
                    if n >= 4:
                        pe.wait_ge(s_ua, nth(it, NU, n - 3))
                    pe.matmul(P[:, n % 4, 0:TC], w1s[:, seg, i * 128:(i + 1) * 128], zs[:, seg, ds(it * TC, TC)],
                              start=True, stop=True).then_inc(s_u1, 1)
                    if n >= 2:
                        pe.wait_ge(s_ug, nth(it, NU, n - 1))
                    pe.matmul(P[:, 4 + n % 2, 0:TC], gate_sel[:, c, :], ws[:, 2 * seg + hh, ds(it * TC, TC)],
                              start=True, stop=True).then_inc(s_bc, 1)

                def last_bias(sq):
                    pe.wait_ge(s_ac, nth(it, 2, sq + 1))
                    for sg in (2 * sq, 2 * sq + 1):
                        for k, (g, b) in enumerate(PRODUCTS):
                            pe.matmul(P[:, 6 + sq, 0:TC], b2s[:, b, sg, :], gate_parts[:, g, sg, ds(it * TC, TC)],
                                      start=(sg == 2 * sq and k == 0), stop=False, skip_group_check=True)

                def expert_out(n):
                    sq, hh, c, j = UNITS[n]
                    seg, i = 4 * sq + j, hh * (CH // 2) + c
                    pe.wait_ge(s_ug, nth(it, NU, n + 1))
                    pe.matmul(P[32 * j:32 * j + 32, 6 + sq, 0:TC], w2[:, i, seg, :], gated[:, n % 4, :],
                              start=False, stop=(hh == 1 and c == CH // 2 - 1), skip_group_check=True).then_inc(s_u2, 1)

                for n in range(NU + LAG):
                    if n < NU:
                        hidden_and_gate(n)
                    if n in (0, NU // 2):
                        last_bias(n // (NU // 2))
                    if n >= LAG:
                        expert_out(n - LAG)
                pe.wait_ge(s_ac, nth(it, 2, 4))
                for sq in range(2):
                    mm = pe.matmul(P[0:SG, 0, 0:TC], out1_w[:, sq, :], mlp_out[:, sq, :], start=(sq == 0), stop=(sq == 1))
                mm.then_inc(s_o1, 1)

        def mlp_act(act):
            act.wait_ge(LO["h_out"], QP * QUADS)
            for n, (at, cols) in enumerate(CHUNKS):
                act.wait_ge(s_z, n + 1)
                act.copy(z[:, at:at + cols], P[:, n, 0:cols]).then_inc(s_zc, 1)
            act.wait_ge(s_zc, 3)
            act.wait_ge(s_set, 1)
            with act.Fori(0, TT // 2) as it:
                for u in range(2):
                    act.copy(z_tile[:, u, :], z[:, ds(it * 256 + u * 128, 128)]).then_inc(s_zt, 1)
                for u in range(2):
                    act.wait_ge(s_sc, nth(it, 2, u + 1))
                    act.copy(scored[:, u, 0, :, 0:SM], P[:, 4 + u, :].rearrange("p (s m) -> p s m", m=SM)).then_inc(s_sr, 1)
                for u in range(2):
                    act.wait_ge(s_t4, nth(it, 4, 2 * u + 2))
                    act.activation(top_e[:, u, :, :], top_e[:, u, :, :], ACT.Exp).then_inc(s_ge, 1)
                    act.wait_ge(s_sh, nth(it, 2, u + 1))
                    act.activation(gate_e[:, u, :], gate_e[:, u, :], ACT.Exp).then_inc(s_ge, 1)
                for u in range(2):
                    act.wait_ge(s_gt, nth(it, 2, u + 1))
                    act.copy(gate_parts[:, 0, :, ds(it * 256 + u * 128, 128)],
                             P[:, 6 + u, :].rearrange("p (s t) -> p s t", s=4)).then_inc(s_g0, 1)
                for u in range(2):
                    act.wait_ge(s_gl, nth(it, 2, u + 1))
                    act.copy(gate_parts[:, 1, :, ds(it * 256 + u * 128, 128)],
                             gate_left[:, u, :].rearrange("p (s t) -> p s t", s=4)).then_inc(s_g1, 1)
            with act.Fori(0, 3) as it:
                for n in range(NU):
                    act.wait_ge(s_u1, nth(it, NU, n + 1))
                    if n >= 4:
                        act.wait_ge(s_ug, nth(it, NU, n - 3))
                    act.activation(act_out[:, n % 4, :], P[:, n % 4, 0:TC], ACT.Gelu_apprx_tanh).then_inc(s_ua, 1)
                    if n == NU // 2 + LAG + 3:
                        act.wait_ge(s_u2, nth(it, NU, NU // 2))
                        act.copy(mlp_out[:, 0, :], P[:, 6, 0:TC]).then_inc(s_ac, 1)
                act.wait_ge(s_u2, nth(it, NU, NU))
                act.copy(mlp_out[:, 1, :], P[:, 7, 0:TC]).then_inc(s_ac, 1)
                act.wait_ge(s_o1, nth(it, 1, 1))
                act.activation(out_t[:, ds(it * TC, TC)], P[0:SG, 0, 0:TC], ACT.Gelu_apprx_tanh,
                               bias=out1_b[:, 0:1]).then_inc(s_ot, 1)

        def mlp_dve(dve):
            dve.wait_ge(LO["h_out"], QP * QUADS)
            dve.memset(z[:, TOK:TZ], 0.0).then_inc(s_zb, 1)
            dve.wait_ge(LO["h_t"], QP + QP * QUADS)
            dve.wait_ge(s_h3, QUADS)
            for u in range(2):
                dve.memset(scored[:, u, 0, :, SM:SM + SK], LOW).then_inc(s_zb, 1)
                dve.memset(top4[:, u, :, SK:2 * SK], LOW).then_inc(s_zb, 1)
            dve.memset(zs[6 * SR:ZR, :, :], 1.0).then_inc(s_set, 1)
            dve.wait_ge(s_zb, 1)
            dve.wait_ge(s_zc, 3)
            dve.tensor_copy(z_parts[:, 0, :], z[:, 0:TP]).then_inc(s_zp, 1)
            dve.wait_ge(s_zp, 1)
            dve.tensor_tensor(z_left[:, :], z[:, 0:TP], z_parts[:, 0, :], ALU.subtract).then_inc(s_zp, 1)
            dve.wait_ge(s_zp, 2)
            dve.tensor_copy(z_parts[:, 1, :], z_left[:, :]).then_inc(s_zp, 1)
            dve.wait_ge(s_zp, 3)
            dve.tensor_tensor(z_parts[:, 2, :], z_left[:, :], z_parts[:, 1, :], ALU.subtract).then_inc(s_zp, 1)
            dve.wait_ge(s_zb, 5)
            with dve.Fori(0, TT // 2) as it:
                for u in range(2):
                    settle(dve, s_sr, nth(it, 2, u + 1))
                    for s in range(SEG):
                        mx = dve.max(top8[:, u, s, :], scored[:, u, 0, s, 0:SM])
                    mx.then_inc(s_mx, 1)
                    dve.wait_ge(s_mx, nth(it, 2, u + 1))
                    dve.tensor_copy(top4[:, u, :, 0:SK], top8[:, u, :, 0:SK]).then_inc(s_t4, 1)
                    dve.tensor_tensor(top_e[:, u, :, :], top8[:, u, :, 0:SK], top8[:, u, :, 0:1].to_broadcast([128, SEG, SK]),
                                      ALU.subtract).then_inc(s_t4, 1)
                    settle(dve, s_t4, nth(it, 4, 2 * u + 1))
                    for s in range(SEG):
                        rp = dve.match_replace(scored[:, u, 1, s, :], top4[:, u, s, :], scored[:, u, 0, s, :], LOW)
                    rp.then_inc(s_rp, 1)
                for u in range(2):
                    dve.wait_ge(s_ge, nth(it, 4, 2 * u + 1))
                    dve.tensor_reduce(gate_sum[:, u, 0, :], top_e[:, u, :, :], AX, ALU.add).then_inc(s_gs, 1)
                    dve.wait_ge(s_gs, nth(it, 6, 3 * u + 1))
                    dve.reciprocal(gate_sum[:, u, 1, :], gate_sum[:, u, 0, :]).then_inc(s_gs, 1)
                    dve.wait_ge(s_ge, nth(it, 4, 2 * u + 2))
                    dve.wait_ge(s_rp, nth(it, 2, u + 1))
                    g = gate[:, u, :].rearrange("p (s m) -> p s m", m=SM)
                    dve.scalar_tensor_tensor(g, scored[:, u, 1, :, 0:SM], LOW,
                                             gate_e[:, u, :].rearrange("p (s m) -> p s m", m=SM),
                                             ALU.is_equal, ALU.mult).then_inc(s_gs, 1)
                    dve.wait_ge(s_gs, nth(it, 6, 3 * u + 3))
                    dve.tensor_tensor(g, g, spread(gate_sum[:, u, 1, :], 2, SM), ALU.mult).then_inc(s_gate, 1)
                for u in range(2):
                    dve.wait_ge(s_g0, nth(it, 2, u + 1))
                    dve.tensor_tensor(gate_left[:, u, :].rearrange("p (s t) -> p s t", s=4),
                                      P[:, 6 + u, :].rearrange("p (s t) -> p s t", s=4),
                                      gate_parts[:, 0, :, ds(it * 256 + u * 128, 128)], ALU.subtract).then_inc(s_gl, 1)
            with dve.Fori(0, 3) as it:
                for n in range(NU):
                    dve.wait_ge(s_ua, nth(it, NU, n + 1))
                    dve.wait_ge(s_bc, nth(it, NU, n + 1))
                    if n >= 4:
                        dve.wait_ge(s_u2, nth(it, NU, n - 3))
                    dve.tensor_tensor(gated[:, n % 4, :], act_out[:, n % 4, :], P[:, 4 + n % 2, 0:TC],
                                      ALU.mult).then_inc(s_ug, 1)

        def mlp_pool(pool):
            with pool.Fori(0, TT // 2) as it:
                for u in range(2):
                    pool.wait_ge(s_mx, nth(it, 2, u + 1))
                    pool.tensor_tensor(gate_e[:, u, :].rearrange("p (s m) -> p s m", m=SM), scored[:, u, 0, :, 0:SM],
                                       top8[:, u, :, 0:1].to_broadcast([128, SEG, SM]), ALU.subtract).then_inc(s_sh, 1)
                for u in range(2):
                    pool.wait_ge(s_g1, nth(it, 2, u + 1))
                    at = ds(it * 256 + u * 128, 128)
                    pool.tensor_tensor(gate_parts[:, 2, :, at], gate_left[:, u, :].rearrange("p (s t) -> p s t", s=4),
                                       gate_parts[:, 1, :, at], ALU.subtract).then_inc(s_g2, 1)

        def last_pe(pe):
            with pe.Fori(0, QUADS) as it:
                settle(pe, LO["resid"], nth(it, QP, QP * QUADS))
                settle(pe, s_or, nth(it, 1, 1))
                for j in range(QP):
                    for e in range(2):
                        mm = pe.matmul(P[64 * e:64 * e + T, 2 + j // 2, (j % 2) * D:(j % 2 + 1) * D], out_r[:, 2 * j + e, :],
                                       out2_w[:, :], start=True, stop=True, skip_group_check=True)
                    if j % 2:
                        mm.then_inc(s_o2, 1)

        def last_act(act):
            act.wait_ge(s_ot, 4)
            with act.Fori(0, QUADS) as it:
                act.wait_ge(s_o2, nth(it, 2, 2))
                act.copy(out_r[:, :, :].rearrange("p b t -> p (b t)"), out_t[:, ds(it * QT, QT)]).then_inc(s_or, 1)

        def last_dve(dve):
            with dve.Fori(0, QUADS) as it:
                dve.wait_ge(LO["h_out"], nth(it, QP, QP * QUADS))
                for g in range(2):
                    dve.wait_ge(s_o2, nth(it, 2, 2 + g + 1))
                    dve.tensor_tensor(attn[0:ROWS, 2 * g:2 * g + 2, :], P[0:ROWS, 2 + g, 0:2 * D].rearrange("p (j d) -> p j d", j=2),
                                      h3_all[0:ROWS, ds(it * QP + 2 * g, 2), :], ALU.add).then_inc(LO["resid"], 2)
                dve.wait_ge(s_out, nth(it, 32, 32))
                dve_ln(dve, LO, it + QUADS, attn, h_out)

        def last_pool(pool):
            with pool.Fori(0, QUADS) as it:
                pool_rstd(pool, LO, it + QUADS)

        def last_sync(sp):
            out = io["out"].rearrange("(q j e) t d -> q e t j d", j=QP, e=2)
            with sp.Fori(0, QUADS) as it:
                sp.wait_ge(LO["h_out"], nth(it, QP, QP * QUADS + QP))
                for e in range(2):
                    sp.dma_start(out[it, e], h_out[64 * e:64 * e + T, :, :]).then_inc(s_out, 16)
            sp.wait_ge(s_out, 32 + 32 * QUADS)


        block = ctx.enter_context(nc.Block())
        @block.sync
        def _(sp):
            l0_sync(sp)
            moe_sync(sp)
            mlp_sync(sp)
            last_sync(sp)

        @block.tensor
        def _(pe):
            prep_pe(pe)
            l0_pe(pe)
            moe_pe(pe)
            l1_pe(pe)
            mlp_pe(pe)
            last_pe(pe)

        @block.vector
        def _(dve):
            prep_dve(dve)
            l0_dve(dve)
            moe_dve(dve)
            l1_dve(dve)
            mlp_dve(dve)
            last_dve(dve)

        @block.scalar
        def _(act):
            l0_act(act)
            moe_act(act)
            l1_act(act)
            mlp_act(act)
            last_act(act)

        @block.gpsimd
        def _(pool):
            prep_pool(pool)
            l0_pool(pool)
            split_pool(pool)
            l1_pool(pool)
            mlp_pool(pool)
            last_pool(pool)


def layout(x, np, **w):
    f = np.float32
    W = {k: np.asarray(v) for k, v in w.items()}
    x = np.asarray(x)
    d = {}
    d["ident"] = np.eye(128, dtype=f)
    d["hmask"] = np.repeat(np.eye(HH, dtype=f), HD, axis=0)
    d["bmask"] = np.repeat(d["hmask"], HD, axis=1)
    p = x.reshape(B, 6, 16, 6, 16, 3).transpose(0, 1, 3, 2, 4, 5).reshape(B, NPATCH, PC, 128)
    pz = np.zeros((B, T, PC, 128), f)
    pz[:, 1:] = p
    d["patches"] = np.ascontiguousarray(pz.reshape(QUADS, QB, T, PC, 128).transpose(0, 4, 3, 1, 2))
    d["w_patch"] = np.ascontiguousarray(W["L0_tok_W_proj"].reshape(PC, 128, D).transpose(1, 0, 2))
    rc = np.zeros((128, 6, D), f)
    for r in (0, 64):
        rc[r:r + T, 0] = W["L0_tok_pos_embedding"]
        rc[r, 1] = W["L0_tok_cls_token"].reshape(D)
        rc[r + 1:r + T, 1] = W["L0_tok_b_proj"]
    rc[:, 2] = W["L0_ffn_norm_weight"]
    eo = lambda a: a.reshape(-1, HH, 2, HD).transpose(0, 2, 1, 3).reshape(-1, 2, FH)
    bv = eo(W["L0_attn_bias_v"][None])[0]
    rc[0:64, 3, 0:FH] = bv[0]
    rc[64:, 3, 0:FH] = bv[1]
    rc[:, 4] = W["L1_attn_bo"]
    rc[:, 5] = W["L1_ffn_g2b"]
    d["rowc"] = rc
    d["lam"] = np.repeat(W["L1_attn_lambda_p"].reshape(1, NH), 128, axis=0)
    halves = lambda a: np.ascontiguousarray(a.reshape(2, FH, -1).transpose(1, 0, 2))
    d["v_q_t"] = np.ascontiguousarray(W["L0_attn_V_Q"].T)
    d["v_k_t"] = np.ascontiguousarray(W["L0_attn_V_K"].T)
    d["v_v_t"] = np.ascontiguousarray(W["L0_attn_V_V"].T)
    d["u_q_t"] = halves(np.ascontiguousarray(W["L0_attn_U_Q"].T))
    d["u_k"] = W["L0_attn_U_K"]
    d["u_v"] = np.ascontiguousarray(eo(W["L0_attn_U_V"]).reshape(R0, D))
    d["m_u"] = np.ascontiguousarray(np.tile(W["L0_attn_M_U"].T, (1, HH)))
    d["m_v"] = np.ascontiguousarray(np.tile(W["L0_attn_M_V"], (1, HH)))
    d["bias_qk"] = np.ascontiguousarray(np.stack([W["L0_attn_bias_q"].reshape(2, FH), W["L0_attn_bias_k"].reshape(2, FH)]).transpose(2, 0, 1))
    d["slots"] = W["L0_ffn_slots"]
    d["slot_scale"] = W["L0_ffn_scale"].reshape(SLOTS, 1)
    d["w_q1"] = halves(W["L1_attn_Wq"])
    d["w_k1"] = halves(W["L1_attn_Wk"])
    d["w_v1"] = halves(eo(W["L1_attn_Wv"]).reshape(D, D))
    d["w_o1"] = halves(W["L1_attn_Wo"])
    w = W["L0_ffn_fc1_weight"].reshape(GROUPS, GS, 2, FH, HID)
    fc1 = np.zeros((GROUPS, FH + 1, 2, GS, HID), f)
    fc1[:, :FH] = w.transpose(0, 3, 2, 1, 4)
    fc1[:, FH, 0] = W["L0_ffn_fc1_bias"].reshape(GROUPS, GS, HID)
    d["fc1"] = fc1
    w = W["L0_ffn_fc2_weight"].reshape(GROUPS, GS, HC, 128, D)
    d["fc2"] = np.ascontiguousarray(w.transpose(0, 3, 2, 1, 4))
    d["fc2_b"] = W["L0_ffn_fc2_bias"].reshape(GROUPS, GS, D)
    d["slot_sel"] = np.repeat(np.eye(GS, dtype=f), 32, axis=1)
    d["w1"] = np.ascontiguousarray(W["L1_ffn_W1"].transpose(0, 2, 1, 3).reshape(SEG * SR, SM * SH))
    d["b1"] = W["L1_ffn_b1"].reshape(128, 128)
    b2 = np.zeros((4, 2, SM, 4, 32), f)
    for s in range(SEG):
        b2[s // 2, s % 2, :, s % 4, :SR] = W["L1_ffn_b2"][s]
    d["b2"] = np.ascontiguousarray(b2.reshape(4, 128, 128).transpose(1, 0, 2)).reshape(128, 512)
    w = np.zeros((4, SH, CH, SEG, 32), f)
    w[..., :SR] = W["L1_ffn_W2"].reshape(SEG, CH, 4, SH, SR).transpose(2, 3, 1, 0, 4)
    d["w2"] = w.reshape(128, CH, SEG, 32)
    d["z_proj"] = halves(np.ascontiguousarray(W["L1_ffn_P"].transpose(1, 0, 2).reshape(D, SEG * SR)))
    sc = np.zeros((SEG, SR, SEG, SM), f)
    for s in range(SEG):
        sc[s, :, s] = W["L1_ffn_C"][s].T
    d["score_w"] = sc.reshape(128, SEG * SM)
    sel = np.zeros((PARTS, 32, SM // 8, 4, SH), f)
    for m in range(32):
        sel[:, m, m // 4, m % 4] = 1
    d["gate_sel"] = sel.reshape(PARTS * 32, 2, 512)
    g1 = np.zeros((4, 32, 2, SG), f)
    g1[:, :SR] = W["L1_ffn_G1"].reshape(2, 4, SR, SG).transpose(1, 2, 0, 3)
    d["out1_w"] = g1.reshape(128, 2, SG)
    d["out1_b"] = W["L1_ffn_g1b"].reshape(SG, 1)
    d["out2_w"] = W["L1_ffn_G2"]
    return d


def kernel(**inputs):
    import numpy as _np
    import concourse.bacc as _bacc
    from concourse import mybir as _mybir
    from concourse.bass_utils import run_bass_kernel_spmd as _run

    nc = _bacc.Bacc("TRN2", target_bir_lowering=False, num_devices=1)
    arrays, io = {}, {}
    for name, a in layout(np=_np, **inputs).items():
        a = _np.ascontiguousarray(a)
        arrays[f"in_{name}_dram"] = a
        io[name] = nc.dram_tensor(f"in_{name}_dram", a.shape, _mybir.dt.from_np(a.dtype), kind="ExternalInput").ap()
    io["out"] = nc.dram_tensor("out_0_dram", (B, T, D), _mybir.dt.float32, kind="ExternalOutput").ap()
    tower(nc, io)
    r = _run(nc, [arrays], core_ids=[0])
    return r.results[0]["out_0_dram"]
```

```python
from contextlib import ExitStack

import concourse.bass as bass
from concourse import mybir

B, T, D = 32, 37, 192
NPATCH = T - 1
PD = 768
PC = PD // 128
NH, HD = 12, 16
HH = NH // 2
FH = D // 2
R0 = 96
RM = 64
SLOTS = 64
HID = 768
HC = HID // 128
PAIRS = B // 2
QP = 4
QB = 2 * QP
QUADS = PAIRS // QP
QT = QB * T
ROWS = 64 + T
GS = 4
GROUPS = SLOTS // GS
TOK = B * T
SEG, SR, SM, SH, SK, SG = 8, 16, 64, 32, 4, 64
CH = SM * SH // 128
TC = 396
TP = 3 * TC
TT = 10
TZ = TT * 128
PARTS = 3
ZR = 6 * SR + PARTS
EPS = 1e-5
TINY = 1e-10
LOW = -3.0e38
WORK = 12310


def tower(nc, io):
    f32 = mybir.dt.float32
    bf16 = mybir.dt.bfloat16
    ALU = mybir.AluOpType
    ACT = mybir.ActivationFunctionType
    AX = mybir.AxisListType.X
    ds = bass.ds

    def spread(ap, axis, n):
        ap = ap.unsqueeze(axis)
        shape = list(ap.shape)
        shape[axis] = n
        return ap.to_broadcast(shape)

    def nth(step, per, n):
        return step * per + n

    def settle(eng, s, value):
        eng.wait_ge(s, value)
        eng.sem_inc(s_settled, 1)

    with ExitStack() as ctx:
        def sb(name, shape, dt=f32):
            return ctx.enter_context(nc.sbuf_tensor(name, shape, dt))

        def sem(name):
            return ctx.enter_context(nc.semaphore(name))

        def dram(name, shape, dt):
            return nc.dram_tensor(name, shape, dt, kind="Internal").ap()

        EXPERT, KH, ZW = 2 * GS * HID, 2 * QB * HH * T, SEG * TP // 2
        early = sb("early", [128, PC * QB * T + PC * D + KH + 2 * SLOTS * B])
        stream = sb("stream", [128, 2 * EXPERT + 2 * HC * GS * D])

        def tenant(home, rows, at, shape, dt=f32):
            n = 1
            for x in shape:
                n *= x
            words = n // (2 if dt == bf16 else 1)
            ap = home[0:rows, at:at + words]
            if dt != f32:
                ap = ap.bitcast(dt)
            names = "abcde"[:len(shape)]
            kw = {c: x for c, x in zip(names, shape)}
            return ap.rearrange(f"p ({' '.join(names)}) -> p {' '.join(names)}", **kw)

        class Tenants:
            def __init__(self, home, at=0):
                self.home, self.at = home, at

            def __call__(self, shape, dt=f32):
                ap = tenant(self.home, shape[0], self.at, shape[1:], dt)
                n = 1
                for x in shape[1:]:
                    n *= x
                self.at += n // (2 if dt == bf16 else 1)
                assert self.at <= self.home.shape[1], (self.at, self.home.shape)
                return ap

        patches = tenant(early, 128, 0, [PC, QB, T])
        w_patch = tenant(early, 128, PC * QB * T, [PC, D])
        k_heads0 = tenant(early, FH, PC * QB * T + PC * D, [1, 2, QB, HH, T])
        y_t = tenant(early, FH + 1, PC * QB * T + PC * D + KH, [2, SLOTS, B])
        fc1 = tenant(stream, FH + 1, 0, [2, 2, GS, HID])
        fc2 = tenant(stream, 128, 2 * EXPERT, [2, HC, GS, D])
        k_heads1 = tenant(stream, FH, 0, [2, 2, QB, HH, T])
        w1s = tenant(stream, ZR, 2 * EXPERT + 2 * HC * GS * D - SEG * SM * SH // 2, [SEG, SM * SH], bf16)
        late = Tenants(stream, KH * 2)
        w_q1 = late([FH, 2, 2 * D]); w_k1 = late([FH, 2, 2 * D]); w_v1 = late([FH, 2, D]); w_o1 = late([FH, 2, D])
        gate_parts = tenant(stream, 128, 0, [PARTS, 4, TZ], bf16)
        zs = tenant(stream, ZR, PARTS * 4 * TZ // 2, [SEG, TP], bf16)
        ws = tenant(early, PARTS * 32, 0, [2 * SEG, TP], bf16)

        ident = sb("ident", [128, 128])
        hmask = sb("hmask", [FH, HH])
        bmask = sb("bmask", [FH, FH])
        rowc = sb("rowc", [128, 6, D])
        embed_add = sb("embed_add", [128, D])
        lam = sb("lam", [128, NH])
        negh = sb("negh", [128, QP])
        prep = Tenants(early, PC * QB * T + PC * D + KH)
        v_q_t = prep([R0, D]); u_q_t = prep([FH, 2, R0])
        v_k_t = prep([R0, D]); u_k = prep([R0, D])
        v_v_t = prep([R0, D]); u_v = prep([R0, D])
        m_u = prep([RM, FH]); m_v = prep([RM, FH])
        bias_qk = sb("bias_qk", [FH, 2, 2])
        mixer = prep([FH, FH])
        u_qm = prep([R0, D])
        middle = sb("middle", [128, PARTS * 4 * 64 + SM // 8 * 64])
        w = Tenants(middle)
        w_q0 = w([FH, 2, D]); w_k0 = w([FH, 2, D]); w_v0 = w([FH, 2, D])
        w = Tenants(middle)
        b2s = w([128, PARTS, 4, 128], bf16)
        gate_sel = w([PARTS * 32, SM // 8, 128], bf16)
        bias_qm = sb("bias_qm", [FH, 2])
        bias_km = sb("bias_km", [FH, 2, HH])
        slots = prep([SLOTS, D]); slot_scale = sb("slot_scale", [SLOTS, 1])
        slot_n = sb("slot_n", [SLOTS, 4])
        slot_dir = prep([SLOTS, D])
        slots_t = sb("slots_t", [FH, 2, SLOTS])

        slot_sel = sb("slot_sel", [GS, 128])
        out1_b = sb("out1_b", [SG, 1])

        h1_all = sb("h1_all", [128, PAIRS, D])
        h3_all = h1_all
        combine_all = sb("combine_all", [128, PAIRS, ROWS])

        work = sb("work", [128, WORK])
        w = Tenants(work)
        v_blk = w([128, QB, HH, 2 * (HD + 1)])
        probs = w([128, 2, HH, 2, 64])
        h_in = w([128, QP, D])
        attn = w([128, QP, D])
        attn2 = w([128, 2, D])
        row_max = w([128, 2, NH])
        rsum = w([128, 2, 2, NH])
        stats = w([128, QP, 6]); mv = w([128, QP, 2])
        rstd = w([128, QP]); var_e = w([128, QP])
        h_out = w([128, QP, D])
        norms = w([128, 4, QP])
        small = w([128, 6, QP])
        rmx = w([128, 6, QP])
        shared = w.at
        h_t = w([FH, 2, QB, T])
        q_t = w([FH, 2, 2, QB * T])
        sq = tenant(work, 128, w.at, [QP, D])
        shifted = w([128, 2, NH, T])
        probs_t = w([128, 2, HH, ROWS])
        tok_t = w([FH, QP, 2, ROWS])
        xn = w([128, QP, D])
        tok = attn
        r = Tenants(work, shared)
        cw2 = r([128, QP, SLOTS])
        dw = r([128, QP, T]); dw2 = r([128, QP, T])
        disp = r([128, QP, SLOTS])
        ce = r([128, QP, SLOTS]); de = r([128, QP, T])
        cw = sb("cw", [128, QP, 2 * SLOTS])
        w = Tenants(work, shared)
        y_ring = w([FH + 1, 2, 2, GS * B])
        hidden = w([128, 2, 2, HID // 2])
        hidden_t = w([128, 2, HC, 128])
        y_out = w([128, 2, D])
        moe_end = w.at
        w = Tenants(work)
        w2 = w([128, CH, SEG, 32])
        act_out = w([128, 4, TC])
        gated = tenant(work, 128, w.at, [8, TC])
        w.at += 4 * TC
        z = w([128, TZ])
        z_left = w([128, TP])
        z_parts = w([128, PARTS, TP], bf16)
        mlp_out = w([128, 2, TC])
        w = Tenants(work, CH * SEG * 32)
        scored = w([128, 2, 2, SEG, SM + SK])
        z_tile = w([128, 2, 128])
        top8 = w([128, 2, SEG, 8]); top4 = w([128, 2, SEG, 8])
        top_e = w([128, 2, SEG, SK])
        gate_sum = w([128, 2, 2, SEG])
        assert w.at <= CH * SEG * 32 + 8 * TC
        w = Tenants(early)
        y2 = w([128, PAIRS, D])
        x3_t = w([FH, 2, B, T])
        comb_r = w([128, QP, ROWS])
        w = Tenants(work, CH * SEG * 32 + 8 * TC + TZ)
        gate_e = w([128, 2, SEG * SM])
        gate = w([128, 2, SEG * SM])
        gate_left = w([128, 2, SEG * SM])

        P = ctx.enter_context(nc.psum_tensor("P", [128, 8, 512], f32))

        def bank(n):
            return P[:, n, :]

        s_small = sem("s_small_loaded")
        s_psum0 = sem("s_psum_cleared")
        s_prep_pe = sem("s_prep_products")
        s_prep_dve = sem("s_prep_taken")
        s_prep_pool = sem("s_prep_powers")
        s_patches = sem("s_patches_loaded")
        s_emb = sem("s_embedded")
        s_hin = sem("s_h_in_ready")
        s_done = sem("s_done")
        s_settled = sem("s_settled_waits")
        s_slot_dir = sem("s_slot_dir"); s_slot_sum = sem("s_slot_sum"); s_consts = sem("s_consts_set"); s_vz = sem("s_v_blk_cleared"); s_prep_misc = sem("s_prep_weights")

        NORM = "resid stats mv var rstd h_out"
        TURN = "h_turned h_t"
        ATTENTION = ("q_made k_made v_made q_ready k_ready_a k_ready_v v_ready scores row_max shifted probs "
                     "probs_turned probs_t mixed sums normed")

        def layer_sems(p, *names):
            return {n: sem(f"{p}_{n}") for n in " ".join(names).split()}

        L0 = layer_sems("l0", TURN, ATTENTION, NORM)
        s_ssq = sem("s_square_sums"); s_ms = sem("s_mean_squares"); s_rr = sem("s_rms")
        s_xn = sem("s_xn"); s_n2 = sem("s_norm_squares"); s_tn = sem("s_tok_norms"); s_tok = sem("s_tok")
        s_tokp = sem("s_tok_turned"); s_tokt = sem("s_tok_t")
        s_lg = sem("s_logits"); s_lt = sem("s_logits_t")
        s_cd = sem("s_routing_steps"); s_ce = sem("s_routing_exps")
        s_cp = sem("s_combine_turned"); s_ct = sem("s_combine_t")
        s_dp = sem("s_dispatch_turned"); s_dt = sem("s_dispatch")
        s_y = sem("s_slot_inputs"); s_yt = sem("s_slot_inputs_taken")
        s_keep = sem("s_h1_kept")


        SMALL_LOADS = [
            (ident, "ident"), (hmask, "hmask"), (bmask, "bmask"), (rowc, "rowc"), (lam, "lam"), (w_patch, "w_patch"),
            (v_q_t, "v_q_t"), (u_q_t, "u_q_t"), (v_k_t, "v_k_t"), (u_k, "u_k"), (v_v_t, "v_v_t"), (u_v, "u_v"),
            (m_u, "m_u"), (m_v, "m_v"), (bias_qk, "bias_qk"), (slots, "slots"), (slot_scale, "slot_scale"),
            (slot_sel, "slot_sel"), (out1_b, "out1_b")]
        SMALL = 16 * len(SMALL_LOADS)

        def pe_turn(pe, L, it, src, ready, per, past=0):
            for j in range(QP):
                pe.wait_ge(ready, nth(it, per, past * per + j + 1))
                for kc in range(2):
                    at = ((j % 2) * 2 + kc) * 128
                    mm = pe.transpose(P[0:FH, 4 + j // 2, at:at + ROWS],
                                      src[0:ROWS, j, kc * FH:(kc + 1) * FH], ident[0:ROWS, 0:ROWS])
                if j % 2:
                    mm.then_inc(L["h_turned"], 1)

        def take_turned(eng, copy, L, it, g, dst):
            eng.wait_ge(L["h_turned"], nth(it, 2, g + 1))
            src = P[0:FH, 4 + g, :].rearrange("p (j k e r) -> p j k e r", j=2, k=2, e=2)
            for j in range(2):
                copy(dst[:, :, 4 * g + 2 * j:4 * g + 2 * j + 2, :], src[:, j, :, :, 0:T]).then_inc(L["h_t"], 1)

        def pe_qk(pe, L, it, maps, w_q, w_k):
            pe.wait_ge(L["h_t"], nth(it, QP, QP))
            for m in range(maps):
                for w, at, made in ((w_q, 4 * m, "q_made"), (w_k, 4 * m + 2, "k_made")):
                    for mc in range(2):
                        for kc in range(2):
                            mm = pe.matmul(P[0:FH, at + mc, 0:QT], w[:, kc, m * D + mc * FH:m * D + (mc + 1) * FH],
                                           h_t[:, kc, :, :], start=(kc == 0), stop=(kc == 1))
                        mm.then_inc(L[made], 1)

        def v_bank(maps):
            return 6 if maps == 1 else 2

        def pe_v(pe, L, it, maps, w_v):
            if maps == 2:
                pe.wait_ge(L["k_ready_a"], nth(it, HH * maps, HH))
                pe.wait_ge(L["k_ready_v"], nth(it, HH * maps, HH))
            for b in range(QB):
                for e in range(2):
                    for kc in range(2):
                        mm = pe.matmul(P[64 * e:64 * e + T, v_bank(maps) + b // 4, (b % 4) * FH:(b % 4 + 1) * FH],
                                       h_t[:, kc, b, :], w_v[:, kc, e * FH:(e + 1) * FH],
                                       start=(kc == 0), stop=(kc == 1), skip_group_check=True)
                if b % 4 == 3:
                    mm.then_inc(L["v_made"], 1)

        def pe_scores(pe, L, it, maps, u, k_heads):
            j, m = u // maps, u % maps
            if u == 0:
                pe.wait_ge(L["q_ready"], nth(it, 2 * maps, 2 * maps))
                pe.wait_ge(L["k_ready_a"], nth(it, HH * maps, HH * maps))
                pe.wait_ge(L["k_ready_v"], nth(it, HH * maps, HH * maps))
            if u >= 2:
                pe.wait_ge(L["shifted"], nth(it, QP * maps, u - 1))
            for e in range(2):
                b = 2 * j + e
                for mc in range(2):
                    mm = pe.matmul(P[64 * e:64 * e + T, u % 2, mc * HH * T:(mc + 1) * HH * T],
                                   q_t[:, m, mc, b * T:(b + 1) * T], k_heads[:, m, mc, b, :, :],
                                   start=True, stop=True, skip_group_check=True)
            mm.then_inc(L["scores"], 1)

        def pe_turn_probs(pe, L, it, maps, u):
            pe.wait_ge(L["probs"], nth(it, QP * maps, u + 1))
            if u == 0:
                pe.wait_ge(L["v_ready"], nth(it, 4, 4))
            for hp in range(HH):
                mm = pe.transpose(P[:, 4 + 2 * (u % 2) + hp // 3, (hp % 3) * ROWS:(hp % 3 + 1) * ROWS],
                                  probs[0:ROWS, u % 2, hp, :, :].rearrange("p a k -> p (a k)"), ident[0:ROWS, 0:ROWS])
            mm.then_inc(L["probs_turned"], 1)

        def pe_mix(pe, L, it, maps, u):
            j = u // maps
            pe.wait_ge(L["probs_t"], nth(it, QP * maps, u + 1))
            if u >= 2:
                pe.wait_ge(L["normed"], nth(it, QP * maps, u - 1))
            for e in range(2):
                for hp in range(HH):
                    w2 = 2 * (HD + 1)
                    mm = pe.matmul(P[64 * e:64 * e + T, 2 + u % 2, hp * w2:(hp + 1) * w2],
                                   probs_t[0:ROWS, u % 2, hp, 64 * e:64 * e + T], v_blk[0:ROWS, 2 * j + e, hp, :],
                                   start=True, stop=True, skip_group_check=True)
            mm.then_inc(L["mixed"], 1)

        def pe_attention(pe, L, it, maps, k_heads, between=None, beside_mix=None):
            U = QP * maps
            for k in range(U + 2):
                if between and k in between:
                    between[k]()
                if k < U:
                    pe_scores(pe, L, it, maps, k, k_heads)
                if 1 <= k <= U:
                    pe_turn_probs(pe, L, it, maps, k - 1)
                if k >= 2:
                    pe_mix(pe, L, it, maps, k - 2)
                    if beside_mix and k - 2 < QP:
                        beside_mix(k - 2)

        def act_q(act, L, it, maps, bias, k_heads):
            for m in range(maps):
                for mc in range(2):
                    act.wait_ge(L["q_made"], nth(it, 2 * maps, 2 * m + mc + 1))
                    act.activation(q_t[:, m, mc, :], P[0:FH, 4 * m + mc, 0:QT], ACT.Identity,
                                   bias=0.0 if bias is None else bias[:, mc:mc + 1]).then_inc(L["q_ready"], 1)
                act.wait_ge(L["k_made"], nth(it, 2 * maps, 2 * m + 1))
                for h in range(HH):
                    act.activation(k_heads[:, m, 0, :, h, :], P[0:FH, 4 * m + 2, 0:QT].rearrange("p (b t) -> p b t", t=T),
                                   ACT.Identity, scale=hmask[:, h:h + 1],
                                   bias=0.0 if bias is None else bias_km[:, 0, h:h + 1]).then_inc(L["k_ready_a"], 1)

        def dve_k(dve, L, it, maps, bias, k_heads):
            for m in range(maps):
                dve.wait_ge(L["k_made"], nth(it, 2 * maps, 2 * m + 2))
                for h in range(HH):
                    src = P[0:FH, 4 * m + 3, 0:QT].rearrange("p (b t) -> p b t", t=T)
                    if bias is None:
                        ins = dve.tensor_scalar(k_heads[:, m, 1, :, h, :], src, hmask[:, h:h + 1], None, ALU.mult)
                    else:
                        ins = dve.tensor_scalar(k_heads[:, m, 1, :, h, :], src, hmask[:, h:h + 1],
                                                bias_km[:, 1, h:h + 1], ALU.mult, ALU.add)
                    ins.then_inc(L["k_ready_v"], 1)

        def dve_v(dve, L, it, maps, bias):
            for half in range(2):
                dve.wait_ge(L["v_made"], nth(it, 2, half + 1))
                for e in range(2):
                    rows = slice(64 * e, 64 * e + T)
                    src = P[rows, v_bank(maps) + half, 0:4 * FH].rearrange("p (b h d) -> p b h d", b=4, d=HD)
                    dst = v_blk[rows, 4 * half:4 * half + 4, :, e * (HD + 1):e * (HD + 1) + HD]
                    if bias:
                        add = spread(rowc[rows, 3, 0:FH].rearrange("p (h d) -> p h d", d=HD), 1, 4)
                        ins = dve.tensor_tensor(dst, src, add, ALU.add)
                    else:
                        ins = dve.tensor_copy(dst, src)
                    ins.then_inc(L["v_ready"], 1)

        def dve_softmax(dve, L, it, maps, u):
            src = P[0:ROWS, u % 2, 0:NH * T].rearrange("p (h k) -> p h k", k=T)
            dve.wait_ge(L["scores"], nth(it, QP * maps, u + 1))
            dve.tensor_reduce(row_max[0:ROWS, u % 2, :], src, AX, ALU.max).then_inc(L["row_max"], 1)
            dve.wait_ge(L["row_max"], nth(it, QP * maps, u + 1))
            if u >= 2:
                dve.wait_ge(L["probs"], nth(it, QP * maps, u - 1))
            dve.tensor_tensor(shifted[0:ROWS, u % 2, :, :], src, spread(row_max[0:ROWS, u % 2, :], 2, T),
                              ALU.subtract).then_inc(L["shifted"], 1)

        def act_exp(act, L, it, maps, u):
            act.wait_ge(L["shifted"], nth(it, QP * maps, u + 1))
            act.activation(probs[0:ROWS, u % 2, :, :, 0:T].rearrange("p a b k -> p (a b) k"), shifted[0:ROWS, u % 2, :, :],
                           ACT.Exp, scale=HD ** -0.5).then_inc(L["probs"], 1)

        def act_probs_t(act, L, it, maps, u):
            act.wait_ge(L["probs_turned"], nth(it, QP * maps, u + 1))
            if u >= 2:
                act.wait_ge(L["mixed"], nth(it, QP * maps, u - 1))
            act.activation(probs_t[:, u % 2, :, :].rearrange("p (g h) t -> p g (h t)", g=2),
                           P[:, 4 + 2 * (u % 2):6 + 2 * (u % 2), 0:3 * ROWS], ACT.Copy).then_inc(L["probs_t"], 1)

        def act_attention(act, L, it, maps, after_first=None):
            U = QP * maps
            for k in range(U + 1):
                if k < U:
                    act_exp(act, L, it, maps, k)
                if k == 0 and after_first:
                    after_first()
                if k >= 1:
                    act_probs_t(act, L, it, maps, k - 1)

        def dve_norm(dve, L, it, maps, u):
            j, m = u // maps, u % maps
            U = QP * maps
            o = P[0:ROWS, 2 + u % 2, 0:NH * (HD + 1)].rearrange("p (h c) -> p h c", c=HD + 1)
            r = rsum[0:ROWS, u % 2]
            dve.wait_ge(L["mixed"], nth(it, U, u + 1))
            step = nth(it, QP * (2 if maps == 1 else 5), j * (2 if maps == 1 else 5) + 2 * m)
            dve.tensor_scalar(r[:, 0, :], o[:, :, HD], 0.5, None, ALU.max).then_inc(L["sums"], 1)
            dve.wait_ge(L["sums"], step + 1)
            dve.reciprocal(r[:, 1, :], r[:, 0, :]).then_inc(L["sums"], 1)
            dve.wait_ge(L["sums"], step + 2)
            if m:
                dve.tensor_tensor(r[:, 0, :], r[:, 1, :], lam[0:ROWS, :], ALU.mult).then_inc(L["sums"], 1)
                dve.wait_ge(L["sums"], step + 3)
            out = attn[0:ROWS, j, :] if m == 0 else attn2[0:ROWS, j % 2, :]
            by = r[:, 0 if m else 1, :]
            out = out.rearrange("p (h d) -> p h d", d=HD)
            dve.tensor_tensor(out, o[:, :, 0:HD], spread(by, 2, HD), ALU.mult).then_inc(L["normed"], 1)
            if m:
                dve.wait_ge(L["normed"], nth(it, U, u + 1))
                dve.tensor_tensor(attn[0:ROWS, j, :], attn[0:ROWS, j, :], attn2[0:ROWS, j % 2, :],
                                  ALU.subtract).then_inc(L["mapped"], 1)

        def dve_attention(dve, L, it, maps, between=None):
            U = QP * maps
            for k in range(U + 2):
                if k < U:
                    dve_softmax(dve, L, it, maps, k)
                if between and k in between:
                    between[k]()
                if k >= 2:
                    dve_norm(dve, L, it, maps, k - 2)

        def pe_turn_rows(pe, it, src, ready, turned):
            for j in range(QP):
                pe.wait_ge(ready, nth(it, QP, j + 1))
                for kc in range(2):
                    at = ((j % 2) * 2 + kc) * ROWS
                    mm = pe.transpose(P[0:FH, 4 + j // 2, at:at + ROWS], src[0:ROWS, j, kc * FH:(kc + 1) * FH],
                                      ident[0:ROWS, 0:ROWS])
                if j % 2:
                    mm.then_inc(turned, 1)

        def take_rows(act, it, turned, taken):
            for g in range(2):
                act.wait_ge(turned, nth(it, 2, g + 1))
                act.copy(tok_t[:, 2 * g:2 * g + 2, :, :].rearrange("p j k t -> p (j k t)"),
                         P[0:FH, 4 + g, 0:4 * ROWS]).then_inc(taken, 1)

        def dve_ln(dve, L, it, src, dst):
            ln_moments(dve, L, it, src)
            ln_scale(dve, L, it, src, dst)

        def ln_moments(dve, L, it, src):
            for j in range(QP):
                dve.wait_ge(L["resid"], nth(it, QP, j + 1))
                dve.bn_stats(stats[0:ROWS, j, :], src[0:ROWS, j, :]).then_inc(L["stats"], 1)
            for j in range(QP):
                settle(dve, L["stats"], nth(it, QP, j + 1))
                dve.bn_aggr(mv[0:ROWS, j, :], stats[0:ROWS, j, :]).then_inc(L["mv"], 1)

        def ln_scale(dve, L, it, src, dst):
            dve.wait_ge(L["rstd"], nth(it, 1, 1))
            for j in range(QP):
                dve.tensor_scalar(dst[0:ROWS, j, :], src[0:ROWS, j, :], mv[0:ROWS, j, 0:1], rstd[0:ROWS, j:j + 1],
                                  ALU.subtract, ALU.mult).then_inc(L["h_out"], 1)

        def pool_rstd(pool, L, it):
            settle(pool, L["mv"], nth(it, QP, QP))
            pool.tensor_scalar(var_e[0:ROWS, :], mv[0:ROWS, :, 1], EPS, None, ALU.add).then_inc(L["var"], 1)
            pool.wait_ge(L["var"], nth(it, 1, 1))
            pool.tensor_tensor(rstd[0:ROWS, :], var_e[0:ROWS, :], negh[0:ROWS, :], ALU.pow).then_inc(L["rstd"], 1)
        fc2_b = sb("fc2_b", [GS, 2, D])
        w = Tenants(stream, PARTS * 4 * TZ // 2 + ZW)
        z_proj = w([FH, 2, 128]); out1_w = w([128, 2, SG]); out2_w = w([SG, D])
        w = Tenants(early, SEG * TP)
        score_w = w([128, SEG * SM])
        w = Tenants(work, moe_end)
        split_in = w([128, 512]); split_left = w([128, 512])
        split_out = w([128, PARTS, 512], bf16)
        out_t = tenant(combine_all[:, :, :].rearrange("p a b -> p (a b)"), SG, 0, [TP])
        out_r = tenant(work, SG, CH * SEG * 32 + 8 * TC, [QB, T])
        y_dram = dram("y_dram", [SLOTS, B, D], f32)
        w1_dram = dram("w1_dram", [PARTS, 128, SM * SH], bf16)
        b1_dram = dram("b1_dram", [PARTS, 128, 128], bf16)
        z_dram = dram("z_dram", [PARTS, 128, TP], bf16)
        s_late2 = sem("s_mlp_weights_loaded")
        s_fc1 = [sem("s_fc1_even"), sem("s_fc1_odd")]
        s_fc2 = [sem("s_fc2_even"), sem("s_fc2_odd")]
        s_yr = sem("s_slot_inputs_staged"); s_hid = sem("s_hidden_made"); s_act = sem("s_hidden_active")
        s_hp = sem("s_hidden_turned"); s_ht = sem("s_hidden_t"); s_fo = sem("s_slots_out_made")
        s_yo = sem("s_slots_out_taken"); s_yd = [sem("s_slots_out_stored_even"), sem("s_slots_out_stored_odd")]
        s_split_in = sem("s_split_loaded"); s_split = sem("s_split_steps"); s_split_out = sem("s_split_stored")
        s_b2 = sem("s_b2_loaded")
        s_late = sem("s_late_weights_loaded"); s_y2 = sem("s_slot_outputs_loaded")
        s_lam = sem("s_lambda"); s_cr = sem("s_combine_staged"); s_mix = sem("s_combined")
        L1 = layer_sems("l1", TURN, ATTENTION, "mapped")
        LO = layer_sems("lo", NORM, TURN)
        s_at = sem("s_attn_turned"); s_att = sem("s_attn_t"); s_wo = sem("s_attn_projected")
        s_hb = sem("s_h_in_and_bias"); s_h3 = sem("s_h3_kept"); s_x3p = sem("s_x3_turned")
        s_w1s = sem("s_w1_stacked"); s_w2 = sem("s_w2_loaded")
        s_z = sem("s_z_made"); s_zc = sem("s_z_taken"); s_zp = sem("s_z_split_steps"); s_zd = sem("s_z_parts_stored")
        s_zs = sem("s_z_parts_stacked"); s_set = sem("s_mlp_ones_set"); s_zb = sem("s_mlp_padding_set")
        s_zt = sem("s_z_tile"); s_sc = sem("s_scores_made"); s_sr = sem("s_scores_taken"); s_mx = sem("s_top8"); s_t4 = sem("s_top4")
        s_rp = sem("s_top_marked"); s_gs = sem("s_gate_steps"); s_gate = sem("s_gates")
        s_sh = sem("s_scores_shifted"); s_ge = sem("s_gate_exps"); s_gt = sem("s_gates_turned")
        s_g0 = sem("s_gate_first_part"); s_g1 = sem("s_gate_second_part"); s_g2 = sem("s_gate_third_part")
        s_gl = sem("s_gate_rest"); s_ws = sem("s_gate_parts_stacked")
        s_u1 = sem("s_unit_hidden"); s_bc = sem("s_unit_gate_spread"); s_ua = sem("s_unit_active")
        s_ug = sem("s_unit_gated"); s_u2 = sem("s_unit_summed")
        s_ac = sem("s_segments_taken"); s_o1 = sem("s_out1_made"); s_ot = sem("s_out1_active")
        s_or = sem("s_out1_staged"); s_o2 = sem("s_out2_made"); s_out = sem("s_out_stored")

        def moe_sync_first(sp):
            for g in range(2):
                sp.dma_start(fc1[:, g], io["fc1"][g]).then_inc(s_fc1[g], 16)
                sp.dma_start(fc2[:, g], io["fc2"][g]).then_inc(s_fc2[g], 16)
                sp.dma_start(fc2_b[:, g, :], io["fc2_b"][g]).then_inc(s_fc2[g], 16)

        def moe_sync(sp):
            def store(g, u):
                sp.dma_start(y_dram.rearrange("s b d -> (s b) d")[ds(g * 128, 128), :], y_out[:, u, :]).then_inc(s_yd[u], 16)

            with sp.Fori(1, GROUPS // 2) as it:
                for u in range(2):
                    sp.wait_ge(s_hid, it * 2 + (u - 1))
                    sp.dma_start(fc1[:, u], io["fc1"][it * 2 + u]).then_inc(s_fc1[u], 16)
                    sp.wait_ge(s_fo, it * 2 + (u - 1))
                    sp.dma_start(fc2[:, u], io["fc2"][it * 2 + u]).then_inc(s_fc2[u], 16)
                    sp.dma_start(fc2_b[:, u, :], io["fc2_b"][it * 2 + u]).then_inc(s_fc2[u], 16)
                    sp.wait_ge(s_yo, it * 2 + (u - 1))
                    store(it * 2 + (u - 2), u)
            for g in (GROUPS - 2, GROUPS - 1):
                sp.wait_ge(s_yo, g + 1)
                store(g, g % 2)
            for dst, name in ((w_q1, "w_q1"), (w_k1, "w_k1"), (w_v1, "w_v1"), (w_o1, "w_o1")):
                sp.dma_start(dst, io[name]).then_inc(s_late, 16)
            for u in range(2):
                sp.wait_ge(s_yd[u], 16 + 16 * (GROUPS // 2))
            for e in range(2):
                sp.dma_start(y2[64 * e:64 * e + SLOTS, :, :],
                             y_dram.rearrange("s (p e) d -> e s p d", e=2)[e]).then_inc(s_y2, 16)
            for dst, name in ((z_proj, "z_proj"), (out1_w, "out1_w"), (out2_w, "out2_w"),
                              (score_w, "score_w")):
                sp.dma_start(dst, io[name]).then_inc(s_late2, 16)
            sp.wait_ge(s_split_out, 16 * 5)
            w1v = w1_dram.rearrange("n (s r) c -> n r s c", r=SR)
            for k, part in enumerate((0, 0, 0, 1, 1, 2)):
                sp.dma_start(w1s[SR * k:SR * (k + 1), :, :], w1v[part]).then_inc(s_w1s, 16)
            b1v = b1_dram.rearrange("n (o s a) c -> n o s (a c)", o=1, s=SEG)
            for part in range(PARTS):
                sp.dma_start(w1s[6 * SR + part:6 * SR + part + 1, :, :], b1v[part]).then_inc(s_w1s, 16)

        def moe_pe(pe):
            with pe.Fori(0, GROUPS // 2) as it:
                for u in range(2):
                    pe.wait_ge(s_fc1[u], nth(it, 16, 16))
                    pe.wait_ge(s_yr, nth(it, 2, u + 1))
                    for n in range(2):
                        for kc in range(2):
                            for j in range(GS):
                                mm = pe.matmul(P[32 * j:32 * j + B, 2 * u + n, 0:HID // 2], y_ring[:, kc, u, B * j:B * (j + 1)],
                                               fc1[:, u, kc, j, n * (HID // 2):(n + 1) * (HID // 2)],
                                               start=(kc == 0), stop=(kc == 1), skip_group_check=True)
                    mm.then_inc(s_hid, 1)
                    pe.wait_ge(s_act, nth(it, 2, u + 1))
                    for c in range(HC):
                        mm = pe.transpose(P[:, 4 + c // 3, (c % 3) * 128:(c % 3 + 1) * 128],
                                          hidden[:, u, c // 3, (c % 3) * 128:(c % 3 + 1) * 128], ident[:, :])
                    mm.then_inc(s_hp, 1)
                    pe.wait_ge(s_ht, nth(it, 2, u + 1))
                    pe.wait_ge(s_fc2[u], nth(it, 32, 32))
                    pe.matmul(P[:, 6 + u, 0:D], slot_sel[:, :], fc2_b[:, u, :],
                              start=True, stop=False, skip_group_check=True)
                    for c in range(HC):
                        for j in range(GS):
                            mm = pe.matmul(P[32 * j:32 * j + B, 6 + u, 0:D], hidden_t[:, u, c, B * j:B * (j + 1)],
                                           fc2[:, u, c, j, :], start=False, stop=(c == HC - 1), skip_group_check=True)
                    mm.then_inc(s_fo, 1)

        def moe_act(act):
            act.wait_ge(s_yt, 2 + 2 * QUADS)
            with act.Fori(0, GROUPS // 2) as it:
                for u in range(2):
                    act.copy(y_ring[:, :, u, :],
                             y_t[:, :, ds(it * 2 * GS + u * GS, GS), :].rearrange("p k s b -> p k (s b)")).then_inc(s_yr, 1)
                    act.wait_ge(s_hid, nth(it, 2, u + 1))
                    act.activation(hidden[:, u, :, :], P[:, 2 * u:2 * u + 2, 0:HID // 2], ACT.Gelu).then_inc(s_act, 1)

        def moe_dve(dve):
            with dve.Fori(0, GROUPS // 2) as it:
                for u in range(2):
                    dve.wait_ge(s_hp, nth(it, 2, u + 1))
                    dve.tensor_copy(hidden_t[:, u, :, :].rearrange("p (a c) s -> p a (c s)", a=2),
                                    P[:, 4:6, 0:3 * 128]).then_inc(s_ht, 1)
                    dve.wait_ge(s_fo, nth(it, 2, u + 1))
                    dve.wait_ge(s_yd[u], nth(it, 16, 16))
                    dve.tensor_copy(y_out[:, u, :], P[:, 6 + u, 0:D]).then_inc(s_yo, 1)

        def split_pool(pool):
            def parts(rows, cols, out, base):
                src, left = split_in[0:rows, 0:cols], split_left[0:rows, 0:cols]
                pool.tensor_copy(out[:, 0, :], src).then_inc(s_split, 1)
                pool.wait_ge(s_split, base + 1)
                pool.tensor_tensor(left, src, out[:, 0, :], ALU.subtract).then_inc(s_split, 1)
                pool.wait_ge(s_split, base + 2)
                pool.tensor_copy(out[:, 1, :], left).then_inc(s_split, 1)
                pool.wait_ge(s_split, base + 3)
                pool.tensor_tensor(out[:, 2, :], left, out[:, 1, :], ALU.subtract).then_inc(s_split, 1)
                pool.wait_ge(s_split, base + 4)

            pool.wait_ge(s_yt, 2 + 2 * QUADS)
            for n in range(4):
                pool.dma_start(split_in[:, :], io["w1"][:, n * 512:(n + 1) * 512]).then_inc(s_split_in, 16)
                pool.wait_ge(s_split_in, 16 * (n + 1))
                parts(128, 512, split_out[:, :, :], 4 * n)
                pool.dma_start(w1_dram.rearrange("n p c -> p n c")[:, :, n * 512:(n + 1) * 512],
                               split_out[:, :, :]).then_inc(s_split_out, 16)
                pool.wait_ge(s_split_out, 16 * (n + 1))
            pool.dma_start(split_in[:, 0:128], io["b1"]).then_inc(s_split_in, 16)
            pool.wait_ge(s_split_in, 16 * 5)
            parts(128, 128, split_out[:, :, 0:128], 16)
            pool.dma_start(b1_dram.rearrange("n p c -> p n c"), split_out[:, :, 0:128]).then_inc(s_split_out, 16)
            pool.wait_ge(s_split_out, 16 * 5)
            pool.dma_start(split_in[:, :], io["b2"]).then_inc(s_split_in, 16)
            pool.wait_ge(s_split_in, 16 * 6)
            parts(128, 512, b2s[:, :, :, :].rearrange("p n s r -> p n (s r)"), 20)
            for n in range(2):
                pool.dma_start(split_in[0:PARTS * 32, :], io["gate_sel"][:, n]).then_inc(s_split_in, 16)
                pool.wait_ge(s_split_in, 16 * (7 + n))
                pool.tensor_copy(gate_sel[:, 4 * n:4 * n + 4, :].rearrange("p c m -> p (c m)"),
                                 split_in[0:PARTS * 32, :]).then_inc(s_split, 1)
                pool.wait_ge(s_split, 25 + n)

        MIX = NH * (HD + 1)

        def steps(eng, step):
            step(0, True, False)
            with eng.Fori(1, QUADS - 1) as it:
                step(it, False, False)
            step(QUADS - 1, False, True)

        def l1_pe(pe):
            def combine(quad, j):
                pe.wait_ge(s_cr, nth(quad, 1, 1))
                pe.matmul(P[0:ROWS, 2 + j % 2, MIX:MIX + D], comb_r[:, j, :],
                          y2[:, ds(quad * QP + j, 1), :].rearrange("p a d -> p (a d)"),
                          start=True, stop=True, skip_group_check=True).then_inc(s_mix, 1)

            def turn_x3(quad):
                for j in range(QP):
                    pe.wait_ge(LO["h_out"], nth(quad, QP, j + 1))
                    for kc in range(2):
                        at = ((j % 2) * 2 + kc) * 128
                        mm = pe.transpose(P[0:FH, 4 + j // 2, at:at + ROWS], h_out[0:ROWS, j, kc * FH:(kc + 1) * FH],
                                          ident[0:ROWS, 0:ROWS])
                    if j % 2:
                        mm.then_inc(LO["h_turned"], 1)

            def step(it, first, last):
                pe_turn(pe, L1, it, h_in, L0["h_out"], QP, QUADS)
                pe_qk(pe, L1, it, 2, w_q1, w_k1)
                pe_v(pe, L1, it, 2, w_v1)

                def x3_taken():
                    if not first:
                        turn_x3(it - 1)
                    pe.wait_ge(LO["h_t"], nth(it, QP, QP))
                pe_attention(pe, L1, it, 2, k_heads1, {1: x3_taken}, None if last else lambda j: combine(it + 1, j))
                pe_turn_rows(pe, it, attn, L1["mapped"], s_at)
                for j in range(QP):
                    pe.wait_ge(s_att, nth(it, 2, j // 2 + 1))
                    for kc in range(2):
                        mm = pe.matmul(P[0:ROWS, 6 + j // 2, (j % 2) * D:(j % 2 + 1) * D], tok_t[:, j, kc, :], w_o1[:, kc, :],
                                       start=(kc == 0), stop=(kc == 1), skip_group_check=True)
                    if j % 2:
                        mm.then_inc(s_wo, 1)

            pe.wait_ge(s_late, 64)
            pe.wait_ge(s_y2, 32)
            for j in range(QP):
                if j >= 2:
                    pe.wait_ge(L0["resid"], QP * QUADS + j - 1)
                combine(0, j)
            steps(pe, step)
            turn_x3(QUADS - 1)

        def l1_dve(dve):
            def combined(quad, j):
                dve.wait_ge(s_mix, nth(quad, QP, j + 1))
                dve.tensor_tensor(xn[0:ROWS, j:j + 1, :], P[0:ROWS, 2 + j % 2, MIX:MIX + D].unsqueeze(1),
                                  h1_all[0:ROWS, ds(quad * QP + j, 1), :], ALU.add).then_inc(L0["resid"], 1)

            def step(it, first, last):
                take_turned(dve, dve.tensor_copy, L1, it, 1, h_t)
                if not first:
                    ln_scale(dve, LO, it - 1, attn, h_out)
                dve_k(dve, L1, it, 2, None, k_heads1)
                dve_v(dve, L1, it, 2, False)

                def with_bias():
                    if not first:
                        dve.wait_ge(s_h3, it)
                    dve.tensor_tensor(h_out[0:ROWS, :, :], h_in[0:ROWS, :, :], spread(rowc[0:ROWS, 4, :], 1, QP),
                                      ALU.add).then_inc(s_hb, 1)
                between = {7: with_bias}
                if not first:
                    between[0] = lambda: take_x3(dve, dve.tensor_copy, it - 1, 1)
                if not last:
                    def scale():
                        dve.wait_ge(s_hb, nth(it, 1, 1))
                        ln_scale(dve, L0, it + (QUADS + 1), xn, h_in)
                    between.update({k + 2: lambda k=k: combined(it + 1, k) for k in range(QP)})
                    between[6] = lambda: ln_moments(dve, L0, it + (QUADS + 1), xn)
                    between[8] = scale
                dve_attention(dve, L1, it, 2, between)
                dve.wait_ge(s_hb, nth(it, 1, 1))
                for g in range(2):
                    dve.wait_ge(s_wo, nth(it, 2, g + 1))
                    dve.tensor_tensor(attn[0:ROWS, 2 * g:2 * g + 2, :], P[0:ROWS, 6 + g, 0:2 * D].rearrange("p (j d) -> p j d", j=2),
                                      h_out[0:ROWS, 2 * g:2 * g + 2, :], ALU.add).then_inc(LO["resid"], 2)
                ln_moments(dve, LO, it, attn)

            dve.wait_ge(s_lam, 1)
            for j in range(QP):
                combined(0, j)
            ln_moments(dve, L0, QUADS, xn)
            ln_scale(dve, L0, QUADS, xn, h_in)
            steps(dve, step)
            ln_scale(dve, LO, QUADS - 1, attn, h_out)
            take_x3(dve, dve.tensor_copy, QUADS - 1, 1)

        def take_x3(eng, copy, quad, g):
            eng.wait_ge(LO["h_turned"], nth(quad, 2, g + 1))
            src = P[0:FH, 4 + g, :].rearrange("p (j k e r) -> p j k e r", j=2, k=2, e=2)
            for j in range(2):
                copy(x3_t[:, :, ds(quad * QB + (4 * g + 2 * j), 2), :], src[:, j, :, :, 0:T]).then_inc(LO["h_t"], 1)

        def l1_act(act):
            def step(it, first, last):
                take_turned(act, act.copy, L1, it, 0, h_t)
                act_q(act, L1, it, 2, None, k_heads1)
                act_attention(act, L1, it, 2, None if first else lambda: take_x3(act, act.copy, it - 1, 0))
                take_rows(act, it, s_at, s_att)

            act.activation(lam[:, :], lam[:, :], ACT.Exp).then_inc(s_lam, 1)
            steps(act, step)
            take_x3(act, act.copy, QUADS - 1, 0)

        def l1_pool(pool):
            def stage(quad):
                pool.tensor_copy(comb_r[:, :, :], combine_all[:, ds(quad * QP, QP), :]).then_inc(s_cr, 1)

            def step(it, first, last):
                if not last:
                    pool.wait_ge(s_mix, nth(it, QP, QP))
                    stage(it + 1)
                    pool_rstd(pool, L0, it + (QUADS + 1))
                pool_rstd(pool, LO, it)
                pool.wait_ge(LO["h_out"], nth(it, QP, QP))
                pool.tensor_tensor(h3_all[0:ROWS, ds(it * QP, QP), :], h_out[0:ROWS, :, :],
                                   spread(rowc[0:ROWS, 5, :], 1, QP), ALU.add).then_inc(s_h3, 1)

            pool.wait_ge(s_ct, QUADS)
            stage(0)
            pool_rstd(pool, L0, QUADS)
            steps(pool, step)


        def prep_pe(pe):
            pe.wait_ge(s_small, SMALL)
            pe.wait_ge(s_psum0, 1)
            pe.matmul(P[0:FH, 0, 0:FH], m_u[:, :], m_v[:, :], start=True, stop=True).then_inc(s_prep_pe, 1)
            for kc in range(2):
                pe.matmul(P[0:FH, 1, kc * D:(kc + 1) * D], v_k_t[:, kc * FH:(kc + 1) * FH], u_k[:, :], start=True, stop=True)
                mm = pe.matmul(P[0:FH, 2, kc * D:(kc + 1) * D], v_v_t[:, kc * FH:(kc + 1) * FH], u_v[:, :], start=True, stop=True)
            mm.then_inc(s_prep_pe, 1)
            pe.wait_ge(s_prep_dve, 1)
            for hc in range(2):
                pe.matmul(P[0:R0, 3, hc * FH:(hc + 1) * FH], u_q_t[:, hc, :], mixer[:, :], start=True, stop=True)
            pe.matmul(P[0:FH, 0, 256:258], mixer[:, :], bias_qk[:, 0, :], start=True, stop=True).then_inc(s_prep_pe, 1)
            pe.wait_ge(s_prep_dve, 2)
            for kc in range(2):
                mm = pe.matmul(P[0:FH, 4, kc * D:(kc + 1) * D], v_q_t[:, kc * FH:(kc + 1) * FH], u_qm[:, :], start=True, stop=True)
            mm.then_inc(s_prep_pe, 1)
            pe.wait_ge(s_slot_dir, 1)
            for kc in range(2):
                mm = pe.transpose(P[0:FH, 5, kc * SLOTS:(kc + 1) * SLOTS], slot_dir[:, kc * FH:(kc + 1) * FH],
                                  ident[0:SLOTS, 0:SLOTS])
            mm.then_inc(s_prep_pe, 1)

        def prep_dve(dve):
            dve.memset(P[:, :, :], 0.0).then_inc(s_psum0, 1)
            dve.memset(negh[:, :], -0.5).then_inc(s_consts, 1)
            dve.memset(v_blk[:, :, :, :], 0.0).then_inc(s_vz, 1)
            dve.memset(cw[:, :, :], 0.0).then_inc(s_consts, 1)
            dve.memset(probs[:, :, :, :, :], 0.0).then_inc(s_consts, 1)
            dve.memset(y_t[FH:FH + 1, :, :, :], 1.0).then_inc(s_consts, 1)
            dve.wait_ge(s_vz, 1)
            dve.memset(v_blk[0:T, :, :, HD:HD + 1], 1.0).then_inc(s_consts, 1)
            dve.memset(v_blk[64:64 + T, :, :, 2 * HD + 1:2 * HD + 2], 1.0).then_inc(s_consts, 1)
            dve.wait_ge(s_small, SMALL)
            dve.tensor_tensor(embed_add[:, :], rowc[:, 0, :], rowc[:, 1, :], ALU.add).then_inc(s_prep_misc, 1)
            dve.tensor_tensor(bias_km[:, :, :], spread(bias_qk[:, 1, :], 2, HH), spread(hmask[:, :], 1, 2),
                              ALU.mult).then_inc(s_prep_misc, 1)
            dve.wait_ge(s_prep_pe, 1)
            dve.tensor_tensor(mixer[:, :], P[0:FH, 0, 0:FH], bmask[:, :], ALU.mult).then_inc(s_prep_dve, 1)
            dve.tensor_tensor_reduce(slot_dir[:, :], slots[:, :], slots[:, :], 1.0, 0.0, ALU.mult, ALU.add,
                                     slot_n[:, 0:1]).then_inc(s_slot_sum, 1)
            dve.wait_ge(s_prep_pe, 3)
            dve.tensor_copy(bias_qm[:, :], P[0:FH, 0, 256:258]).then_inc(s_prep_misc, 1)
            dve.tensor_copy(u_qm[:, :], P[0:R0, 3, 0:D]).then_inc(s_prep_dve, 1)
            dve.tensor_copy(w_k0[:, :, :], P[0:FH, 1, 0:2 * D].rearrange("p (k d) -> p k d", k=2)).then_inc(s_prep_misc, 1)
            dve.tensor_copy(w_v0[:, :, :], P[0:FH, 2, 0:2 * D].rearrange("p (k d) -> p k d", k=2)).then_inc(s_prep_misc, 1)
            dve.wait_ge(s_prep_pe, 4)
            dve.tensor_copy(w_q0[:, :, :], P[0:FH, 4, 0:2 * D].rearrange("p (k d) -> p k d", k=2)).then_inc(s_prep_misc, 1)
            dve.wait_ge(s_prep_pool, 2)
            dve.tensor_tensor(slot_n[:, 3:4], slot_n[:, 2:3], slot_scale[:, :], ALU.mult).then_inc(s_slot_sum, 1)
            dve.wait_ge(s_slot_sum, 2)
            dve.tensor_scalar(slot_dir[:, :], slots[:, :], slot_n[:, 3:4], None, ALU.mult).then_inc(s_slot_dir, 1)
            dve.wait_ge(s_prep_pe, 5)
            dve.tensor_copy(slots_t[:, :, :], P[0:FH, 5, 0:2 * SLOTS].rearrange("p (k s) -> p k s", k=2)).then_inc(s_prep_misc, 1)

        PREP_MISC = 7

        def prep_pool(pool):
            pool.wait_ge(s_slot_sum, 1)
            pool.wait_ge(s_consts, 6)
            pool.tensor_scalar(slot_n[:, 1:2], slot_n[:, 0:1], TINY, None, ALU.max).then_inc(s_prep_pool, 1)
            pool.wait_ge(s_prep_pool, 1)
            pool.tensor_tensor(slot_n[:, 2:3], slot_n[:, 1:2], negh[0:SLOTS, 0:1], ALU.pow).then_inc(s_prep_pool, 1)

        def l0_pe(pe):
            pe.wait_ge(s_prep_misc, PREP_MISC)
            pe.wait_ge(s_consts, 6)

            def embed(quad):
                pe.wait_ge(s_patches, nth(quad, 16, 16))
                for j in range(QP):
                    for e in range(2):
                        for c in range(PC):
                            mm = pe.matmul(P[64 * e:64 * e + T, 2 + j // 2, (j % 2) * D:(j % 2 + 1) * D],
                                           patches[:, c, 2 * j + e, :], w_patch[:, c, :],
                                           start=(c == 0), stop=(c == PC - 1), skip_group_check=True)
                    mm.then_inc(s_emb, 1)

            def quad(it, more):
                pe.wait_ge(s_yt, nth(it, 2, 2))
                pe_turn(pe, L0, it, h_in, s_hin, QP)
                pe_qk(pe, L0, it, 1, w_q0, w_k0)
                pe_v(pe, L0, it, 1, w_v0)
                pe_attention(pe, L0, it, 1, k_heads0)
                if more:
                    pe.wait_ge(L0["normed"], nth(it, QP, QP))
                    embed(it + 1)
                pe_turn_rows(pe, it, tok, s_tok, s_tokp)
                for j in range(QP):
                    pe.wait_ge(s_tokt, nth(it, 2, j // 2 + 1))
                    for kc in range(2):
                        mm = pe.matmul(P[0:ROWS, 6, j * SLOTS:(j + 1) * SLOTS], tok_t[:, j, kc, :], slots_t[:, kc, :],
                                       start=(kc == 0), stop=(kc == 1), skip_group_check=True)
                mm.then_inc(s_lg, 1)
                for j in range(QP):
                    for e in range(2):
                        for kc in range(2):
                            mm = pe.matmul(P[64 * e:64 * e + SLOTS, 7, j * T:(j + 1) * T], slots_t[:, kc, :],
                                           tok_t[:, j, kc, 64 * e:64 * e + T],
                                           start=(kc == 0), stop=(kc == 1), skip_group_check=True)
                mm.then_inc(s_lt, 1)
                settle(pe, s_cd, nth(it, 11, 11))
                for j in range(QP):
                    for e in range(2):
                        r = slice(64 * e, 64 * e + SLOTS)
                        mm = pe.matmul(P[64 * e:64 * e + T, 1, j * SLOTS:(j + 1) * SLOTS], dw[r, j, :], ident[r, r],
                                       start=True, stop=True, skip_group_check=True)
                mm.then_inc(s_dp, 1)
                for j in range(QP):
                    mm = pe.transpose(P[:, 0, j * ROWS:(j + 1) * ROWS], cw[0:ROWS, j, :], ident[0:ROWS, 0:ROWS])
                mm.then_inc(s_cp, 1)
                pe.wait_ge(s_dt, nth(it, 1, 1))
                for kc in range(2):
                    for e, j in [(e, j) for e in range(2) for j in range(QP)]:
                        mm = pe.matmul(P[0:FH, 6 + kc - 2 * e, j * SLOTS:(j + 1) * SLOTS],
                                       xn[64 * e:64 * e + T, j, kc * FH:(kc + 1) * FH], disp[64 * e:64 * e + T, j, :],
                                       start=True, stop=True, skip_group_check=True)
                    mm.then_inc(s_y, 1)

            embed(0)
            with pe.Fori(0, QUADS - 1) as it:
                quad(it, True)
            quad(QUADS - 1, False)

        def take_y(copy, it, kc):
            dst = y_t[0:FH, kc, :, ds(it * QB, QB)].rearrange("p s (j e) -> p e j s", e=2)
            for e in range(2):
                ins = copy(dst[:, e], P[0:FH, 6 + kc - 2 * e, 0:QP * SLOTS].rearrange("p (j s) -> p j s", j=QP))
            ins.then_inc(s_yt, 1)

        def l0_dve(dve):
            dve.wait_ge(s_prep_misc, PREP_MISC)
            with dve.Fori(0, QUADS) as it:
                for g in range(2):
                    dve.wait_ge(s_emb, nth(it, QP, 2 * g + 2))
                    dve.tensor_tensor(h_in[0:ROWS, 2 * g:2 * g + 2, :],
                                      P[0:ROWS, 2 + g, 0:2 * D].rearrange("p (j d) -> p j d", j=2),
                                      spread(embed_add[0:ROWS, :], 1, 2), ALU.add).then_inc(s_hin, 2)
                take_turned(dve, dve.tensor_copy, L0, it, 1, h_t)
                dve_k(dve, L0, it, 1, bias_km, k_heads0)
                dve_v(dve, L0, it, 1, True)
                dve_attention(dve, L0, it, 1)
                for j in range(QP):
                    dve.wait_ge(L0["normed"], nth(it, QP, j + 1))
                    dve.tensor_tensor(attn[0:ROWS, j, :], attn[0:ROWS, j, :], h_in[0:ROWS, j, :],
                                      ALU.add).then_inc(L0["resid"], 1)
                dve_ln(dve, L0, it, attn, h_out)
                for j in range(QP):
                    dve.wait_ge(L0["h_out"], nth(it, QP, j + 1))
                    dve.tensor_tensor_reduce(sq[0:ROWS, j, :], h_out[0:ROWS, j, :], h_out[0:ROWS, j, :], 1.0, 0.0,
                                             ALU.mult, ALU.add, norms[0:ROWS, 0, j:j + 1]).then_inc(s_ssq, 1)
                dve.wait_ge(s_rr, nth(it, 1, 1))
                for j in range(QP):
                    dve.scalar_tensor_tensor(xn[0:ROWS, j, :], h_out[0:ROWS, j, :], norms[0:ROWS, 2, j:j + 1],
                                             rowc[0:ROWS, 2, :], ALU.mult, ALU.mult).then_inc(s_xn, 1)
                for j in range(QP):
                    dve.wait_ge(s_xn, nth(it, QP, j + 1))
                    dve.tensor_tensor_reduce(sq[0:ROWS, j, :], xn[0:ROWS, j, :], xn[0:ROWS, j, :], 1.0, 0.0,
                                             ALU.mult, ALU.add, norms[0:ROWS, 3, j:j + 1]).then_inc(s_n2, 1)
                dve.wait_ge(s_tn, nth(it, 1, 1))
                for j in range(QP):
                    dve.tensor_scalar(tok[0:ROWS, j, :], xn[0:ROWS, j, :], small[0:ROWS, 1, j:j + 1], None,
                                      ALU.mult).then_inc(s_tok, 1)
                lg = P[0:ROWS, 6, 0:QP * SLOTS].rearrange("p (j s) -> p j s", j=QP)
                lt = P[:, 7, 0:QP * T].rearrange("p (j t) -> p j t", j=QP)
                dve.wait_ge(s_lg, nth(it, 1, 1))
                dve.tensor_reduce(rmx[0:ROWS, 0, :], lg, AX, ALU.max).then_inc(s_cd, 1)
                dve.wait_ge(s_lt, nth(it, 1, 1))
                dve.tensor_reduce(rmx[:, 3, :], lt, AX, ALU.max).then_inc(s_cd, 1)
                dve.wait_ge(s_cd, nth(it, 11, 1))
                dve.tensor_tensor(cw2[0:ROWS, :, :], lg, spread(rmx[0:ROWS, 0, :], 2, SLOTS), ALU.subtract).then_inc(s_cd, 1)
                dve.wait_ge(s_cd, nth(it, 11, 2))
                dve.tensor_tensor(dw2[:, :, :], lt, spread(rmx[:, 3, :], 2, T), ALU.subtract).then_inc(s_cd, 1)
                dve.wait_ge(s_ce, nth(it, 2, 1))
                dve.tensor_reduce(rmx[0:ROWS, 1, :], ce[0:ROWS, :, :], AX, ALU.add).then_inc(s_cd, 1)
                dve.wait_ge(s_ce, nth(it, 2, 2))
                dve.tensor_reduce(rmx[:, 4, :], de[:, :, :], AX, ALU.add).then_inc(s_cd, 1)
                dve.wait_ge(s_cd, nth(it, 11, 5))
                dve.reciprocal(rmx[0:ROWS, 2, :], rmx[0:ROWS, 1, :]).then_inc(s_cd, 1)
                dve.wait_ge(s_cd, nth(it, 11, 6))
                dve.reciprocal(rmx[:, 5, :], rmx[:, 4, :]).then_inc(s_cd, 1)
                dve.wait_ge(s_cd, nth(it, 11, 7))
                for e in range(2):
                    r = slice(64 * e, 64 * e + T)
                    dve.tensor_tensor(cw[r, :, e * SLOTS:(e + 1) * SLOTS], ce[r, :, :], spread(rmx[r, 2, :], 2, SLOTS),
                                      ALU.mult).then_inc(s_cd, 1)
                dve.wait_ge(s_cd, nth(it, 11, 8))
                dve.tensor_tensor(dw[:, :, :], de[:, :, :], spread(rmx[:, 5, :], 2, T), ALU.mult).then_inc(s_cd, 1)
                dve.wait_ge(s_dp, nth(it, 1, 1))
                dve.tensor_copy(disp[0:ROWS, :, :], P[0:ROWS, 1, 0:QP * SLOTS].rearrange("p (j s) -> p j s", j=QP)).then_inc(s_dt, 1)
                dve.wait_ge(s_y, nth(it, 2, 1))
                take_y(dve.tensor_copy, it, 0)

        def l0_act(act):
            act.wait_ge(s_prep_misc, PREP_MISC)
            act.wait_ge(s_consts, 6)
            with act.Fori(0, QUADS) as it:
                take_turned(act, act.copy, L0, it, 0, h_t)
                act_q(act, L0, it, 1, bias_qm, k_heads0)
                act_attention(act, L0, it, 1)
                take_rows(act, it, s_tokp, s_tokt)
                act.wait_ge(s_cd, nth(it, 11, 3))
                act.activation(ce[0:ROWS, :, :], cw2[0:ROWS, :, :], ACT.Exp).then_inc(s_ce, 1)
                act.wait_ge(s_cd, nth(it, 11, 4))
                act.activation(de[:, :, :], dw2[:, :, :], ACT.Exp).then_inc(s_ce, 1)
                act.wait_ge(s_cp, nth(it, 1, 1))
                act.copy(combine_all[:, ds(it * QP, QP), :],
                         P[:, 0, 0:QP * ROWS].rearrange("p (j t) -> p j t", j=QP)).then_inc(s_ct, 1)
                act.wait_ge(s_y, nth(it, 2, 2))
                take_y(act.copy, it, 1)

        def l0_pool(pool):
            with pool.Fori(0, QUADS) as it:
                pool_rstd(pool, L0, it)
                settle(pool, s_ssq, nth(it, QP, QP))
                pool.tensor_scalar(norms[0:ROWS, 1, :], norms[0:ROWS, 0, :], 1.0 / D, EPS, ALU.mult, ALU.add).then_inc(s_ms, 1)
                pool.wait_ge(s_ms, nth(it, 2, 1))
                pool.tensor_tensor(norms[0:ROWS, 2, :], norms[0:ROWS, 1, :], negh[0:ROWS, :], ALU.pow).then_inc(s_rr, 1)
                settle(pool, s_n2, nth(it, QP, QP))
                pool.tensor_scalar(small[0:ROWS, 0, :], norms[0:ROWS, 3, :], TINY, None, ALU.max).then_inc(s_ms, 1)
                pool.wait_ge(s_ms, nth(it, 2, 2))
                pool.tensor_tensor(small[0:ROWS, 1, :], small[0:ROWS, 0, :], negh[0:ROWS, :], ALU.pow).then_inc(s_tn, 1)
                pool.wait_ge(L0["h_out"], nth(it, QP, QP))
                pool.tensor_copy(h1_all[0:ROWS, ds(it * QP, QP), :], h_out[0:ROWS, :, :]).then_inc(s_keep, 1)

        def l0_sync(sp):
            sp.sem_inc(s_yt, 2)
            sp.sem_inc(LO["h_t"], QP)
            sp.sem_inc(s_ot, 1)
            sp.sem_inc(s_o2, 2)
            sp.sem_inc(s_ac, 2)
            sp.sem_inc(s_out, 32)
            for u in range(2):
                sp.sem_inc(s_yd[u], 16)
            for dst, name in SMALL_LOADS:
                sp.dma_start(dst[:], io[name]).then_inc(s_small, 16)
            sp.dma_start(patches[:, :, :, :], io["patches"][0]).then_inc(s_patches, 16)
            moe_sync_first(sp)
            with sp.Fori(1, QUADS) as it:
                sp.wait_ge(s_emb, it * QP)
                sp.dma_start(patches[:, :, :, :], io["patches"][it]).then_inc(s_patches, 16)

        CHUNKS = [(n * TC, min(TC, TOK - n * TC)) for n in range(3)]
        SPLIT = 4
        UNITS = [(sq, hh, c, j) for sq in range(2) for hh in range(2) for c in range(CH // 2) for j in range(4)]
        NU = len(UNITS)
        AHEAD = 2
        STACKED = 16 * 4 * PARTS
        PRODUCTS = [(0, 0), (0, 1), (1, 0), (0, 2), (1, 1), (2, 0)]

        def mlp_sync(sp):
            sp.wait_ge(LO["h_t"], QP + QP * QUADS)
            sp.wait_ge(s_h3, QUADS)
            sp.dma_start(w2[:, :, :, :], io["w2"]).then_inc(s_w2, 16)
            sp.wait_ge(s_zp, SPLIT)
            sp.dma_start(z_dram.rearrange("n p t -> p n t"), z_parts[:, :, :]).then_inc(s_zd, 16)
            sp.wait_ge(s_zd, 16)
            zv = z_dram.rearrange("n (s r) t -> n r s t", r=SR)
            for k, part in enumerate((0, 1, 2, 0, 1, 0)):
                sp.dma_start(zs[SR * k:SR * (k + 1), :, :], zv[part]).then_inc(s_zs, 16)
            for n in range(3):
                if n:
                    sp.wait_ge(s_ws, n * STACKED)
                tiles = -(-(n + 1) * TC // 128)
                sp.wait_ge(s_g1, tiles)
                sp.wait_ge(s_g2, tiles)
                for part in range(PARTS):
                    for q in range(4):
                        dst = ws[32 * part:32 * (part + 1), :, n * TC:(n + 1) * TC]
                        sp.dma_start(dst.rearrange("p (s q) t -> p q s t", q=4)[:, q],
                                     gate_parts[32 * q:32 * (q + 1), part, :, n * TC:(n + 1) * TC]).then_inc(s_ws, 16)

        def tile_pairs(eng, step):
            with eng.Fori(0, TT // 2 - 1) as it:
                step(it, False)
            step(TT // 2 - 1, True)

        def mlp_pe(pe):
            pe.wait_ge(LO["h_t"], QP + QP * QUADS)
            pe.wait_ge(s_late2, 16 * 4)
            for n, (at, cols) in enumerate(CHUNKS):
                for kc in range(2):
                    mm = pe.matmul(P[:, n, 0:cols], z_proj[:, kc, :],
                                   x3_t[:, kc, :, :].rearrange("p b t -> p (b t)")[:, at:at + cols],
                                   start=(kc == 0), stop=(kc == 1))
                mm.then_inc(s_z, 1)
            def scores(pair):
                for u in range(2):
                    pe.wait_ge(s_zt, nth(pair, 2, u + 1))
                    pe.matmul(P[:, 4 + u, :], z_tile[:, u, :], score_w[:, :], start=True, stop=True).then_inc(s_sc, 1)

            def step(it, last):
                if not last:
                    pe.wait_ge(s_sr, nth(it, 2, 2))
                    scores(it + 1)
                for u in range(2):
                    pe.wait_ge(s_gate, nth(it, 2, u + 1))
                    for sg in range(4):
                        mm = pe.transpose(P[:, 6 + u, sg * 128:(sg + 1) * 128], gate[:, u, sg * 128:(sg + 1) * 128],
                                          ident[:, :])
                    mm.then_inc(s_gt, 1)

            scores(0)
            tile_pairs(pe, step)
            pe.wait_ge(s_zs, 16 * 6)
            pe.wait_ge(s_w1s, 16 * 9)
            pe.wait_ge(s_set, 1)
            pe.wait_ge(s_split, 26)
            pe.wait_ge(s_w2, 16)
            with pe.Fori(0, 3) as it:
                pe.wait_ge(s_ws, nth(it, STACKED, STACKED))

                def hidden_rows(n):
                    sq, hh, c, j = UNITS[n]
                    seg, i = 4 * sq + j, hh * (CH // 2) + c
                    if n == 0:
                        pe.wait_ge(s_ot, nth(it, 1, 1))
                    if n >= 3:
                        pe.wait_ge(s_ua, nth(it, NU, n - 2))
                    pe.matmul(P[:, n % 3, 0:TC], w1s[:, seg, i * 128:(i + 1) * 128], zs[:, seg, ds(it * TC, TC)],
                              start=True, stop=True).then_inc(s_u1, 1)

                def gate_rows(n):
                    sq, hh, c, j = UNITS[n]
                    seg = 4 * sq + j
                    if n >= 3:
                        pe.wait_ge(s_ug, nth(it, NU, n - 2))
                    pe.matmul(P[:, 3 + n % 3, 0:TC], gate_sel[:, c, :], ws[:, 2 * seg + hh, ds(it * TC, TC)],
                              start=True, stop=True).then_inc(s_bc, 1)

                def last_bias(sq):
                    pe.wait_ge(s_ac, nth(it, 2, sq + 1))
                    for sg in (2 * sq, 2 * sq + 1):
                        for k, (g, b) in enumerate(PRODUCTS):
                            pe.matmul(P[:, 6 + sq, 0:TC], b2s[:, b, sg, :], gate_parts[:, g, sg, ds(it * TC, TC)],
                                      start=(sg == 2 * sq and k == 0), stop=False, skip_group_check=True)

                def expert_out(n):
                    sq, hh, c, j = UNITS[n]
                    seg, i = 4 * sq + j, hh * (CH // 2) + c
                    pe.wait_ge(s_ug, nth(it, NU, n + 1))
                    pe.matmul(P[32 * j:32 * j + 32, 6 + sq, 0:TC], w2[:, i, seg, :], gated[:, n % 8, :],
                              start=False, stop=(hh == 1 and c == CH // 2 - 1), skip_group_check=True).then_inc(s_u2, 1)

                for k in range(AHEAD):
                    hidden_rows(k)
                for n in range(0, NU + 4, 4):
                    for k in range(n, min(n + 4, NU)):
                        if k + AHEAD < NU:
                            hidden_rows(k + AHEAD)
                        gate_rows(k)
                    if n in (0, NU // 2):
                        last_bias(n // (NU // 2))
                    if n >= 4:
                        for k in range(n - 4, n):
                            expert_out(k)
                pe.wait_ge(s_ac, nth(it, 2, 4))
                for sq in range(2):
                    mm = pe.matmul(P[0:SG, 0, 0:TC], out1_w[:, sq, :], mlp_out[:, sq, :], start=(sq == 0), stop=(sq == 1))
                mm.then_inc(s_o1, 1)

        def mlp_act(act):
            act.wait_ge(LO["h_out"], QP * QUADS)
            for n, (at, cols) in enumerate(CHUNKS):
                act.wait_ge(s_z, n + 1)
                act.copy(z[:, at:at + cols], P[:, n, 0:cols]).then_inc(s_zc, 1)
            act.wait_ge(s_zc, 3)
            act.wait_ge(s_set, 1)

            def stage_tiles(pair):
                for u in range(2):
                    act.copy(z_tile[:, u, :], z[:, ds(pair * 256 + u * 128, 128)]).then_inc(s_zt, 1)

            def take_scores(pair):
                for u in range(2):
                    act.wait_ge(s_sc, nth(pair, 2, u + 1))
                    act.copy(scored[:, u, 0, :, 0:SM], P[:, 4 + u, :].rearrange("p (s m) -> p s m", m=SM)).then_inc(s_sr, 1)

            def step(it, last):
                if not last:
                    stage_tiles(it + 1)
                for u in range(2):
                    act.wait_ge(s_t4, nth(it, 4, 2 * u + 2))
                    act.activation(top_e[:, u, :, :], top_e[:, u, :, :], ACT.Exp).then_inc(s_ge, 1)
                    act.wait_ge(s_sh, nth(it, 2, u + 1))
                    act.activation(gate_e[:, u, :], gate_e[:, u, :], ACT.Exp).then_inc(s_ge, 1)
                if not last:
                    act.wait_ge(s_rp, nth(it, 2, 2))
                    take_scores(it + 1)
                for u in range(2):
                    act.wait_ge(s_gt, nth(it, 2, u + 1))
                    act.copy(gate_parts[:, 0, :, ds(it * 256 + u * 128, 128)],
                             P[:, 6 + u, :].rearrange("p (s t) -> p s t", s=4)).then_inc(s_g0, 1)
                for u in range(2):
                    act.wait_ge(s_gl, nth(it, 2, u + 1))
                    act.copy(gate_parts[:, 1, :, ds(it * 256 + u * 128, 128)],
                             gate_left[:, u, :].rearrange("p (s t) -> p s t", s=4)).then_inc(s_g1, 1)

            stage_tiles(0)
            take_scores(0)
            tile_pairs(act, step)
            act.wait_ge(s_g2, TT)
            with act.Fori(0, 3) as it:
                for n in range(NU):
                    act.wait_ge(s_u1, nth(it, NU, n + 1))
                    if n >= 4:
                        act.wait_ge(s_ug, nth(it, NU, n - 3))
                    act.activation(act_out[:, n % 4, :], P[:, n % 3, 0:TC], ACT.Gelu_apprx_tanh).then_inc(s_ua, 1)
                    if n == NU // 2 + 7:
                        act.wait_ge(s_u2, nth(it, NU, NU // 2))
                        act.copy(mlp_out[:, 0, :], P[:, 6, 0:TC]).then_inc(s_ac, 1)
                act.wait_ge(s_u2, nth(it, NU, NU))
                act.copy(mlp_out[:, 1, :], P[:, 7, 0:TC]).then_inc(s_ac, 1)
                act.wait_ge(s_o1, nth(it, 1, 1))
                act.activation(out_t[:, ds(it * TC, TC)], P[0:SG, 0, 0:TC], ACT.Gelu_apprx_tanh,
                               bias=out1_b[:, 0:1]).then_inc(s_ot, 1)

        def mlp_dve(dve):
            dve.wait_ge(LO["h_out"], QP * QUADS)
            dve.memset(z[:, TOK:TZ], 0.0).then_inc(s_zb, 1)
            dve.wait_ge(LO["h_t"], QP + QP * QUADS)
            dve.wait_ge(s_h3, QUADS)
            for u in range(2):
                dve.memset(scored[:, u, 0, :, SM:SM + SK], LOW).then_inc(s_zb, 1)
                dve.memset(top4[:, u, :, SK:2 * SK], LOW).then_inc(s_zb, 1)
            dve.memset(zs[6 * SR:ZR, :, :], 1.0).then_inc(s_set, 1)
            dve.wait_ge(s_zb, 1)
            dve.wait_ge(s_zc, 3)
            dve.tensor_copy(z_parts[:, 0, :], z[:, 0:TP]).then_inc(s_zp, 1)
            dve.wait_ge(s_zp, 1)
            dve.tensor_tensor(z_left[:, :], z[:, 0:TP], z_parts[:, 0, :], ALU.subtract).then_inc(s_zp, 1)
            dve.wait_ge(s_zp, 2)
            dve.tensor_copy(z_parts[:, 1, :], z_left[:, :]).then_inc(s_zp, 1)
            dve.wait_ge(s_zp, 3)
            dve.tensor_tensor(z_parts[:, 2, :], z_left[:, :], z_parts[:, 1, :], ALU.subtract).then_inc(s_zp, 1)
            dve.wait_ge(s_zb, 5)
            with dve.Fori(0, TT // 2) as it:
                for u in range(2):
                    settle(dve, s_sr, nth(it, 2, u + 1))
                    for s in range(SEG):
                        mx = dve.max(top8[:, u, s, :], scored[:, u, 0, s, 0:SM])
                    mx.then_inc(s_mx, 1)
                    dve.wait_ge(s_mx, nth(it, 2, u + 1))
                    dve.tensor_copy(top4[:, u, :, 0:SK], top8[:, u, :, 0:SK]).then_inc(s_t4, 1)
                    dve.tensor_tensor(top_e[:, u, :, :], top8[:, u, :, 0:SK], top8[:, u, :, 0:1].to_broadcast([128, SEG, SK]),
                                      ALU.subtract).then_inc(s_t4, 1)
                    settle(dve, s_t4, nth(it, 4, 2 * u + 1))
                    for s in range(SEG):
                        rp = dve.match_replace(scored[:, u, 1, s, :], top4[:, u, s, :], scored[:, u, 0, s, :], LOW)
                    rp.then_inc(s_rp, 1)
                for u in range(2):
                    dve.wait_ge(s_ge, nth(it, 4, 2 * u + 1))
                    dve.tensor_reduce(gate_sum[:, u, 0, :], top_e[:, u, :, :], AX, ALU.add).then_inc(s_gs, 1)
                    dve.wait_ge(s_gs, nth(it, 6, 3 * u + 1))
                    dve.reciprocal(gate_sum[:, u, 1, :], gate_sum[:, u, 0, :]).then_inc(s_gs, 1)
                    dve.wait_ge(s_ge, nth(it, 4, 2 * u + 2))
                    dve.wait_ge(s_rp, nth(it, 2, u + 1))
                    g = gate[:, u, :].rearrange("p (s m) -> p s m", m=SM)
                    dve.scalar_tensor_tensor(g, scored[:, u, 1, :, 0:SM], LOW,
                                             gate_e[:, u, :].rearrange("p (s m) -> p s m", m=SM),
                                             ALU.is_equal, ALU.mult).then_inc(s_gs, 1)
                    dve.wait_ge(s_gs, nth(it, 6, 3 * u + 3))
                    dve.tensor_tensor(g, g, spread(gate_sum[:, u, 1, :], 2, SM), ALU.mult).then_inc(s_gate, 1)
                for u in range(2):
                    dve.wait_ge(s_g0, nth(it, 2, u + 1))
                    dve.tensor_tensor(gate_left[:, u, :].rearrange("p (s t) -> p s t", s=4),
                                      P[:, 6 + u, :].rearrange("p (s t) -> p s t", s=4),
                                      gate_parts[:, 0, :, ds(it * 256 + u * 128, 128)], ALU.subtract).then_inc(s_gl, 1)
            with dve.Fori(0, 3) as it:
                for n in range(NU):
                    dve.wait_ge(s_ua, nth(it, NU, n + 1))
                    dve.wait_ge(s_bc, nth(it, NU, n + 1))
                    if n >= 8:
                        dve.wait_ge(s_u2, nth(it, NU, n - 7))
                    dve.tensor_tensor(gated[:, n % 8, :], act_out[:, n % 4, :], P[:, 3 + n % 3, 0:TC],
                                      ALU.mult).then_inc(s_ug, 1)

        def mlp_pool(pool):
            pool.wait_ge(s_zd, 16)
            with pool.Fori(0, TT // 2) as it:
                for u in range(2):
                    pool.wait_ge(s_mx, nth(it, 2, u + 1))
                    pool.tensor_tensor(gate_e[:, u, :].rearrange("p (s m) -> p s m", m=SM), scored[:, u, 0, :, 0:SM],
                                       top8[:, u, :, 0:1].to_broadcast([128, SEG, SM]), ALU.subtract).then_inc(s_sh, 1)
                for u in range(2):
                    pool.wait_ge(s_g1, nth(it, 2, u + 1))
                    at = ds(it * 256 + u * 128, 128)
                    pool.tensor_tensor(gate_parts[:, 2, :, at], gate_left[:, u, :].rearrange("p (s t) -> p s t", s=4),
                                       gate_parts[:, 1, :, at], ALU.subtract).then_inc(s_g2, 1)

        def last_pe(pe):
            with pe.Fori(0, QUADS) as it:
                settle(pe, LO["resid"], nth(it, QP, QP * QUADS))
                settle(pe, s_or, nth(it, 1, 1))
                for j in range(QP):
                    for e in range(2):
                        mm = pe.matmul(P[64 * e:64 * e + T, 2 + j // 2, (j % 2) * D:(j % 2 + 1) * D], out_r[:, 2 * j + e, :],
                                       out2_w[:, :], start=True, stop=True, skip_group_check=True)
                    if j % 2:
                        mm.then_inc(s_o2, 1)

        def last_act(act):
            act.wait_ge(s_ot, 4)
            with act.Fori(0, QUADS) as it:
                act.wait_ge(s_o2, nth(it, 2, 2))
                act.copy(out_r[:, :, :].rearrange("p b t -> p (b t)"), out_t[:, ds(it * QT, QT)]).then_inc(s_or, 1)

        def last_dve(dve):
            with dve.Fori(0, QUADS) as it:
                dve.wait_ge(LO["h_out"], nth(it, QP, QP * QUADS))
                for g in range(2):
                    dve.wait_ge(s_o2, nth(it, 2, 2 + g + 1))
                    dve.tensor_tensor(attn[0:ROWS, 2 * g:2 * g + 2, :], P[0:ROWS, 2 + g, 0:2 * D].rearrange("p (j d) -> p j d", j=2),
                                      h3_all[0:ROWS, ds(it * QP + 2 * g, 2), :], ALU.add).then_inc(LO["resid"], 2)
                dve.wait_ge(s_out, nth(it, 32, 32))
                dve_ln(dve, LO, it + QUADS, attn, h_out)

        def last_pool(pool):
            with pool.Fori(0, QUADS) as it:
                pool_rstd(pool, LO, it + QUADS)

        def last_sync(sp):
            out = io["out"].rearrange("(q j e) t d -> q e t j d", j=QP, e=2)
            with sp.Fori(0, QUADS) as it:
                sp.wait_ge(LO["h_out"], nth(it, QP, QP * QUADS + QP))
                for e in range(2):
                    sp.dma_start(out[it, e], h_out[64 * e:64 * e + T, :, :]).then_inc(s_out, 16)
            sp.wait_ge(s_out, 32 + 32 * QUADS)


        block = ctx.enter_context(nc.Block())
        @block.sync
        def _(sp):
            l0_sync(sp)
            moe_sync(sp)
            mlp_sync(sp)
            last_sync(sp)

        @block.tensor
        def _(pe):
            prep_pe(pe)
            l0_pe(pe)
            moe_pe(pe)
            l1_pe(pe)
            mlp_pe(pe)
            last_pe(pe)

        @block.vector
        def _(dve):
            prep_dve(dve)
            l0_dve(dve)
            moe_dve(dve)
            l1_dve(dve)
            mlp_dve(dve)
            last_dve(dve)

        @block.scalar
        def _(act):
            l0_act(act)
            moe_act(act)
            l1_act(act)
            mlp_act(act)
            last_act(act)

        @block.gpsimd
        def _(pool):
            prep_pool(pool)
            l0_pool(pool)
            split_pool(pool)
            l1_pool(pool)
            mlp_pool(pool)
            last_pool(pool)


def layout(x, np, **w):
    f = np.float32
    W = {k: np.asarray(v) for k, v in w.items()}
    x = np.asarray(x)
    d = {}
    d["ident"] = np.eye(128, dtype=f)
    d["hmask"] = np.repeat(np.eye(HH, dtype=f), HD, axis=0)
    d["bmask"] = np.repeat(d["hmask"], HD, axis=1)
    p = x.reshape(B, 6, 16, 6, 16, 3).transpose(0, 1, 3, 2, 4, 5).reshape(B, NPATCH, PC, 128)
    pz = np.zeros((B, T, PC, 128), f)
    pz[:, 1:] = p
    d["patches"] = np.ascontiguousarray(pz.reshape(QUADS, QB, T, PC, 128).transpose(0, 4, 3, 1, 2))
    d["w_patch"] = np.ascontiguousarray(W["L0_tok_W_proj"].reshape(PC, 128, D).transpose(1, 0, 2))
    rc = np.zeros((128, 6, D), f)
    for r in (0, 64):
        rc[r:r + T, 0] = W["L0_tok_pos_embedding"]
        rc[r, 1] = W["L0_tok_cls_token"].reshape(D)
        rc[r + 1:r + T, 1] = W["L0_tok_b_proj"]
    rc[:, 2] = W["L0_ffn_norm_weight"]
    eo = lambda a: a.reshape(-1, HH, 2, HD).transpose(0, 2, 1, 3).reshape(-1, 2, FH)
    bv = eo(W["L0_attn_bias_v"][None])[0]
    rc[0:64, 3, 0:FH] = bv[0]
    rc[64:, 3, 0:FH] = bv[1]
    rc[:, 4] = W["L1_attn_bo"]
    rc[:, 5] = W["L1_ffn_g2b"]
    d["rowc"] = rc
    d["lam"] = np.repeat(W["L1_attn_lambda_p"].reshape(1, NH), 128, axis=0)
    halves = lambda a: np.ascontiguousarray(a.reshape(2, FH, -1).transpose(1, 0, 2))
    d["v_q_t"] = np.ascontiguousarray(W["L0_attn_V_Q"].T)
    d["v_k_t"] = np.ascontiguousarray(W["L0_attn_V_K"].T)
    d["v_v_t"] = np.ascontiguousarray(W["L0_attn_V_V"].T)
    d["u_q_t"] = halves(np.ascontiguousarray(W["L0_attn_U_Q"].T))
    d["u_k"] = W["L0_attn_U_K"]
    d["u_v"] = np.ascontiguousarray(eo(W["L0_attn_U_V"]).reshape(R0, D))
    d["m_u"] = np.ascontiguousarray(np.tile(W["L0_attn_M_U"].T, (1, HH)))
    d["m_v"] = np.ascontiguousarray(np.tile(W["L0_attn_M_V"], (1, HH)))
    d["bias_qk"] = np.ascontiguousarray(np.stack([W["L0_attn_bias_q"].reshape(2, FH), W["L0_attn_bias_k"].reshape(2, FH)]).transpose(2, 0, 1))
    d["slots"] = W["L0_ffn_slots"]
    d["slot_scale"] = W["L0_ffn_scale"].reshape(SLOTS, 1)
    d["w_q1"] = halves(W["L1_attn_Wq"])
    d["w_k1"] = halves(W["L1_attn_Wk"])
    d["w_v1"] = halves(eo(W["L1_attn_Wv"]).reshape(D, D))
    d["w_o1"] = halves(W["L1_attn_Wo"])
    w = W["L0_ffn_fc1_weight"].reshape(GROUPS, GS, 2, FH, HID)
    fc1 = np.zeros((GROUPS, FH + 1, 2, GS, HID), f)
    fc1[:, :FH] = w.transpose(0, 3, 2, 1, 4)
    fc1[:, FH, 0] = W["L0_ffn_fc1_bias"].reshape(GROUPS, GS, HID)
    d["fc1"] = fc1
    w = W["L0_ffn_fc2_weight"].reshape(GROUPS, GS, HC, 128, D)
    d["fc2"] = np.ascontiguousarray(w.transpose(0, 3, 2, 1, 4))
    d["fc2_b"] = W["L0_ffn_fc2_bias"].reshape(GROUPS, GS, D)
    d["slot_sel"] = np.repeat(np.eye(GS, dtype=f), 32, axis=1)
    d["w1"] = np.ascontiguousarray(W["L1_ffn_W1"].transpose(0, 2, 1, 3).reshape(SEG * SR, SM * SH))
    d["b1"] = W["L1_ffn_b1"].reshape(128, 128)
    b2 = np.zeros((4, 2, SM, 4, 32), f)
    for s in range(SEG):
        b2[s // 2, s % 2, :, s % 4, :SR] = W["L1_ffn_b2"][s]
    d["b2"] = np.ascontiguousarray(b2.reshape(4, 128, 128).transpose(1, 0, 2)).reshape(128, 512)
    w = np.zeros((4, SH, CH, SEG, 32), f)
    w[..., :SR] = W["L1_ffn_W2"].reshape(SEG, CH, 4, SH, SR).transpose(2, 3, 1, 0, 4)
    d["w2"] = w.reshape(128, CH, SEG, 32)
    d["z_proj"] = halves(np.ascontiguousarray(W["L1_ffn_P"].transpose(1, 0, 2).reshape(D, SEG * SR)))
    sc = np.zeros((SEG, SR, SEG, SM), f)
    for s in range(SEG):
        sc[s, :, s] = W["L1_ffn_C"][s].T
    d["score_w"] = sc.reshape(128, SEG * SM)
    sel = np.zeros((PARTS, 32, SM // 8, 4, SH), f)
    for m in range(32):
        sel[:, m, m // 4, m % 4] = 1
    d["gate_sel"] = sel.reshape(PARTS * 32, 2, 512)
    g1 = np.zeros((4, 32, 2, SG), f)
    g1[:, :SR] = W["L1_ffn_G1"].reshape(2, 4, SR, SG).transpose(1, 2, 0, 3)
    d["out1_w"] = g1.reshape(128, 2, SG)
    d["out1_b"] = W["L1_ffn_g1b"].reshape(SG, 1)
    d["out2_w"] = W["L1_ffn_G2"]
    return d


def kernel(**inputs):
    import numpy as _np
    import concourse.bacc as _bacc
    from concourse import mybir as _mybir
    from concourse.bass_utils import run_bass_kernel_spmd as _run

    nc = _bacc.Bacc("TRN2", target_bir_lowering=False, num_devices=1)
    arrays, io = {}, {}
    for name, a in layout(np=_np, **inputs).items():
        a = _np.ascontiguousarray(a)
        arrays[f"in_{name}_dram"] = a
        io[name] = nc.dram_tensor(f"in_{name}_dram", a.shape, _mybir.dt.from_np(a.dtype), kind="ExternalInput").ap()
    io["out"] = nc.dram_tensor("out_0_dram", (B, T, D), _mybir.dt.float32, kind="ExternalOutput").ap()
    tower(nc, io)
    r = _run(nc, [arrays], core_ids=[0])
    return r.results[0]["out_0_dram"]
```

```python
from contextlib import ExitStack

import concourse.bass as bass
from concourse import mybir

B, T, D = 32, 37, 192
NPATCH = T - 1
PD = 768
PC = PD // 128
NH, HD = 12, 16
HH = NH // 2
FH = D // 2
R0 = 96
RM = 64
SLOTS = 64
HID = 768
HC = HID // 128
PAIRS = B // 2
QP = 4
QB = 2 * QP
QUADS = PAIRS // QP
QT = QB * T
ROWS = 64 + T
GS = 4
GROUPS = SLOTS // GS
TOK = B * T
SEG, SR, SM, SH, SK, SG = 8, 16, 64, 32, 4, 64
CH = SM * SH // 128
TC = 396
TP = 3 * TC
TT = 10
TZ = TT * 128
PARTS = 3
ZR = 6 * SR + PARTS
EPS = 1e-5
TINY = 1e-10
LOW = -3.0e38
WORK = 12310


def tower(nc, io):
    f32 = mybir.dt.float32
    bf16 = mybir.dt.bfloat16
    ALU = mybir.AluOpType
    ACT = mybir.ActivationFunctionType
    AX = mybir.AxisListType.X
    ds = bass.ds

    def spread(ap, axis, n):
        ap = ap.unsqueeze(axis)
        shape = list(ap.shape)
        shape[axis] = n
        return ap.to_broadcast(shape)

    def nth(step, per, n):
        return step * per + n

    def settle(eng, s, value):
        eng.wait_ge(s, value)
        eng.sem_inc(s_settled, 1)

    with ExitStack() as ctx:
        def sb(name, shape, dt=f32):
            return ctx.enter_context(nc.sbuf_tensor(name, shape, dt))

        def sem(name):
            return ctx.enter_context(nc.semaphore(name))

        def dram(name, shape, dt):
            return nc.dram_tensor(name, shape, dt, kind="Internal").ap()

        EXPERT, KH, ZW = 2 * GS * HID, 2 * QB * HH * T, SEG * TP // 2
        early = sb("early", [128, PC * QB * T + PC * D + KH + 2 * SLOTS * B])
        stream = sb("stream", [128, 2 * EXPERT + 2 * HC * GS * D])

        def tenant(home, rows, at, shape, dt=f32):
            n = 1
            for x in shape:
                n *= x
            words = n // (2 if dt == bf16 else 1)
            ap = home[0:rows, at:at + words]
            if dt != f32:
                ap = ap.bitcast(dt)
            names = "abcde"[:len(shape)]
            kw = {c: x for c, x in zip(names, shape)}
            return ap.rearrange(f"p ({' '.join(names)}) -> p {' '.join(names)}", **kw)

        class Tenants:
            def __init__(self, home, at=0):
                self.home, self.at = home, at

            def __call__(self, shape, dt=f32):
                ap = tenant(self.home, shape[0], self.at, shape[1:], dt)
                n = 1
                for x in shape[1:]:
                    n *= x
                self.at += n // (2 if dt == bf16 else 1)
                assert self.at <= self.home.shape[1], (self.at, self.home.shape)
                return ap

        patches = tenant(early, 128, 0, [PC, QB, T])
        w_patch = tenant(early, 128, PC * QB * T, [PC, D])
        k_heads0 = tenant(early, FH, PC * QB * T + PC * D, [1, 2, QB, HH, T])
        y_t = tenant(early, FH + 1, PC * QB * T + PC * D + KH, [2, SLOTS, B])
        fc1 = tenant(stream, FH + 1, 0, [2, 2, GS, HID])
        fc2 = tenant(stream, 128, 2 * EXPERT, [2, HC, GS, D])
        k_heads1 = tenant(stream, FH, 0, [2, 2, QB, HH, T])
        w1s = tenant(stream, ZR, 2 * EXPERT + 2 * HC * GS * D - SEG * SM * SH // 2, [SEG, SM * SH], bf16)
        late = Tenants(stream, KH * 2)
        w_q1 = late([FH, 2, 2 * D])
        w_k1 = late([FH, 2, 2 * D])
        w_v1 = late([FH, 2, D])
        w_o1 = late([FH, 2, D])
        gate_parts = tenant(stream, 128, 0, [PARTS, 4, TZ], bf16)
        zs = tenant(stream, ZR, PARTS * 4 * TZ // 2, [SEG, TP], bf16)
        ws = tenant(early, PARTS * 32, 0, [2 * SEG, TP], bf16)

        ident = sb("ident", [128, 128])
        hmask = sb("hmask", [FH, HH])
        bmask = sb("bmask", [FH, FH])
        rowc = sb("rowc", [128, 6, D])
        embed_add = sb("embed_add", [128, D])
        lam = sb("lam", [128, NH])
        negh = sb("negh", [128, QP])
        prep = Tenants(early, PC * QB * T + PC * D + KH)
        v_q_t = prep([R0, D])
        u_q_t = prep([FH, 2, R0])
        v_k_t = prep([R0, D])
        u_k = prep([R0, D])
        v_v_t = prep([R0, D])
        u_v = prep([R0, D])
        m_u = prep([RM, FH])
        m_v = prep([RM, FH])
        bias_qk = sb("bias_qk", [FH, 2, 2])
        mixer = prep([FH, FH])
        u_qm = prep([R0, D])
        middle = sb("middle", [128, PARTS * 4 * 64 + SM // 8 * 64])
        w = Tenants(middle)
        w_q0 = w([FH, 2, D])
        w_k0 = w([FH, 2, D])
        w_v0 = w([FH, 2, D])
        w = Tenants(middle)
        b2s = w([128, PARTS, 4, 128], bf16)
        gate_sel = w([PARTS * 32, SM // 8, 128], bf16)
        bias_qm = sb("bias_qm", [FH, 2])
        bias_km = sb("bias_km", [FH, 2, HH])
        slots = prep([SLOTS, D])
        slot_scale = sb("slot_scale", [SLOTS, 1])
        slot_n = sb("slot_n", [SLOTS, 4])
        slot_dir = prep([SLOTS, D])
        slots_t = sb("slots_t", [FH, 2, SLOTS])

        slot_sel = sb("slot_sel", [GS, 128])
        out1_b = sb("out1_b", [SG, 1])

        h1_all = sb("h1_all", [128, PAIRS, D])
        h3_all = h1_all
        combine_all = sb("combine_all", [128, PAIRS, ROWS])

        work = sb("work", [128, WORK])
        w = Tenants(work)
        v_blk = w([128, QB, HH, 2 * (HD + 1)])
        probs = w([128, 2, HH, 2, 64])
        h_in = w([128, QP, D])
        attn = w([128, QP, D])
        attn2 = w([128, 2, D])
        row_max = w([128, 2, NH])
        rsum = w([128, 2, 2, NH])
        stats = w([128, QP, 6])
        mv = w([128, QP, 2])
        rstd = w([128, QP])
        var_e = w([128, QP])
        h_out = w([128, QP, D])
        norms = w([128, 4, QP])
        small = w([128, 6, QP])
        rmx = w([128, 6, QP])
        shared = w.at
        h_t = w([FH, 2, QB, T])
        q_t = w([FH, 2, 2, QB * T])
        sq = tenant(work, 128, w.at, [QP, D])
        shifted = w([128, 2, NH, T])
        turned = w.at
        probs_t = w([128, 2, HH, ROWS])
        tok_t = w([FH, QP, 2, ROWS])
        xn = w([128, QP, D])
        tok = attn
        r = Tenants(work, turned)
        cw2 = r([128, QP, SLOTS])
        dw = r([128, QP, T])
        dw2 = r([128, QP, T])
        disp = r([128, QP, SLOTS])
        ce = r([128, QP, SLOTS])
        de = r([128, QP, T])
        assert r.at <= turned + 2 * HH * ROWS
        cw = sb("cw", [128, QP, 2 * SLOTS])
        w = Tenants(work, shared)
        y_ring = w([FH + 1, 2, 2, GS * B])
        hidden = w([128, 2, 2, HID // 2])
        hidden_t = w([128, 2, HC, 128])
        y_out = w([128, 2, D])
        moe_end = w.at
        w = Tenants(work)
        w2 = w([128, CH, SEG, 32])
        act_out = w([128, 4, TC])
        gated = tenant(work, 128, w.at, [8, TC])
        w.at += 4 * TC
        z = w([128, TZ])
        z_left = w([128, TP])
        z_parts = w([128, PARTS, TP], bf16)
        mlp_out = w([128, 2, TC])
        w = Tenants(work, CH * SEG * 32)
        scored = w([128, 2, 2, SEG, SM + SK])
        z_tile = w([128, 2, 128])
        top8 = w([128, 2, SEG, 8])
        top4 = w([128, 2, SEG, 8])
        top_e = w([128, 2, SEG, SK])
        gate_sum = w([128, 2, 2, SEG])
        assert w.at <= CH * SEG * 32 + 8 * TC
        w = Tenants(early)
        y2 = w([128, PAIRS, D])
        x3_t = w([FH, 2, B, T])
        comb_r = w([128, QP, ROWS])
        w = Tenants(work, CH * SEG * 32 + 8 * TC + TZ)
        gate_e = w([128, 2, SEG * SM])
        gate = w([128, 2, SEG * SM])
        gate_left = w([128, 2, SEG * SM])

        P = ctx.enter_context(nc.psum_tensor("P", [128, 8, 512], f32))

        s_small = sem("s_small_loaded")
        s_psum0 = sem("s_psum_cleared")
        s_prep_pe = sem("s_prep_products")
        s_prep_dve = sem("s_prep_taken")
        s_prep_pool = sem("s_prep_powers")
        s_patches = sem("s_patches_loaded")
        s_wpatch = sem("s_patch_weights_loaded")
        s_emb = sem("s_embedded")
        s_hin = sem("s_h_in_ready")
        s_done = sem("s_done")
        s_settled = sem("s_settled_waits")
        s_slot_dir = sem("s_slot_dir")
        s_slot_sum = sem("s_slot_sum")
        s_consts = sem("s_consts_set")
        s_vz = sem("s_v_blk_cleared")
        s_prep_misc = sem("s_prep_weights")

        NORM = "resid stats mv var rstd h_out"
        TURN = "h_turned h_t"
        ATTENTION = ("q_made k_made v_made q_ready k_ready_a k_ready_v v_ready scores row_max shifted probs "
                     "probs_turned probs_t mixed sums normed")

        def layer_sems(p, *names):
            return {n: sem(f"{p}_{n}") for n in " ".join(names).split()}

        L0 = layer_sems("l0", TURN, ATTENTION, NORM)
        s_ssq = sem("s_square_sums")
        s_ms = sem("s_mean_squares")
        s_rr = sem("s_rms")
        s_xn = sem("s_xn")
        s_n2 = sem("s_norm_squares")
        s_tn = sem("s_tok_norms")
        s_tok = sem("s_tok")
        s_tokp = sem("s_tok_turned")
        s_tokt = sem("s_tok_t")
        s_lg = sem("s_logits")
        s_lt = sem("s_logits_t")
        s_cd = sem("s_routing_steps")
        s_ce = sem("s_routing_exps")
        s_cp = sem("s_combine_turned")
        s_ct = sem("s_combine_t")
        s_dp = sem("s_dispatch_turned")
        s_dt = sem("s_dispatch")
        s_y = sem("s_slot_inputs")
        s_yt = sem("s_slot_inputs_taken")
        s_keep = sem("s_h1_kept")

        SMALL_LOADS = [
            (ident, "ident"), (hmask, "hmask"), (bmask, "bmask"), (rowc, "rowc"), (lam, "lam"),
            (v_q_t, "v_q_t"), (u_q_t, "u_q_t"), (v_k_t, "v_k_t"), (u_k, "u_k"), (v_v_t, "v_v_t"), (u_v, "u_v"),
            (m_u, "m_u"), (m_v, "m_v"), (bias_qk, "bias_qk"), (slots, "slots"), (slot_scale, "slot_scale"),
            (slot_sel, "slot_sel"), (out1_b, "out1_b")]
        SMALL = 16 * len(SMALL_LOADS)

        def pe_turn(pe, L, it, src, ready, per, past=0):
            for j in range(QP):
                pe.wait_ge(ready, nth(it, per, past * per + j + 1))
                for kc in range(2):
                    at = ((j % 2) * 2 + kc) * 128
                    mm = pe.transpose(P[0:FH, 4 + j // 2, at:at + ROWS],
                                      src[0:ROWS, j, kc * FH:(kc + 1) * FH], ident[0:ROWS, 0:ROWS])
                if j % 2:
                    mm.then_inc(L["h_turned"], 1)

        def take_turned(eng, copy, L, it, g, dst):
            eng.wait_ge(L["h_turned"], nth(it, 2, g + 1))
            src = P[0:FH, 4 + g, :].rearrange("p (j k e r) -> p j k e r", j=2, k=2, e=2)
            for j in range(2):
                copy(dst[:, :, 4 * g + 2 * j:4 * g + 2 * j + 2, :], src[:, j, :, :, 0:T]).then_inc(L["h_t"], 1)

        def pe_qk(pe, L, it, which, w_q, w_k):
            pe.wait_ge(L["h_t"], nth(it, QP, QP))
            for m in which:
                for w, at, made in ((w_q, 4 * m, "q_made"), (w_k, 4 * m + 2, "k_made")):
                    for mc in range(2):
                        for kc in range(2):
                            mm = pe.matmul(P[0:FH, at + mc, 0:QT], w[:, kc, m * D + mc * FH:m * D + (mc + 1) * FH],
                                           h_t[:, kc, :, :], start=(kc == 0), stop=(kc == 1))
                        mm.then_inc(L[made], 1)

        def v_bank(maps):
            return 6 if maps == 1 else 2

        def pe_v(pe, L, it, maps, w_v):
            if maps == 2:
                pe.wait_ge(L["k_ready_a"], nth(it, HH * maps, HH))
                pe.wait_ge(L["k_ready_v"], nth(it, HH * maps, HH))
            for b in range(QB):
                for e in range(2):
                    for kc in range(2):
                        mm = pe.matmul(P[64 * e:64 * e + T, v_bank(maps) + b // 4, (b % 4) * FH:(b % 4 + 1) * FH],
                                       h_t[:, kc, b, :], w_v[:, kc, e * FH:(e + 1) * FH],
                                       start=(kc == 0), stop=(kc == 1), skip_group_check=True)
                if b % 4 == 3:
                    mm.then_inc(L["v_made"], 1)

        def pe_scores(pe, L, it, maps, u, k_heads):
            j, m = u // maps, u % maps
            if u == 0:
                pe.wait_ge(L["q_ready"], nth(it, 2 * maps, 2 * maps))
                pe.wait_ge(L["k_ready_a"], nth(it, HH * maps, HH * maps))
                pe.wait_ge(L["k_ready_v"], nth(it, HH * maps, HH * maps))
            if u >= 2:
                pe.wait_ge(L["shifted"], nth(it, QP * maps, u - 1))
            for e in range(2):
                b = 2 * j + e
                for mc in range(2):
                    mm = pe.matmul(P[64 * e:64 * e + T, u % 2, mc * HH * T:(mc + 1) * HH * T],
                                   q_t[:, m, mc, b * T:(b + 1) * T], k_heads[:, m, mc, b, :, :],
                                   start=True, stop=True, skip_group_check=True)
            mm.then_inc(L["scores"], 1)

        def pe_turn_probs(pe, L, it, maps, u):
            pe.wait_ge(L["probs"], nth(it, QP * maps, u + 1))
            if u == 0 and maps == 1:
                pe.wait_ge(L["v_ready"], nth(it, 4, 4))
            for hp in range(HH):
                mm = pe.transpose(P[:, 4 + 2 * (u % 2) + hp // 3, (hp % 3) * ROWS:(hp % 3 + 1) * ROWS],
                                  probs[0:ROWS, u % 2, hp, :, :].rearrange("p a k -> p (a k)"), ident[0:ROWS, 0:ROWS])
            mm.then_inc(L["probs_turned"], 1)

        def pe_mix(pe, L, it, maps, u):
            j = u // maps
            pe.wait_ge(L["probs_t"], nth(it, QP * maps, u + 1))
            if u == 0:
                pe.wait_ge(L["v_ready"], nth(it, 4, 4))
            if u >= 2:
                pe.wait_ge(L["normed"], nth(it, QP * maps, u - 1))
            for e in range(2):
                for hp in range(HH):
                    w2 = 2 * (HD + 1)
                    mm = pe.matmul(P[64 * e:64 * e + T, 2 + u % 2, hp * w2:(hp + 1) * w2],
                                   probs_t[0:ROWS, u % 2, hp, 64 * e:64 * e + T], v_blk[0:ROWS, 2 * j + e, hp, :],
                                   start=True, stop=True, skip_group_check=True)
            mm.then_inc(L["mixed"], 1)

        def pe_attention(pe, L, it, maps, k_heads, after_first=None, before_turn=None, beside_mix=None):
            U = QP * maps
            for k in range(U + 2):
                if k == 1 and after_first:
                    after_first()
                if k < U:
                    pe_scores(pe, L, it, maps, k, k_heads)
                if k == 1 and before_turn:
                    before_turn()
                if 1 <= k <= U:
                    pe_turn_probs(pe, L, it, maps, k - 1)
                if k >= 2:
                    pe_mix(pe, L, it, maps, k - 2)
                    if beside_mix and k - 2 < QP:
                        beside_mix(k - 2)

        def act_q(act, L, it, maps, which, bias, k_heads):
            for m in which:
                for mc in range(2):
                    act.wait_ge(L["q_made"], nth(it, 2 * maps, 2 * m + mc + 1))
                    act.activation(q_t[:, m, mc, :], P[0:FH, 4 * m + mc, 0:QT], ACT.Identity,
                                   bias=0.0 if bias is None else bias[:, mc:mc + 1]).then_inc(L["q_ready"], 1)
                act.wait_ge(L["k_made"], nth(it, 2 * maps, 2 * m + 1))
                for h in range(HH):
                    act.activation(k_heads[:, m, 0, :, h, :], P[0:FH, 4 * m + 2, 0:QT].rearrange("p (b t) -> p b t", t=T),
                                   ACT.Identity, scale=hmask[:, h:h + 1],
                                   bias=0.0 if bias is None else bias_km[:, 0, h:h + 1]).then_inc(L["k_ready_a"], 1)

        def dve_k(dve, L, it, maps, which, bias, k_heads):
            for m in which:
                dve.wait_ge(L["k_made"], nth(it, 2 * maps, 2 * m + 2))
                for h in range(HH):
                    src = P[0:FH, 4 * m + 3, 0:QT].rearrange("p (b t) -> p b t", t=T)
                    if bias is None:
                        ins = dve.tensor_scalar(k_heads[:, m, 1, :, h, :], src, hmask[:, h:h + 1], None, ALU.mult)
                    else:
                        ins = dve.tensor_scalar(k_heads[:, m, 1, :, h, :], src, hmask[:, h:h + 1],
                                                bias_km[:, 1, h:h + 1], ALU.mult, ALU.add)
                    ins.then_inc(L["k_ready_v"], 1)

        def dve_v(dve, L, it, maps, bias):
            for half in range(2):
                dve.wait_ge(L["v_made"], nth(it, 2, half + 1))
                for e in range(2):
                    rows = slice(64 * e, 64 * e + T)
                    src = P[rows, v_bank(maps) + half, 0:4 * FH].rearrange("p (b h d) -> p b h d", b=4, d=HD)
                    dst = v_blk[rows, 4 * half:4 * half + 4, :, e * (HD + 1):e * (HD + 1) + HD]
                    if bias:
                        add = spread(rowc[rows, 3, 0:FH].rearrange("p (h d) -> p h d", d=HD), 1, 4)
                        ins = dve.tensor_tensor(dst, src, add, ALU.add)
                    else:
                        ins = dve.tensor_copy(dst, src)
                    ins.then_inc(L["v_ready"], 1)

        def dve_softmax(dve, L, it, maps, u):
            src = P[0:ROWS, u % 2, 0:NH * T].rearrange("p (h k) -> p h k", k=T)
            dve.wait_ge(L["scores"], nth(it, QP * maps, u + 1))
            dve.tensor_reduce(row_max[0:ROWS, u % 2, :], src, AX, ALU.max).then_inc(L["row_max"], 1)
            dve.wait_ge(L["row_max"], nth(it, QP * maps, u + 1))
            if u >= 2:
                dve.wait_ge(L["probs"], nth(it, QP * maps, u - 1))
            dve.tensor_tensor(shifted[0:ROWS, u % 2, :, :], src, spread(row_max[0:ROWS, u % 2, :], 2, T),
                              ALU.subtract).then_inc(L["shifted"], 1)

        def act_exp(act, L, it, maps, u):
            act.wait_ge(L["shifted"], nth(it, QP * maps, u + 1))
            act.activation(probs[0:ROWS, u % 2, :, :, 0:T].rearrange("p a b k -> p (a b) k"), shifted[0:ROWS, u % 2, :, :],
                           ACT.Exp, scale=HD ** -0.5).then_inc(L["probs"], 1)

        def act_probs_t(act, L, it, maps, u):
            act.wait_ge(L["probs_turned"], nth(it, QP * maps, u + 1))
            if u >= 2:
                act.wait_ge(L["mixed"], nth(it, QP * maps, u - 1))
            act.activation(probs_t[:, u % 2, :, :].rearrange("p (g h) t -> p g (h t)", g=2),
                           P[:, 4 + 2 * (u % 2):6 + 2 * (u % 2), 0:3 * ROWS], ACT.Copy).then_inc(L["probs_t"], 1)

        def act_attention(act, L, it, maps, after_first=None):
            U = QP * maps
            for k in range(U + 1):
                if k < U:
                    act_exp(act, L, it, maps, k)
                if k == 0 and after_first:
                    after_first()
                if k >= 1:
                    act_probs_t(act, L, it, maps, k - 1)

        def dve_norm(dve, L, it, maps, u):
            j, m = u // maps, u % maps
            U = QP * maps
            o = P[0:ROWS, 2 + u % 2, 0:NH * (HD + 1)].rearrange("p (h c) -> p h c", c=HD + 1)
            r = rsum[0:ROWS, u % 2]
            dve.wait_ge(L["mixed"], nth(it, U, u + 1))
            step = nth(it, QP * (2 if maps == 1 else 5), j * (2 if maps == 1 else 5) + 2 * m)
            dve.tensor_scalar(r[:, 0, :], o[:, :, HD], 0.5, None, ALU.max).then_inc(L["sums"], 1)
            dve.wait_ge(L["sums"], step + 1)
            dve.reciprocal(r[:, 1, :], r[:, 0, :]).then_inc(L["sums"], 1)
            dve.wait_ge(L["sums"], step + 2)
            if m:
                dve.tensor_tensor(r[:, 0, :], r[:, 1, :], lam[0:ROWS, :], ALU.mult).then_inc(L["sums"], 1)
                dve.wait_ge(L["sums"], step + 3)
            out = attn[0:ROWS, j, :] if m == 0 else attn2[0:ROWS, j % 2, :]
            by = r[:, 0 if m else 1, :]
            out = out.rearrange("p (h d) -> p h d", d=HD)
            dve.tensor_tensor(out, o[:, :, 0:HD], spread(by, 2, HD), ALU.mult).then_inc(L["normed"], 1)
            if m:
                dve.wait_ge(L["normed"], nth(it, U, u + 1))
                dve.tensor_tensor(attn[0:ROWS, j, :], attn[0:ROWS, j, :], attn2[0:ROWS, j % 2, :],
                                  ALU.subtract).then_inc(L["mapped"], 1)

        def dve_attention(dve, L, it, maps, between=None):
            U = QP * maps
            for k in range(U + 2):
                if k < U:
                    dve_softmax(dve, L, it, maps, k)
                if between and k in between:
                    between[k]()
                if k >= 2:
                    dve_norm(dve, L, it, maps, k - 2)

        def pe_turn_rows(pe, it, src, ready, turned, bank):
            for j in range(QP):
                pe.wait_ge(ready, nth(it, QP, j + 1))
                for kc in range(2):
                    at = ((j % 2) * 2 + kc) * ROWS
                    mm = pe.transpose(P[0:FH, bank + j // 2, at:at + ROWS], src[0:ROWS, j, kc * FH:(kc + 1) * FH],
                                      ident[0:ROWS, 0:ROWS])
                if j % 2:
                    mm.then_inc(turned, 1)

        def take_rows(act, it, turned, taken, bank):
            for g in range(2):
                act.wait_ge(turned, nth(it, 2, g + 1))
                act.copy(tok_t[:, 2 * g:2 * g + 2, :, :].rearrange("p j k t -> p (j k t)"),
                         P[0:FH, bank + g, 0:4 * ROWS]).then_inc(taken, 1)

        def dve_ln(dve, L, it, src, dst):
            ln_moments(dve, L, it, src)
            ln_scale(dve, L, it, src, dst)

        def ln_moments(dve, L, it, src):
            for j in range(QP):
                dve.wait_ge(L["resid"], nth(it, QP, j + 1))
                dve.bn_stats(stats[0:ROWS, j, :], src[0:ROWS, j, :]).then_inc(L["stats"], 1)
            for j in range(QP):
                settle(dve, L["stats"], nth(it, QP, j + 1))
                dve.bn_aggr(mv[0:ROWS, j, :], stats[0:ROWS, j, :]).then_inc(L["mv"], 1)

        def ln_scale(dve, L, it, src, dst):
            dve.wait_ge(L["rstd"], nth(it, 1, 1))
            for j in range(QP):
                dve.tensor_scalar(dst[0:ROWS, j, :], src[0:ROWS, j, :], mv[0:ROWS, j, 0:1], rstd[0:ROWS, j:j + 1],
                                  ALU.subtract, ALU.mult).then_inc(L["h_out"], 1)

        def pool_rstd(pool, L, it):
            settle(pool, L["mv"], nth(it, QP, QP))
            pool.tensor_scalar(var_e[0:ROWS, :], mv[0:ROWS, :, 1], EPS, None, ALU.add).then_inc(L["var"], 1)
            pool.wait_ge(L["var"], nth(it, 1, 1))
            pool.tensor_tensor(rstd[0:ROWS, :], var_e[0:ROWS, :], negh[0:ROWS, :], ALU.pow).then_inc(L["rstd"], 1)
        fc2_b = sb("fc2_b", [GS, 2, D])
        w = Tenants(stream, PARTS * 4 * TZ // 2 + ZW)
        z_proj = w([FH, 2, 128])
        out1_w = w([128, 2, SG])
        out2_w = w([SG, D])
        w = Tenants(early, SEG * TP)
        score_w = w([128, SEG * SM])
        w = Tenants(work, moe_end)
        split_in = w([128, 512])
        split_left = w([128, 512])
        split_out = w([128, PARTS, 512], bf16)
        out_t = tenant(combine_all[:, :, :].rearrange("p a b -> p (a b)"), SG, 0, [TP])
        y_dram = dram("y_dram", [SLOTS, B, D], f32)
        w1_dram = dram("w1_dram", [PARTS, 128, SM * SH], bf16)
        b1_dram = dram("b1_dram", [PARTS, 128, 128], bf16)
        z_dram = dram("z_dram", [PARTS, 128, TP], bf16)
        s_late2 = sem("s_mlp_weights_loaded")
        s_fc1 = [sem("s_fc1_even"), sem("s_fc1_odd")]
        s_fc2 = [sem("s_fc2_even"), sem("s_fc2_odd")]
        s_yr = sem("s_slot_inputs_staged")
        s_hid = sem("s_hidden_made")
        s_act = sem("s_hidden_active")
        s_hp = sem("s_hidden_turned")
        s_ht = sem("s_hidden_t")
        s_fo = sem("s_slots_out_made")
        s_yo = sem("s_slots_out_taken")
        s_yd = [sem("s_slots_out_stored_even"), sem("s_slots_out_stored_odd")]
        s_split_in = sem("s_split_loaded")
        s_split = sem("s_split_steps")
        s_split_out = sem("s_split_stored")
        s_b2 = sem("s_b2_loaded")
        s_late = sem("s_late_weights_loaded")
        s_y2 = sem("s_slot_outputs_loaded")
        s_lam = sem("s_lambda")
        s_cr = sem("s_combine_staged")
        s_mix = sem("s_combined")
        L1 = layer_sems("l1", TURN, ATTENTION, "mapped")
        LO = layer_sems("lo", NORM, TURN)
        s_at = sem("s_attn_turned")
        s_att = sem("s_attn_t")
        s_wo = sem("s_attn_projected")
        s_hb = sem("s_h_in_and_bias")
        s_h3 = sem("s_h3_kept")
        s_x3p = sem("s_x3_turned")
        s_w1s = sem("s_w1_stacked")
        s_w2 = sem("s_w2_loaded")
        s_z = sem("s_z_made")
        s_zc = sem("s_z_taken")
        s_zp = sem("s_z_split_steps")
        s_zd = sem("s_z_parts_stored")
        s_zs = sem("s_z_parts_stacked")
        s_set = sem("s_mlp_ones_set")
        s_zb = sem("s_mlp_padding_set")
        s_zt = sem("s_z_tile")
        s_sc = sem("s_scores_made")
        s_sr = sem("s_scores_taken")
        s_mx = sem("s_top8")
        s_t4 = sem("s_top4")
        s_rp = sem("s_top_marked")
        s_gs = sem("s_gate_steps")
        s_gate = sem("s_gates")
        s_sh = sem("s_scores_shifted")
        s_ge = sem("s_gate_exps")
        s_gt = sem("s_gates_turned")
        s_g0 = sem("s_gate_first_part")
        s_g1 = sem("s_gate_second_part")
        s_g2 = sem("s_gate_third_part")
        s_gl = sem("s_gate_rest")
        s_ws = sem("s_gate_parts_stacked")
        s_u1 = sem("s_unit_hidden")
        s_bc = sem("s_unit_gate_spread")
        s_ua = sem("s_unit_active")
        s_ug = sem("s_unit_gated")
        s_u2 = sem("s_unit_summed")
        s_ac = sem("s_segments_taken")
        s_o1 = sem("s_out1_made")
        s_ot = sem("s_out1_active")
        s_o2 = sem("s_out2_made")
        s_out = [sem("s_out_stored_even"), sem("s_out_stored_odd")]

        def moe_sync_first(sp):
            for g in range(2):
                sp.dma_start(fc1[:, g], io["fc1"][g]).then_inc(s_fc1[g], 16)
                sp.dma_start(fc2[:, g], io["fc2"][g]).then_inc(s_fc2[g], 16)
                sp.dma_start(fc2_b[:, g, :], io["fc2_b"][g]).then_inc(s_fc2[g], 16)

        def moe_sync(sp):
            def store(g, u):
                sp.dma_start(y_dram.rearrange("s b d -> (s b) d")[ds(g * 128, 128), :], y_out[:, u, :]).then_inc(s_yd[u], 16)

            with sp.Fori(1, GROUPS // 2) as it:
                for u in range(2):
                    sp.wait_ge(s_hid, it * 2 + (u - 1))
                    sp.dma_start(fc1[:, u], io["fc1"][it * 2 + u]).then_inc(s_fc1[u], 16)
                    sp.wait_ge(s_fo, it * 2 + (u - 1))
                    sp.dma_start(fc2[:, u], io["fc2"][it * 2 + u]).then_inc(s_fc2[u], 16)
                    sp.dma_start(fc2_b[:, u, :], io["fc2_b"][it * 2 + u]).then_inc(s_fc2[u], 16)
                    sp.wait_ge(s_yo, it * 2 + (u - 1))
                    store(it * 2 + (u - 2), u)
            for g in (GROUPS - 2, GROUPS - 1):
                sp.wait_ge(s_yo, g + 1)
                store(g, g % 2)
            for dst, name in ((w_q1, "w_q1"), (w_k1, "w_k1"), (w_v1, "w_v1"), (w_o1, "w_o1")):
                sp.dma_start(dst, io[name]).then_inc(s_late, 16)
            for u in range(2):
                sp.wait_ge(s_yd[u], 16 + 16 * (GROUPS // 2))
            for e in range(2):
                sp.dma_start(y2[64 * e:64 * e + SLOTS, :, :],
                             y_dram.rearrange("s (p e) d -> e s p d", e=2)[e]).then_inc(s_y2, 16)
            for dst, name in ((z_proj, "z_proj"), (out1_w, "out1_w"), (out2_w, "out2_w"),
                              (score_w, "score_w")):
                sp.dma_start(dst, io[name]).then_inc(s_late2, 16)
            sp.wait_ge(s_split_out, 16 * 5)
            w1v = w1_dram.rearrange("n (s r) c -> n r s c", r=SR)
            for k, part in enumerate((0, 0, 0, 1, 1, 2)):
                sp.dma_start(w1s[SR * k:SR * (k + 1), :, :], w1v[part]).then_inc(s_w1s, 16)
            b1v = b1_dram.rearrange("n (o s a) c -> n o s (a c)", o=1, s=SEG)
            for part in range(PARTS):
                sp.dma_start(w1s[6 * SR + part:6 * SR + part + 1, :, :], b1v[part]).then_inc(s_w1s, 16)

        def moe_pe(pe):
            with pe.Fori(0, GROUPS // 2) as it:
                for u in range(2):
                    pe.wait_ge(s_fc1[u], nth(it, 16, 16))
                    pe.wait_ge(s_yr, nth(it, 2, u + 1))
                    for n in range(2):
                        for kc in range(2):
                            for j in range(GS):
                                mm = pe.matmul(P[32 * j:32 * j + B, 2 * u + n, 0:HID // 2], y_ring[:, kc, u, B * j:B * (j + 1)],
                                               fc1[:, u, kc, j, n * (HID // 2):(n + 1) * (HID // 2)],
                                               start=(kc == 0), stop=(kc == 1), skip_group_check=True)
                    mm.then_inc(s_hid, 1)
                    pe.wait_ge(s_act, nth(it, 2, u + 1))
                    for c in range(HC):
                        mm = pe.transpose(P[:, 4 + c // 3, (c % 3) * 128:(c % 3 + 1) * 128],
                                          hidden[:, u, c // 3, (c % 3) * 128:(c % 3 + 1) * 128], ident[:, :])
                    mm.then_inc(s_hp, 1)
                    pe.wait_ge(s_ht, nth(it, 2, u + 1))
                    pe.wait_ge(s_fc2[u], nth(it, 32, 32))
                    pe.matmul(P[:, 6 + u, 0:D], slot_sel[:, :], fc2_b[:, u, :],
                              start=True, stop=False, skip_group_check=True)
                    for c in range(HC):
                        for j in range(GS):
                            mm = pe.matmul(P[32 * j:32 * j + B, 6 + u, 0:D], hidden_t[:, u, c, B * j:B * (j + 1)],
                                           fc2[:, u, c, j, :], start=False, stop=(c == HC - 1), skip_group_check=True)
                    mm.then_inc(s_fo, 1)

        def moe_act(act):
            act.wait_ge(s_yt, 2 + 2 * QUADS)
            with act.Fori(0, GROUPS // 2) as it:
                for u in range(2):
                    act.copy(y_ring[:, :, u, :],
                             y_t[:, :, ds(it * 2 * GS + u * GS, GS), :].rearrange("p k s b -> p k (s b)")).then_inc(s_yr, 1)
                    act.wait_ge(s_hid, nth(it, 2, u + 1))
                    act.activation(hidden[:, u, :, :], P[:, 2 * u:2 * u + 2, 0:HID // 2], ACT.Gelu).then_inc(s_act, 1)

        def moe_dve(dve):
            with dve.Fori(0, GROUPS // 2) as it:
                for u in range(2):
                    dve.wait_ge(s_hp, nth(it, 2, u + 1))
                    dve.tensor_copy(hidden_t[:, u, :, :].rearrange("p (a c) s -> p a (c s)", a=2),
                                    P[:, 4:6, 0:3 * 128]).then_inc(s_ht, 1)
                    dve.wait_ge(s_fo, nth(it, 2, u + 1))
                    dve.wait_ge(s_yd[u], nth(it, 16, 16))
                    dve.tensor_copy(y_out[:, u, :], P[:, 6 + u, 0:D]).then_inc(s_yo, 1)

        def split_pool(pool):
            def parts(rows, cols, out, base):
                src, left = split_in[0:rows, 0:cols], split_left[0:rows, 0:cols]
                pool.tensor_copy(out[:, 0, :], src).then_inc(s_split, 1)
                pool.wait_ge(s_split, base + 1)
                pool.tensor_tensor(left, src, out[:, 0, :], ALU.subtract).then_inc(s_split, 1)
                pool.wait_ge(s_split, base + 2)
                pool.tensor_copy(out[:, 1, :], left).then_inc(s_split, 1)
                pool.wait_ge(s_split, base + 3)
                pool.tensor_tensor(out[:, 2, :], left, out[:, 1, :], ALU.subtract).then_inc(s_split, 1)
                pool.wait_ge(s_split, base + 4)

            pool.wait_ge(s_yt, 2 + 2 * QUADS)
            for n in range(4):
                pool.dma_start(split_in[:, :], io["w1"][:, n * 512:(n + 1) * 512]).then_inc(s_split_in, 16)
                pool.wait_ge(s_split_in, 16 * (n + 1))
                parts(128, 512, split_out[:, :, :], 4 * n)
                pool.dma_start(w1_dram.rearrange("n p c -> p n c")[:, :, n * 512:(n + 1) * 512],
                               split_out[:, :, :]).then_inc(s_split_out, 16)
                pool.wait_ge(s_split_out, 16 * (n + 1))
            pool.dma_start(split_in[:, 0:128], io["b1"]).then_inc(s_split_in, 16)
            pool.wait_ge(s_split_in, 16 * 5)
            parts(128, 128, split_out[:, :, 0:128], 16)
            pool.dma_start(b1_dram.rearrange("n p c -> p n c"), split_out[:, :, 0:128]).then_inc(s_split_out, 16)
            pool.wait_ge(s_split_out, 16 * 5)
            pool.dma_start(split_in[:, :], io["b2"]).then_inc(s_split_in, 16)
            pool.wait_ge(s_split_in, 16 * 6)
            parts(128, 512, b2s[:, :, :, :].rearrange("p n s r -> p n (s r)"), 20)
            for n in range(2):
                pool.dma_start(split_in[0:PARTS * 32, :], io["gate_sel"][:, n]).then_inc(s_split_in, 16)
                pool.wait_ge(s_split_in, 16 * (7 + n))
                pool.tensor_copy(gate_sel[:, 4 * n:4 * n + 4, :].rearrange("p c m -> p (c m)"),
                                 split_in[0:PARTS * 32, :]).then_inc(s_split, 1)
                pool.wait_ge(s_split, 25 + n)

        MIX = NH * (HD + 1)

        def steps(eng, step):
            step(0, True, False)
            with eng.Fori(1, QUADS - 1) as it:
                step(it, False, False)
            step(QUADS - 1, False, True)

        def l1_pe(pe):
            def combine(quad, j):
                pe.wait_ge(s_cr, nth(quad, 1, 1))
                pe.matmul(P[0:ROWS, 2 + j % 2, MIX:MIX + D], comb_r[:, j, :],
                          y2[:, ds(quad * QP + j, 1), :].rearrange("p a d -> p (a d)"),
                          start=True, stop=True, skip_group_check=True).then_inc(s_mix, 1)

            def turn_x3(quad):
                for j in range(QP):
                    pe.wait_ge(LO["h_out"], nth(quad, QP, j + 1))
                    for kc in range(2):
                        at = ((j % 2) * 2 + kc) * 128
                        mm = pe.transpose(P[0:FH, 4 + j // 2, at:at + ROWS], h_out[0:ROWS, j, kc * FH:(kc + 1) * FH],
                                          ident[0:ROWS, 0:ROWS])
                    if j % 2:
                        mm.then_inc(LO["h_turned"], 1)

            def step(it, first, last):
                if not first:
                    pe.wait_ge(LO["resid"], nth(it, QP, 0))
                pe_qk(pe, L1, it, (1,), w_q1, w_k1)
                pe_v(pe, L1, it, 2, w_v1)

                def x3_taken():
                    pe.wait_ge(LO["h_t"], nth(it, QP, QP))
                pe_attention(pe, L1, it, 2, k_heads1, None if first else lambda: turn_x3(it - 1), x3_taken,
                             None if last else lambda j: combine(it + 1, j))
                if not last:
                    pe_turn(pe, L1, it + 1, h_in, L0["h_out"], QP, QUADS)
                pe_turn_rows(pe, it, attn, L1["mapped"], s_at, 6)
                if not last:
                    pe_qk(pe, L1, it + 1, (0,), w_q1, w_k1)
                for j in range(QP):
                    pe.wait_ge(s_att, nth(it, 2, j // 2 + 1))
                    for kc in range(2):
                        mm = pe.matmul(P[0:ROWS, 4 + j // 2, (j % 2) * D:(j % 2 + 1) * D], tok_t[:, j, kc, :], w_o1[:, kc, :],
                                       start=(kc == 0), stop=(kc == 1), skip_group_check=True)
                    if j % 2:
                        mm.then_inc(s_wo, 1)

            pe.wait_ge(s_late, 64)
            pe.wait_ge(s_y2, 32)
            for j in range(QP):
                if j >= 2:
                    pe.wait_ge(L0["resid"], QP * QUADS + j - 1)
                combine(0, j)
            pe_turn(pe, L1, 0, h_in, L0["h_out"], QP, QUADS)
            pe_qk(pe, L1, 0, (0,), w_q1, w_k1)
            steps(pe, step)
            turn_x3(QUADS - 1)

        def l1_dve(dve):
            def combined(quad, j):
                dve.wait_ge(s_mix, nth(quad, QP, j + 1))
                dve.tensor_tensor(xn[0:ROWS, j:j + 1, :], P[0:ROWS, 2 + j % 2, MIX:MIX + D].unsqueeze(1),
                                  h1_all[0:ROWS, ds(quad * QP + j, 1), :], ALU.add).then_inc(L0["resid"], 1)

            def start(quad):
                take_turned(dve, dve.tensor_copy, L1, quad, 1, h_t)
                dve_k(dve, L1, quad, 2, (0,), None, k_heads1)

            def step(it, first, last):
                dve_k(dve, L1, it, 2, (1,), None, k_heads1)
                if not first:
                    ln_scale(dve, LO, it - 1, attn, h_out)
                def with_bias():
                    if not first:
                        dve.wait_ge(s_h3, it)
                    dve.tensor_tensor(h_out[0:ROWS, :, :], h_in[0:ROWS, :, :], spread(rowc[0:ROWS, 4, :], 1, QP),
                                      ALU.add).then_inc(s_hb, 1)
                between = {1: lambda: dve_v(dve, L1, it, 2, False), 7: with_bias}
                if not first:
                    between[0] = lambda: take_x3(dve, dve.tensor_copy, it - 1, 1)
                if not last:
                    def scale():
                        dve.wait_ge(s_hb, nth(it, 1, 1))
                        ln_scale(dve, L0, it + (QUADS + 1), xn, h_in)
                    between.update({k + 2: lambda k=k: combined(it + 1, k) for k in range(QP)})
                    between[6] = lambda: ln_moments(dve, L0, it + (QUADS + 1), xn)
                    between[8] = scale
                dve_attention(dve, L1, it, 2, between)
                if not last:
                    start(it + 1)
                dve.wait_ge(s_hb, nth(it, 1, 1))
                for g in range(2):
                    dve.wait_ge(s_wo, nth(it, 2, g + 1))
                    dve.tensor_tensor(attn[0:ROWS, 2 * g:2 * g + 2, :], P[0:ROWS, 4 + g, 0:2 * D].rearrange("p (j d) -> p j d", j=2),
                                      h_out[0:ROWS, 2 * g:2 * g + 2, :], ALU.add).then_inc(LO["resid"], 2)
                ln_moments(dve, LO, it, attn)

            dve.wait_ge(s_lam, 1)
            for j in range(QP):
                combined(0, j)
            ln_moments(dve, L0, QUADS, xn)
            ln_scale(dve, L0, QUADS, xn, h_in)
            start(0)
            steps(dve, step)
            ln_scale(dve, LO, QUADS - 1, attn, h_out)
            take_x3(dve, dve.tensor_copy, QUADS - 1, 1)

        def take_x3(eng, copy, quad, g):
            eng.wait_ge(LO["h_turned"], nth(quad, 2, g + 1))
            src = P[0:FH, 4 + g, :].rearrange("p (j k e r) -> p j k e r", j=2, k=2, e=2)
            for j in range(2):
                copy(x3_t[:, :, ds(quad * QB + (4 * g + 2 * j), 2), :], src[:, j, :, :, 0:T]).then_inc(LO["h_t"], 1)

        def l1_act(act):
            def step(it, first, last):
                act_q(act, L1, it, 2, (1,), None, k_heads1)
                act_attention(act, L1, it, 2, None if first else lambda: take_x3(act, act.copy, it - 1, 0))
                if not last:
                    take_turned(act, act.copy, L1, it + 1, 0, h_t)
                take_rows(act, it, s_at, s_att, 6)
                if not last:
                    act_q(act, L1, it + 1, 2, (0,), None, k_heads1)

            act.activation(lam[:, :], lam[:, :], ACT.Exp).then_inc(s_lam, 1)
            take_turned(act, act.copy, L1, 0, 0, h_t)
            act_q(act, L1, 0, 2, (0,), None, k_heads1)
            steps(act, step)
            take_x3(act, act.copy, QUADS - 1, 0)

        def l1_pool(pool):
            def stage(quad):
                pool.tensor_copy(comb_r[:, :, :], combine_all[:, ds(quad * QP, QP), :]).then_inc(s_cr, 1)

            def step(it, first, last):
                if not last:
                    pool.wait_ge(s_mix, nth(it, QP, QP))
                    stage(it + 1)
                    pool_rstd(pool, L0, it + (QUADS + 1))
                pool_rstd(pool, LO, it)
                pool.wait_ge(LO["h_out"], nth(it, QP, QP))
                pool.tensor_tensor(h3_all[0:ROWS, ds(it * QP, QP), :], h_out[0:ROWS, :, :],
                                   spread(rowc[0:ROWS, 5, :], 1, QP), ALU.add).then_inc(s_h3, 1)

            pool.wait_ge(s_ct, QUADS)
            stage(0)
            pool_rstd(pool, L0, QUADS)
            steps(pool, step)


        def prep_pe(pe):
            pe.wait_ge(s_small, SMALL)
            pe.matmul(P[0:FH, 0, 0:FH], m_u[:, :], m_v[:, :], start=True, stop=True).then_inc(s_prep_pe, 1)
            for kc in range(2):
                pe.matmul(P[0:FH, 1, kc * D:(kc + 1) * D], v_k_t[:, kc * FH:(kc + 1) * FH], u_k[:, :], start=True, stop=True)
                mm = pe.matmul(P[0:FH, 6, kc * D:(kc + 1) * D], v_v_t[:, kc * FH:(kc + 1) * FH], u_v[:, :], start=True, stop=True)
            mm.then_inc(s_prep_pe, 1)
            pe.wait_ge(s_prep_dve, 1)
            for hc in range(2):
                pe.matmul(P[0:R0, 7, hc * FH:(hc + 1) * FH], u_q_t[:, hc, :], mixer[:, :], start=True, stop=True)
            pe.matmul(P[0:FH, 0, 256:258], mixer[:, :], bias_qk[:, 0, :], start=True, stop=True).then_inc(s_prep_pe, 1)
            pe.wait_ge(s_prep_dve, 2)
            for kc in range(2):
                mm = pe.matmul(P[0:FH, 4, kc * D:(kc + 1) * D], v_q_t[:, kc * FH:(kc + 1) * FH], u_qm[:, :], start=True, stop=True)
            mm.then_inc(s_prep_pe, 1)
            pe.wait_ge(s_slot_dir, 1)
            for kc in range(2):
                mm = pe.transpose(P[0:FH, 5, kc * SLOTS:(kc + 1) * SLOTS], slot_dir[:, kc * FH:(kc + 1) * FH],
                                  ident[0:SLOTS, 0:SLOTS])
            mm.then_inc(s_prep_pe, 1)

        def prep_dve(dve):
            dve.memset(P[:, :, :], 0.0).then_inc(s_psum0, 1)
            dve.memset(negh[:, :], -0.5).then_inc(s_consts, 1)
            dve.memset(v_blk[:, :, :, :], 0.0).then_inc(s_vz, 1)
            dve.memset(cw[:, :, :], 0.0).then_inc(s_consts, 1)
            dve.memset(probs[:, :, :, :, :], 0.0).then_inc(s_consts, 1)
            dve.memset(y_t[FH:FH + 1, :, :, :], 1.0).then_inc(s_consts, 1)
            dve.wait_ge(s_vz, 1)
            dve.memset(v_blk[0:T, :, :, HD:HD + 1], 1.0).then_inc(s_consts, 1)
            dve.memset(v_blk[64:64 + T, :, :, 2 * HD + 1:2 * HD + 2], 1.0).then_inc(s_consts, 1)
            dve.wait_ge(s_small, SMALL)
            dve.tensor_tensor(embed_add[:, :], rowc[:, 0, :], rowc[:, 1, :], ALU.add).then_inc(s_prep_misc, 1)
            dve.tensor_tensor(bias_km[:, :, :], spread(bias_qk[:, 1, :], 2, HH), spread(hmask[:, :], 1, 2),
                              ALU.mult).then_inc(s_prep_misc, 1)
            dve.wait_ge(s_prep_pe, 1)
            dve.tensor_tensor(mixer[:, :], P[0:FH, 0, 0:FH], bmask[:, :], ALU.mult).then_inc(s_prep_dve, 1)
            dve.tensor_tensor_reduce(slot_dir[:, :], slots[:, :], slots[:, :], 1.0, 0.0, ALU.mult, ALU.add,
                                     slot_n[:, 0:1]).then_inc(s_slot_sum, 1)
            dve.wait_ge(s_prep_pe, 3)
            dve.tensor_copy(bias_qm[:, :], P[0:FH, 0, 256:258]).then_inc(s_prep_misc, 1)
            dve.tensor_copy(u_qm[:, :], P[0:R0, 7, 0:D]).then_inc(s_prep_dve, 1)
            dve.tensor_copy(w_k0[:, :, :], P[0:FH, 1, 0:2 * D].rearrange("p (k d) -> p k d", k=2)).then_inc(s_prep_misc, 1)
            dve.tensor_copy(w_v0[:, :, :], P[0:FH, 6, 0:2 * D].rearrange("p (k d) -> p k d", k=2)).then_inc(s_prep_misc, 1)
            dve.wait_ge(s_prep_pe, 4)
            dve.tensor_copy(w_q0[:, :, :], P[0:FH, 4, 0:2 * D].rearrange("p (k d) -> p k d", k=2)).then_inc(s_prep_misc, 1)
            dve.wait_ge(s_prep_pool, 2)
            dve.tensor_tensor(slot_n[:, 3:4], slot_n[:, 2:3], slot_scale[:, :], ALU.mult).then_inc(s_slot_sum, 1)
            dve.wait_ge(s_slot_sum, 2)
            dve.tensor_scalar(slot_dir[:, :], slots[:, :], slot_n[:, 3:4], None, ALU.mult).then_inc(s_slot_dir, 1)
            dve.wait_ge(s_prep_pe, 5)
            dve.tensor_copy(slots_t[:, :, :], P[0:FH, 5, 0:2 * SLOTS].rearrange("p (k s) -> p k s", k=2)).then_inc(s_prep_misc, 1)

        PREP_MISC = 7

        def prep_pool(pool):
            pool.wait_ge(s_slot_sum, 1)
            pool.wait_ge(s_consts, 6)
            pool.tensor_scalar(slot_n[:, 1:2], slot_n[:, 0:1], TINY, None, ALU.max).then_inc(s_prep_pool, 1)
            pool.wait_ge(s_prep_pool, 1)
            pool.tensor_tensor(slot_n[:, 2:3], slot_n[:, 1:2], negh[0:SLOTS, 0:1], ALU.pow).then_inc(s_prep_pool, 1)

        def l0_steps(eng, step):
            with eng.Fori(0, QUADS - 1) as it:
                step(it, False)
            step(QUADS - 1, True)

        def embed(pe, quad):
            pe.wait_ge(s_patches, nth(quad, 16, 16))
            for j in range(QP):
                for e in range(2):
                    for c in range(PC):
                        mm = pe.matmul(P[64 * e:64 * e + T, 2 + j // 2, (j % 2) * D:(j % 2 + 1) * D],
                                       patches[:, c, 2 * j + e, :], w_patch[:, c, :],
                                       start=(c == 0), stop=(c == PC - 1), skip_group_check=True)
                mm.then_inc(s_emb, 1)

        def l0_pe(pe):
            pe.wait_ge(s_prep_misc, PREP_MISC)
            pe.wait_ge(s_consts, 6)

            def start(quad):
                pe_turn(pe, L0, quad, h_in, s_hin, QP)
                pe_qk(pe, L0, quad, (0,), w_q0, w_k0)

            def step(it, last):
                def slot_inputs_taken():
                    pe.wait_ge(s_yt, nth(it, 2, 2))
                pe_attention(pe, L0, it, 1, k_heads0, before_turn=slot_inputs_taken)
                if not last:
                    pe.wait_ge(L0["normed"], nth(it, QP, QP))
                    embed(pe, it + 1)
                pe_turn_rows(pe, it, tok, s_tok, s_tokp, 4)
                for j in range(QP):
                    pe.wait_ge(s_tokt, nth(it, 2, j // 2 + 1))
                    for kc in range(2):
                        mm = pe.matmul(P[0:ROWS, 6, j * SLOTS:(j + 1) * SLOTS], tok_t[:, j, kc, :], slots_t[:, kc, :],
                                       start=(kc == 0), stop=(kc == 1), skip_group_check=True)
                mm.then_inc(s_lg, 1)
                for j in range(QP):
                    for e in range(2):
                        for kc in range(2):
                            mm = pe.matmul(P[64 * e:64 * e + SLOTS, 7, j * T:(j + 1) * T], slots_t[:, kc, :],
                                           tok_t[:, j, kc, 64 * e:64 * e + T],
                                           start=(kc == 0), stop=(kc == 1), skip_group_check=True)
                mm.then_inc(s_lt, 1)
                if not last:
                    start(it + 1)
                settle(pe, s_cd, nth(it, 11, 11))
                for j in range(QP):
                    for e in range(2):
                        r = slice(64 * e, 64 * e + SLOTS)
                        mm = pe.matmul(P[64 * e:64 * e + T, 4, j * SLOTS:(j + 1) * SLOTS], dw[r, j, :], ident[r, r],
                                       start=True, stop=True, skip_group_check=True)
                mm.then_inc(s_dp, 1)
                for j in range(QP):
                    mm = pe.transpose(P[:, 5, j * ROWS:(j + 1) * ROWS], cw[0:ROWS, j, :], ident[0:ROWS, 0:ROWS])
                mm.then_inc(s_cp, 1)
                if not last:
                    pe_v(pe, L0, it + 1, 1, w_v0)
                    pe.wait_ge(L0["k_ready_a"], nth(it, HH, 2 * HH))
                    pe.wait_ge(L0["k_ready_v"], nth(it, HH, 2 * HH))
                pe.wait_ge(s_dt, nth(it, 1, 1))
                pe.wait_ge(s_ct, nth(it, 1, 1))
                for kc in range(2):
                    for e, j in [(e, j) for e in range(2) for j in range(QP)]:
                        mm = pe.matmul(P[0:FH, 2 + kc + 2 * e, j * SLOTS:(j + 1) * SLOTS],
                                       xn[64 * e:64 * e + T, j, kc * FH:(kc + 1) * FH], disp[64 * e:64 * e + T, j, :],
                                       start=True, stop=True, skip_group_check=True)
                    mm.then_inc(s_y, 1)

            start(0)
            pe_v(pe, L0, 0, 1, w_v0)
            l0_steps(pe, step)

        def take_y(copy, it, kc):
            dst = y_t[0:FH, kc, :, ds(it * QB, QB)].rearrange("p s (j e) -> p e j s", e=2)
            for e in range(2):
                ins = copy(dst[:, e], P[0:FH, 2 + kc + 2 * e, 0:QP * SLOTS].rearrange("p (j s) -> p j s", j=QP))
            ins.then_inc(s_yt, 1)

        def l0_dve(dve):
            dve.wait_ge(s_prep_misc, PREP_MISC)

            def embedded(quad):
                for g in range(2):
                    dve.wait_ge(s_emb, nth(quad, QP, 2 * g + 2))
                    dve.tensor_tensor(h_in[0:ROWS, 2 * g:2 * g + 2, :],
                                      P[0:ROWS, 2 + g, 0:2 * D].rearrange("p (j d) -> p j d", j=2),
                                      spread(embed_add[0:ROWS, :], 1, 2), ALU.add).then_inc(s_hin, 2)

            def step(it, last):
                dve_attention(dve, L0, it, 1)
                for j in range(QP):
                    dve.wait_ge(L0["normed"], nth(it, QP, j + 1))
                    dve.tensor_tensor(attn[0:ROWS, j, :], attn[0:ROWS, j, :], h_in[0:ROWS, j, :],
                                      ALU.add).then_inc(L0["resid"], 1)
                dve_ln(dve, L0, it, attn, h_out)
                for j in range(QP):
                    dve.wait_ge(L0["h_out"], nth(it, QP, j + 1))
                    dve.tensor_tensor_reduce(sq[0:ROWS, j, :], h_out[0:ROWS, j, :], h_out[0:ROWS, j, :], 1.0, 0.0,
                                             ALU.mult, ALU.add, norms[0:ROWS, 0, j:j + 1]).then_inc(s_ssq, 1)
                dve.wait_ge(s_rr, nth(it, 1, 1))
                for j in range(QP):
                    dve.scalar_tensor_tensor(xn[0:ROWS, j, :], h_out[0:ROWS, j, :], norms[0:ROWS, 2, j:j + 1],
                                             rowc[0:ROWS, 2, :], ALU.mult, ALU.mult).then_inc(s_xn, 1)
                for j in range(QP):
                    dve.wait_ge(s_xn, nth(it, QP, j + 1))
                    dve.tensor_tensor_reduce(sq[0:ROWS, j, :], xn[0:ROWS, j, :], xn[0:ROWS, j, :], 1.0, 0.0,
                                             ALU.mult, ALU.add, norms[0:ROWS, 3, j:j + 1]).then_inc(s_n2, 1)
                dve.wait_ge(s_tn, nth(it, 1, 1))
                for j in range(QP):
                    dve.tensor_scalar(tok[0:ROWS, j, :], xn[0:ROWS, j, :], small[0:ROWS, 1, j:j + 1], None,
                                      ALU.mult).then_inc(s_tok, 1)
                if not last:
                    embedded(it + 1)
                lg = P[0:ROWS, 6, 0:QP * SLOTS].rearrange("p (j s) -> p j s", j=QP)
                lt = P[:, 7, 0:QP * T].rearrange("p (j t) -> p j t", j=QP)
                dve.wait_ge(s_lg, nth(it, 1, 1))
                dve.tensor_reduce(rmx[0:ROWS, 0, :], lg, AX, ALU.max).then_inc(s_cd, 1)
                dve.wait_ge(s_lt, nth(it, 1, 1))
                dve.tensor_reduce(rmx[:, 3, :], lt, AX, ALU.max).then_inc(s_cd, 1)
                dve.wait_ge(s_cd, nth(it, 11, 1))
                dve.tensor_tensor(cw2[0:ROWS, :, :], lg, spread(rmx[0:ROWS, 0, :], 2, SLOTS), ALU.subtract).then_inc(s_cd, 1)
                dve.wait_ge(s_cd, nth(it, 11, 2))
                dve.tensor_tensor(dw2[:, :, :], lt, spread(rmx[:, 3, :], 2, T), ALU.subtract).then_inc(s_cd, 1)
                if not last:
                    take_turned(dve, dve.tensor_copy, L0, it + 1, 1, h_t)
                dve.wait_ge(s_ce, nth(it, 2, 1))
                dve.tensor_reduce(rmx[0:ROWS, 1, :], ce[0:ROWS, :, :], AX, ALU.add).then_inc(s_cd, 1)
                dve.wait_ge(s_ce, nth(it, 2, 2))
                dve.tensor_reduce(rmx[:, 4, :], de[:, :, :], AX, ALU.add).then_inc(s_cd, 1)
                dve.wait_ge(s_cd, nth(it, 11, 5))
                dve.reciprocal(rmx[0:ROWS, 2, :], rmx[0:ROWS, 1, :]).then_inc(s_cd, 1)
                dve.wait_ge(s_cd, nth(it, 11, 6))
                dve.reciprocal(rmx[:, 5, :], rmx[:, 4, :]).then_inc(s_cd, 1)
                dve.wait_ge(s_cd, nth(it, 11, 7))
                for e in range(2):
                    r = slice(64 * e, 64 * e + T)
                    dve.tensor_tensor(cw[r, :, e * SLOTS:(e + 1) * SLOTS], ce[r, :, :], spread(rmx[r, 2, :], 2, SLOTS),
                                      ALU.mult).then_inc(s_cd, 1)
                dve.wait_ge(s_cd, nth(it, 11, 8))
                dve.tensor_tensor(dw[:, :, :], de[:, :, :], spread(rmx[:, 5, :], 2, T), ALU.mult).then_inc(s_cd, 1)
                if not last:
                    dve_k(dve, L0, it + 1, 1, (0,), bias_km, k_heads0)
                dve.wait_ge(s_dp, nth(it, 1, 1))
                dve.tensor_copy(disp[0:ROWS, :, :], P[0:ROWS, 4, 0:QP * SLOTS].rearrange("p (j s) -> p j s", j=QP)).then_inc(s_dt, 1)
                if not last:
                    dve_v(dve, L0, it + 1, 1, True)
                dve.wait_ge(s_y, nth(it, 2, 1))
                take_y(dve.tensor_copy, it, 0)

            embedded(0)
            take_turned(dve, dve.tensor_copy, L0, 0, 1, h_t)
            dve_k(dve, L0, 0, 1, (0,), bias_km, k_heads0)
            dve_v(dve, L0, 0, 1, True)
            l0_steps(dve, step)

        def l0_act(act):
            act.wait_ge(s_prep_misc, PREP_MISC)
            act.wait_ge(s_consts, 6)

            def step(it, last):
                act_attention(act, L0, it, 1)
                take_rows(act, it, s_tokp, s_tokt, 4)
                act.wait_ge(s_cd, nth(it, 11, 3))
                act.activation(ce[0:ROWS, :, :], cw2[0:ROWS, :, :], ACT.Exp).then_inc(s_ce, 1)
                act.wait_ge(s_cd, nth(it, 11, 4))
                act.activation(de[:, :, :], dw2[:, :, :], ACT.Exp).then_inc(s_ce, 1)
                if not last:
                    take_turned(act, act.copy, L0, it + 1, 0, h_t)
                if not last:
                    act_q(act, L0, it + 1, 1, (0,), bias_qm, k_heads0)
                act.wait_ge(s_cp, nth(it, 1, 1))
                act.copy(combine_all[:, ds(it * QP, QP), :],
                         P[:, 5, 0:QP * ROWS].rearrange("p (j t) -> p j t", j=QP)).then_inc(s_ct, 1)
                act.wait_ge(s_y, nth(it, 2, 2))
                take_y(act.copy, it, 1)

            take_turned(act, act.copy, L0, 0, 0, h_t)
            act_q(act, L0, 0, 1, (0,), bias_qm, k_heads0)
            l0_steps(act, step)

        def l0_pool(pool):
            with pool.Fori(0, QUADS) as it:
                pool_rstd(pool, L0, it)
                settle(pool, s_ssq, nth(it, QP, QP))
                pool.tensor_scalar(norms[0:ROWS, 1, :], norms[0:ROWS, 0, :], 1.0 / D, EPS, ALU.mult, ALU.add).then_inc(s_ms, 1)
                pool.wait_ge(s_ms, nth(it, 2, 1))
                pool.tensor_tensor(norms[0:ROWS, 2, :], norms[0:ROWS, 1, :], negh[0:ROWS, :], ALU.pow).then_inc(s_rr, 1)
                settle(pool, s_n2, nth(it, QP, QP))
                pool.tensor_scalar(small[0:ROWS, 0, :], norms[0:ROWS, 3, :], TINY, None, ALU.max).then_inc(s_ms, 1)
                pool.wait_ge(s_ms, nth(it, 2, 2))
                pool.tensor_tensor(small[0:ROWS, 1, :], small[0:ROWS, 0, :], negh[0:ROWS, :], ALU.pow).then_inc(s_tn, 1)
                pool.wait_ge(L0["h_out"], nth(it, QP, QP))
                pool.tensor_copy(h1_all[0:ROWS, ds(it * QP, QP), :], h_out[0:ROWS, :, :]).then_inc(s_keep, 1)

        def l0_sync(sp):
            sp.dma_start(w_patch[:, :, :], io["w_patch"]).then_inc(s_wpatch, 16)
            sp.dma_start(patches[:, :, :, :], io["patches"][0]).then_inc(s_patches, 16)
            sp.sem_inc(s_yt, 2)
            sp.sem_inc(LO["h_t"], QP)
            sp.sem_inc(s_ot, 1)
            sp.sem_inc(s_ac, 2)
            for u in range(2):
                sp.sem_inc(s_yd[u], 16)
            for dst, name in SMALL_LOADS:
                sp.dma_start(dst[:], io[name]).then_inc(s_small, 16)
            moe_sync_first(sp)
            with sp.Fori(1, QUADS) as it:
                sp.wait_ge(s_emb, it * QP)
                sp.dma_start(patches[:, :, :, :], io["patches"][it]).then_inc(s_patches, 16)

        CHUNKS = [(n * TC, min(TC, TOK - n * TC)) for n in range(3)]
        SPLIT = 4
        UNITS = [(sq, hh, c, j) for sq in range(2) for hh in range(2) for c in range(CH // 2) for j in range(4)]
        NU = len(UNITS)
        AHEAD = 2
        STACKED = 16 * 4 * PARTS
        PRODUCTS = [(0, 0), (0, 1), (1, 0), (0, 2), (1, 1), (2, 0)]

        def mlp_sync(sp):
            sp.wait_ge(LO["h_t"], QP + QP * QUADS)
            sp.wait_ge(s_h3, QUADS)
            sp.dma_start(w2[:, :, :, :], io["w2"]).then_inc(s_w2, 16)
            sp.wait_ge(s_zp, SPLIT)
            sp.dma_start(z_dram.rearrange("n p t -> p n t"), z_parts[:, :, :]).then_inc(s_zd, 16)
            sp.wait_ge(s_zd, 16)
            zv = z_dram.rearrange("n (s r) t -> n r s t", r=SR)
            for k, part in enumerate((0, 1, 2, 0, 1, 0)):
                sp.dma_start(zs[SR * k:SR * (k + 1), :, :], zv[part]).then_inc(s_zs, 16)
            for n in range(3):
                if n:
                    sp.wait_ge(s_ws, n * STACKED)
                tiles = -(-(n + 1) * TC // 128)
                sp.wait_ge(s_g1, tiles)
                sp.wait_ge(s_g2, tiles)
                for part in range(PARTS):
                    for q in range(4):
                        dst = ws[32 * part:32 * (part + 1), :, n * TC:(n + 1) * TC]
                        sp.dma_start(dst.rearrange("p (s q) t -> p q s t", q=4)[:, q],
                                     gate_parts[32 * q:32 * (q + 1), part, :, n * TC:(n + 1) * TC]).then_inc(s_ws, 16)

        def tile_pairs(eng, step):
            with eng.Fori(0, TT // 2 - 1) as it:
                step(it, False)
            step(TT // 2 - 1, True)

        def mlp_pe(pe):
            pe.wait_ge(LO["h_t"], QP + QP * QUADS)
            pe.wait_ge(s_late2, 16 * 4)
            for n, (at, cols) in enumerate(CHUNKS):
                for kc in range(2):
                    mm = pe.matmul(P[:, n, 0:cols], z_proj[:, kc, :],
                                   x3_t[:, kc, :, :].rearrange("p b t -> p (b t)")[:, at:at + cols],
                                   start=(kc == 0), stop=(kc == 1))
                mm.then_inc(s_z, 1)
            def scores(pair):
                for u in range(2):
                    pe.wait_ge(s_zt, nth(pair, 2, u + 1))
                    pe.matmul(P[:, 4 + u, :], z_tile[:, u, :], score_w[:, :], start=True, stop=True).then_inc(s_sc, 1)

            def step(it, last):
                if not last:
                    pe.wait_ge(s_sr, nth(it, 2, 2))
                    scores(it + 1)
                for u in range(2):
                    pe.wait_ge(s_gate, nth(it, 2, u + 1))
                    for sg in range(4):
                        mm = pe.transpose(P[:, 6 + u, sg * 128:(sg + 1) * 128], gate[:, u, sg * 128:(sg + 1) * 128],
                                          ident[:, :])
                    mm.then_inc(s_gt, 1)

            scores(0)
            tile_pairs(pe, step)
            pe.wait_ge(s_zs, 16 * 6)
            pe.wait_ge(s_w1s, 16 * 9)
            pe.wait_ge(s_set, 1)
            pe.wait_ge(s_split, 26)
            pe.wait_ge(s_w2, 16)
            with pe.Fori(0, 3) as it:
                pe.wait_ge(s_ws, nth(it, STACKED, STACKED))

                def hidden_rows(n):
                    sq, hh, c, j = UNITS[n]
                    seg, i = 4 * sq + j, hh * (CH // 2) + c
                    if n == 0:
                        pe.wait_ge(s_ot, nth(it, 1, 1))
                    if n >= 3:
                        pe.wait_ge(s_ua, nth(it, NU, n - 2))
                    pe.matmul(P[:, n % 3, 0:TC], w1s[:, seg, i * 128:(i + 1) * 128], zs[:, seg, ds(it * TC, TC)],
                              start=True, stop=True).then_inc(s_u1, 1)

                def gate_rows(n):
                    sq, hh, c, j = UNITS[n]
                    seg = 4 * sq + j
                    if n >= 3:
                        pe.wait_ge(s_ug, nth(it, NU, n - 2))
                    pe.matmul(P[:, 3 + n % 3, 0:TC], gate_sel[:, c, :], ws[:, 2 * seg + hh, ds(it * TC, TC)],
                              start=True, stop=True).then_inc(s_bc, 1)

                def last_bias(sq):
                    pe.wait_ge(s_ac, nth(it, 2, sq + 1))
                    for sg in (2 * sq, 2 * sq + 1):
                        for k, (g, b) in enumerate(PRODUCTS):
                            pe.matmul(P[:, 6 + sq, 0:TC], b2s[:, b, sg, :], gate_parts[:, g, sg, ds(it * TC, TC)],
                                      start=(sg == 2 * sq and k == 0), stop=False, skip_group_check=True)

                def expert_out(n):
                    sq, hh, c, j = UNITS[n]
                    seg, i = 4 * sq + j, hh * (CH // 2) + c
                    pe.wait_ge(s_ug, nth(it, NU, n + 1))
                    pe.matmul(P[32 * j:32 * j + 32, 6 + sq, 0:TC], w2[:, i, seg, :], gated[:, n % 8, :],
                              start=False, stop=(hh == 1 and c == CH // 2 - 1), skip_group_check=True).then_inc(s_u2, 1)

                for k in range(AHEAD):
                    hidden_rows(k)
                for n in range(0, NU + 4, 4):
                    for k in range(n, min(n + 4, NU)):
                        if k + AHEAD < NU:
                            hidden_rows(k + AHEAD)
                        gate_rows(k)
                    if n in (0, NU // 2):
                        last_bias(n // (NU // 2))
                    if n >= 4:
                        for k in range(n - 4, n):
                            expert_out(k)
                pe.wait_ge(s_ac, nth(it, 2, 4))
                for sq in range(2):
                    mm = pe.matmul(P[0:SG, 0, 0:TC], out1_w[:, sq, :], mlp_out[:, sq, :], start=(sq == 0), stop=(sq == 1))
                mm.then_inc(s_o1, 1)

        def mlp_act(act):
            act.wait_ge(LO["h_out"], QP * QUADS)
            for n, (at, cols) in enumerate(CHUNKS):
                act.wait_ge(s_z, n + 1)
                act.copy(z[:, at:at + cols], P[:, n, 0:cols]).then_inc(s_zc, 1)
            act.wait_ge(s_zc, 3)
            act.wait_ge(s_set, 1)

            def stage_tiles(pair):
                for u in range(2):
                    act.copy(z_tile[:, u, :], z[:, ds(pair * 256 + u * 128, 128)]).then_inc(s_zt, 1)

            def take_scores(pair):
                for u in range(2):
                    act.wait_ge(s_sc, nth(pair, 2, u + 1))
                    act.copy(scored[:, u, 0, :, 0:SM], P[:, 4 + u, :].rearrange("p (s m) -> p s m", m=SM)).then_inc(s_sr, 1)

            def step(it, last):
                if not last:
                    stage_tiles(it + 1)
                for u in range(2):
                    act.wait_ge(s_t4, nth(it, 4, 2 * u + 2))
                    act.activation(top_e[:, u, :, :], top_e[:, u, :, :], ACT.Exp).then_inc(s_ge, 1)
                    act.wait_ge(s_sh, nth(it, 2, u + 1))
                    act.activation(gate_e[:, u, :], gate_e[:, u, :], ACT.Exp).then_inc(s_ge, 1)
                if not last:
                    act.wait_ge(s_rp, nth(it, 2, 2))
                    take_scores(it + 1)
                for u in range(2):
                    act.wait_ge(s_gt, nth(it, 2, u + 1))
                    act.copy(gate_parts[:, 0, :, ds(it * 256 + u * 128, 128)],
                             P[:, 6 + u, :].rearrange("p (s t) -> p s t", s=4)).then_inc(s_g0, 1)
                for u in range(2):
                    act.wait_ge(s_gl, nth(it, 2, u + 1))
                    act.copy(gate_parts[:, 1, :, ds(it * 256 + u * 128, 128)],
                             gate_left[:, u, :].rearrange("p (s t) -> p s t", s=4)).then_inc(s_g1, 1)

            stage_tiles(0)
            take_scores(0)
            tile_pairs(act, step)
            act.wait_ge(s_g2, TT)
            with act.Fori(0, 3) as it:
                for n in range(NU):
                    act.wait_ge(s_u1, nth(it, NU, n + 1))
                    if n >= 4:
                        act.wait_ge(s_ug, nth(it, NU, n - 3))
                    act.activation(act_out[:, n % 4, :], P[:, n % 3, 0:TC], ACT.Gelu_apprx_tanh).then_inc(s_ua, 1)
                    if n == NU // 2 + 7:
                        act.wait_ge(s_u2, nth(it, NU, NU // 2))
                        act.copy(mlp_out[:, 0, :], P[:, 6, 0:TC]).then_inc(s_ac, 1)
                act.wait_ge(s_u2, nth(it, NU, NU))
                act.copy(mlp_out[:, 1, :], P[:, 7, 0:TC]).then_inc(s_ac, 1)
                act.wait_ge(s_o1, nth(it, 1, 1))
                act.activation(out_t[:, ds(it * TC, TC)], P[0:SG, 0, 0:TC], ACT.Gelu_apprx_tanh,
                               bias=out1_b[:, 0:1]).then_inc(s_ot, 1)

        def mlp_dve(dve):
            dve.wait_ge(LO["h_out"], QP * QUADS)
            dve.memset(z[:, TOK:TZ], 0.0).then_inc(s_zb, 1)
            dve.wait_ge(LO["h_t"], QP + QP * QUADS)
            dve.wait_ge(s_h3, QUADS)
            for u in range(2):
                dve.memset(scored[:, u, 0, :, SM:SM + SK], LOW).then_inc(s_zb, 1)
                dve.memset(top4[:, u, :, SK:2 * SK], LOW).then_inc(s_zb, 1)
            dve.memset(zs[6 * SR:ZR, :, :], 1.0).then_inc(s_set, 1)
            dve.wait_ge(s_zb, 1)
            dve.wait_ge(s_zc, 3)
            dve.tensor_copy(z_parts[:, 0, :], z[:, 0:TP]).then_inc(s_zp, 1)
            dve.wait_ge(s_zp, 1)
            dve.tensor_tensor(z_left[:, :], z[:, 0:TP], z_parts[:, 0, :], ALU.subtract).then_inc(s_zp, 1)
            dve.wait_ge(s_zp, 2)
            dve.tensor_copy(z_parts[:, 1, :], z_left[:, :]).then_inc(s_zp, 1)
            dve.wait_ge(s_zp, 3)
            dve.tensor_tensor(z_parts[:, 2, :], z_left[:, :], z_parts[:, 1, :], ALU.subtract).then_inc(s_zp, 1)
            dve.wait_ge(s_zb, 5)
            with dve.Fori(0, TT // 2) as it:
                for u in range(2):
                    settle(dve, s_sr, nth(it, 2, u + 1))
                    for s in range(SEG):
                        mx = dve.max(top8[:, u, s, :], scored[:, u, 0, s, 0:SM])
                    mx.then_inc(s_mx, 1)
                    dve.wait_ge(s_mx, nth(it, 2, u + 1))
                    dve.tensor_copy(top4[:, u, :, 0:SK], top8[:, u, :, 0:SK]).then_inc(s_t4, 1)
                    dve.tensor_tensor(top_e[:, u, :, :], top8[:, u, :, 0:SK], top8[:, u, :, 0:1].to_broadcast([128, SEG, SK]),
                                      ALU.subtract).then_inc(s_t4, 1)
                    settle(dve, s_t4, nth(it, 4, 2 * u + 1))
                    for s in range(SEG):
                        rp = dve.match_replace(scored[:, u, 1, s, :], top4[:, u, s, :], scored[:, u, 0, s, :], LOW)
                    rp.then_inc(s_rp, 1)
                for u in range(2):
                    dve.wait_ge(s_ge, nth(it, 4, 2 * u + 1))
                    dve.tensor_reduce(gate_sum[:, u, 0, :], top_e[:, u, :, :], AX, ALU.add).then_inc(s_gs, 1)
                    dve.wait_ge(s_gs, nth(it, 6, 3 * u + 1))
                    dve.reciprocal(gate_sum[:, u, 1, :], gate_sum[:, u, 0, :]).then_inc(s_gs, 1)
                    dve.wait_ge(s_ge, nth(it, 4, 2 * u + 2))
                    dve.wait_ge(s_rp, nth(it, 2, u + 1))
                    g = gate[:, u, :].rearrange("p (s m) -> p s m", m=SM)
                    dve.scalar_tensor_tensor(g, scored[:, u, 1, :, 0:SM], LOW,
                                             gate_e[:, u, :].rearrange("p (s m) -> p s m", m=SM),
                                             ALU.is_equal, ALU.mult).then_inc(s_gs, 1)
                    dve.wait_ge(s_gs, nth(it, 6, 3 * u + 3))
                    dve.tensor_tensor(g, g, spread(gate_sum[:, u, 1, :], 2, SM), ALU.mult).then_inc(s_gate, 1)
                for u in range(2):
                    dve.wait_ge(s_g0, nth(it, 2, u + 1))
                    dve.tensor_tensor(gate_left[:, u, :].rearrange("p (s t) -> p s t", s=4),
                                      P[:, 6 + u, :].rearrange("p (s t) -> p s t", s=4),
                                      gate_parts[:, 0, :, ds(it * 256 + u * 128, 128)], ALU.subtract).then_inc(s_gl, 1)
            with dve.Fori(0, 3) as it:
                for n in range(NU):
                    dve.wait_ge(s_ua, nth(it, NU, n + 1))
                    dve.wait_ge(s_bc, nth(it, NU, n + 1))
                    if n >= 8:
                        dve.wait_ge(s_u2, nth(it, NU, n - 7))
                    dve.tensor_tensor(gated[:, n % 8, :], act_out[:, n % 4, :], P[:, 3 + n % 3, 0:TC],
                                      ALU.mult).then_inc(s_ug, 1)

        def mlp_pool(pool):
            pool.wait_ge(s_zd, 16)
            with pool.Fori(0, TT // 2) as it:
                for u in range(2):
                    pool.wait_ge(s_mx, nth(it, 2, u + 1))
                    pool.tensor_tensor(gate_e[:, u, :].rearrange("p (s m) -> p s m", m=SM), scored[:, u, 0, :, 0:SM],
                                       top8[:, u, :, 0:1].to_broadcast([128, SEG, SM]), ALU.subtract).then_inc(s_sh, 1)
                for u in range(2):
                    pool.wait_ge(s_g1, nth(it, 2, u + 1))
                    at = ds(it * 256 + u * 128, 128)
                    pool.tensor_tensor(gate_parts[:, 2, :, at], gate_left[:, u, :].rearrange("p (s t) -> p s t", s=4),
                                       gate_parts[:, 1, :, at], ALU.subtract).then_inc(s_g2, 1)

        summed, normed = (attn, xn), (h_out, h_in)

        def last_pe(pe):
            for q in range(QUADS):
                if q == 0:
                    pe.wait_ge(s_ot, 4)
                if q >= 2:
                    pe.wait_ge(LO["resid"], QP * (QUADS + q - 1))
                for j in range(QP):
                    for e in range(2):
                        b = q * QB + 2 * j + e
                        mm = pe.matmul(P[64 * e:64 * e + T, 2 + 2 * (q % 2) + j // 2, (j % 2) * D:(j % 2 + 1) * D],
                                       out_t[:, b * T:(b + 1) * T], out2_w[:, :], start=True, stop=True,
                                       skip_group_check=True)
                    if j % 2:
                        mm.then_inc(s_o2, 1)

        def last_dve(dve):
            def residual(q):
                if q >= 2:
                    dve.wait_ge(LO["h_out"], QP * (QUADS + q - 1))
                for g in range(2):
                    dve.wait_ge(s_o2, 2 * q + g + 1)
                    dve.tensor_tensor(summed[q % 2][0:ROWS, 2 * g:2 * g + 2, :],
                                      P[0:ROWS, 2 + 2 * (q % 2) + g, 0:2 * D].rearrange("p (j d) -> p j d", j=2),
                                      h3_all[0:ROWS, q * QP + 2 * g:q * QP + 2 * g + 2, :], ALU.add).then_inc(LO["resid"], 2)

            residual(0)
            ln_moments(dve, LO, QUADS, summed[0])
            for q in range(QUADS):
                if q + 1 < QUADS:
                    residual(q + 1)
                if q >= 2:
                    dve.wait_ge(s_out[q % 2], 32 * (q // 2))
                ln_scale(dve, LO, QUADS + q, summed[q % 2], normed[q % 2])
                if q + 1 < QUADS:
                    ln_moments(dve, LO, QUADS + q + 1, summed[(q + 1) % 2])

        def last_pool(pool):
            for q in range(QUADS):
                pool_rstd(pool, LO, QUADS + q)

        def last_sync(sp):
            out = io["out"].rearrange("(q j e) t d -> q e t j d", j=QP, e=2)
            for q in range(QUADS):
                sp.wait_ge(LO["h_out"], QP * (QUADS + q + 1))
                for e in range(2):
                    sp.dma_start(out[q, e], normed[q % 2][64 * e:64 * e + T, :, :]).then_inc(s_out[q % 2], 16)
            for u in range(2):
                sp.wait_ge(s_out[u], 32 * (QUADS // 2))


        block = ctx.enter_context(nc.Block())
        @block.sync
        def _(sp):
            l0_sync(sp)
            moe_sync(sp)
            mlp_sync(sp)
            last_sync(sp)

        @block.tensor
        def _(pe):
            pe.wait_ge(s_wpatch, 16)
            pe.wait_ge(s_psum0, 1)
            embed(pe, 0)
            prep_pe(pe)
            l0_pe(pe)
            moe_pe(pe)
            l1_pe(pe)
            mlp_pe(pe)
            last_pe(pe)

        @block.vector
        def _(dve):
            prep_dve(dve)
            l0_dve(dve)
            moe_dve(dve)
            l1_dve(dve)
            mlp_dve(dve)
            last_dve(dve)

        @block.scalar
        def _(act):
            l0_act(act)
            moe_act(act)
            l1_act(act)
            mlp_act(act)

        @block.gpsimd
        def _(pool):
            prep_pool(pool)
            l0_pool(pool)
            split_pool(pool)
            l1_pool(pool)
            mlp_pool(pool)
            last_pool(pool)


def layout(x, np, **w):
    f = np.float32
    W = {k: np.asarray(v) for k, v in w.items()}
    x = np.asarray(x)
    d = {}
    d["ident"] = np.eye(128, dtype=f)
    d["hmask"] = np.repeat(np.eye(HH, dtype=f), HD, axis=0)
    d["bmask"] = np.repeat(d["hmask"], HD, axis=1)
    p = x.reshape(B, 6, 16, 6, 16, 3).transpose(0, 1, 3, 2, 4, 5).reshape(B, NPATCH, PC, 128)
    pz = np.zeros((B, T, PC, 128), f)
    pz[:, 1:] = p
    d["patches"] = np.ascontiguousarray(pz.reshape(QUADS, QB, T, PC, 128).transpose(0, 4, 3, 1, 2))
    d["w_patch"] = np.ascontiguousarray(W["L0_tok_W_proj"].reshape(PC, 128, D).transpose(1, 0, 2))
    rc = np.zeros((128, 6, D), f)
    for r in (0, 64):
        rc[r:r + T, 0] = W["L0_tok_pos_embedding"]
        rc[r, 1] = W["L0_tok_cls_token"].reshape(D)
        rc[r + 1:r + T, 1] = W["L0_tok_b_proj"]
    rc[:, 2] = W["L0_ffn_norm_weight"]
    eo = lambda a: a.reshape(-1, HH, 2, HD).transpose(0, 2, 1, 3).reshape(-1, 2, FH)
    bv = eo(W["L0_attn_bias_v"][None])[0]
    rc[0:64, 3, 0:FH] = bv[0]
    rc[64:, 3, 0:FH] = bv[1]
    rc[:, 4] = W["L1_attn_bo"]
    rc[:, 5] = W["L1_ffn_g2b"]
    d["rowc"] = rc
    d["lam"] = np.repeat(W["L1_attn_lambda_p"].reshape(1, NH), 128, axis=0)
    halves = lambda a: np.ascontiguousarray(a.reshape(2, FH, -1).transpose(1, 0, 2))
    d["v_q_t"] = np.ascontiguousarray(W["L0_attn_V_Q"].T)
    d["v_k_t"] = np.ascontiguousarray(W["L0_attn_V_K"].T)
    d["v_v_t"] = np.ascontiguousarray(W["L0_attn_V_V"].T)
    d["u_q_t"] = halves(np.ascontiguousarray(W["L0_attn_U_Q"].T))
    d["u_k"] = W["L0_attn_U_K"]
    d["u_v"] = np.ascontiguousarray(eo(W["L0_attn_U_V"]).reshape(R0, D))
    d["m_u"] = np.ascontiguousarray(np.tile(W["L0_attn_M_U"].T, (1, HH)))
    d["m_v"] = np.ascontiguousarray(np.tile(W["L0_attn_M_V"], (1, HH)))
    d["bias_qk"] = np.ascontiguousarray(np.stack([W["L0_attn_bias_q"].reshape(2, FH), W["L0_attn_bias_k"].reshape(2, FH)]).transpose(2, 0, 1))
    d["slots"] = W["L0_ffn_slots"]
    d["slot_scale"] = W["L0_ffn_scale"].reshape(SLOTS, 1)
    d["w_q1"] = halves(W["L1_attn_Wq"])
    d["w_k1"] = halves(W["L1_attn_Wk"])
    d["w_v1"] = halves(eo(W["L1_attn_Wv"]).reshape(D, D))
    d["w_o1"] = halves(W["L1_attn_Wo"])
    w = W["L0_ffn_fc1_weight"].reshape(GROUPS, GS, 2, FH, HID)
    fc1 = np.zeros((GROUPS, FH + 1, 2, GS, HID), f)
    fc1[:, :FH] = w.transpose(0, 3, 2, 1, 4)
    fc1[:, FH, 0] = W["L0_ffn_fc1_bias"].reshape(GROUPS, GS, HID)
    d["fc1"] = fc1
    w = W["L0_ffn_fc2_weight"].reshape(GROUPS, GS, HC, 128, D)
    d["fc2"] = np.ascontiguousarray(w.transpose(0, 3, 2, 1, 4))
    d["fc2_b"] = W["L0_ffn_fc2_bias"].reshape(GROUPS, GS, D)
    d["slot_sel"] = np.repeat(np.eye(GS, dtype=f), 32, axis=1)
    d["w1"] = np.ascontiguousarray(W["L1_ffn_W1"].transpose(0, 2, 1, 3).reshape(SEG * SR, SM * SH))
    d["b1"] = W["L1_ffn_b1"].reshape(128, 128)
    b2 = np.zeros((4, 2, SM, 4, 32), f)
    for s in range(SEG):
        b2[s // 2, s % 2, :, s % 4, :SR] = W["L1_ffn_b2"][s]
    d["b2"] = np.ascontiguousarray(b2.reshape(4, 128, 128).transpose(1, 0, 2)).reshape(128, 512)
    w = np.zeros((4, SH, CH, SEG, 32), f)
    w[..., :SR] = W["L1_ffn_W2"].reshape(SEG, CH, 4, SH, SR).transpose(2, 3, 1, 0, 4)
    d["w2"] = w.reshape(128, CH, SEG, 32)
    d["z_proj"] = halves(np.ascontiguousarray(W["L1_ffn_P"].transpose(1, 0, 2).reshape(D, SEG * SR)))
    sc = np.zeros((SEG, SR, SEG, SM), f)
    for s in range(SEG):
        sc[s, :, s] = W["L1_ffn_C"][s].T
    d["score_w"] = sc.reshape(128, SEG * SM)
    sel = np.zeros((PARTS, 32, SM // 8, 4, SH), f)
    for m in range(32):
        sel[:, m, m // 4, m % 4] = 1
    d["gate_sel"] = sel.reshape(PARTS * 32, 2, 512)
    g1 = np.zeros((4, 32, 2, SG), f)
    g1[:, :SR] = W["L1_ffn_G1"].reshape(2, 4, SR, SG).transpose(1, 2, 0, 3)
    d["out1_w"] = g1.reshape(128, 2, SG)
    d["out1_b"] = W["L1_ffn_g1b"].reshape(SG, 1)
    d["out2_w"] = W["L1_ffn_G2"]
    return d


def kernel(**inputs):
    import numpy as _np
    import concourse.bacc as _bacc
    from concourse import mybir as _mybir
    from concourse.bass_utils import run_bass_kernel_spmd as _run

    nc = _bacc.Bacc("TRN2", target_bir_lowering=False, num_devices=1)
    arrays, io = {}, {}
    for name, a in layout(np=_np, **inputs).items():
        a = _np.ascontiguousarray(a)
        arrays[f"in_{name}_dram"] = a
        io[name] = nc.dram_tensor(f"in_{name}_dram", a.shape, _mybir.dt.from_np(a.dtype), kind="ExternalInput").ap()
    io["out"] = nc.dram_tensor("out_0_dram", (B, T, D), _mybir.dt.float32, kind="ExternalOutput").ap()
    tower(nc, io)
    r = _run(nc, [arrays], core_ids=[0])
    return r.results[0]["out_0_dram"]
```
